# Optimizing a Trainium2 kernel written in Bass

```python
import numpy as np
import jax
import jax.numpy as jnp

def _softmax(x, axis=-1):
    return jax.nn.softmax(x, axis=axis)

def _gelu(x):
    return jax.nn.gelu(x, approximate=True)

def _silu(x):
    return jax.nn.silu(x)

def _sigmoid(x):
    return jax.nn.sigmoid(x)

def _layernorm(x, axis=-1, eps=1e-05):
    m = jnp.mean(x, axis=axis, keepdims=True)
    v = jnp.var(x, axis=axis, keepdims=True)
    return (x - m) / jnp.sqrt(v + eps)

def _scatter_add(tgt, idx, src, axis=0):
    return tgt.at[idx].add(src)

def _segment_sum(src, seg, n):
    return jax.ops.segment_sum(src, seg, n)
kernel_name = 'mk_decoder_preln_d1_seqx_r2_27368e'

def setup_inputs(seed: int=0):
    np.random.seed(seed)
    _w = jnp.asarray

    def _rec_inputs():
        import jax
        import jax.numpy as jnp
        _rk = jax.random.key(seed)
        x = -0.0002928 + 1 * jax.random.normal(jax.random.fold_in(_rk, 1), (4, 1024, 512), jnp.float32)
        _lenS = 1024 - jax.random.randint(jax.random.fold_in(_rk, 7), (4,), 0, max(1, 1024 // 4) + 1, jnp.int32)
        _lenS2 = 1601 - jax.random.randint(jax.random.fold_in(_rk, 8), (4,), 0, max(1, 1601 // 4) + 1, jnp.int32)
        _ctx_1024P = jax.random.normal(jax.random.fold_in(_rk, 11), (4, 16, 512), jnp.float32)
        _ctx_1024c = jax.random.dirichlet(jax.random.fold_in(_rk, 511), 0.3 * jnp.ones((16,), jnp.float32), (4, 1601))
        _ctx_1024t = jnp.einsum('bsk,bkd->bsd', _ctx_1024c, _ctx_1024P)
        _ctx_1024t = _ctx_1024t * jax.lax.rsqrt(jnp.mean(jnp.square(_ctx_1024t)) + 1e-12) * 0.953939
        ctx_1024 = -1.39393e-06 + 0.999914 * (_ctx_1024t + 0.3 * jax.random.normal(jax.random.fold_in(_rk, 611), (4, 1601, 512), jnp.float32))
        _validS = jnp.arange(1024)[None, :] < _lenS[:, None]
        _validS2 = jnp.arange(1601)[None, :] < _lenS2[:, None]
        _causal = jnp.tril(jnp.ones((1024, 1024), dtype=bool))
        mask_1x1xSxS2_ik0 = jnp.where(jnp.broadcast_to(_validS2[0:1, None, None, :], (1, 1, 1024, 1601)), 0, 1).astype(jnp.int32)
        return (x, ctx_1024, mask_1x1xSxS2_ik0)
    x, ctx_1024, mask_1x1xSxS2_ik0 = _rec_inputs()

    def _L0_attn_setup():
        import jax, jax.numpy as jnp
        import numpy as np
        B, S, D, DV = (1, 2048, 512, 512)
        key = jax.random.key(seed)
        kq, kk, kv, ks, kp = jax.random.split(key, 5)
        return {'q': jax.random.normal(kq, (B, S, D), dtype=jnp.float32), 'k': jax.random.normal(kk, (B, S, D), dtype=jnp.float32), 'v': jax.random.normal(kv, (B, S, DV), dtype=jnp.float32), 'scale_factor': jax.random.normal(ks, (1,), dtype=jnp.float32), 'dropout_p': jax.random.uniform(kp, (1,), dtype=jnp.float32)}
    _L0_attn_all = _L0_attn_setup()
    _L0_attn_in = {k: v for k, v in _L0_attn_all.items() if k in ('k', 'v', 'scale_factor', 'dropout_p')}
    del _L0_attn_all

    def _L0_xattn_setup():
        import jax, jax.numpy as jnp
        import numpy as np
        D = 512
        H = 16
        DK = D // H
        B = 1
        S = 2048

        def _split_heads(x):
            b, s, _ = x.shape
            return x.reshape(b, s, H, DK).transpose(0, 2, 1, 3)
        key = jax.random.key(seed)
        ks = jax.random.split(key, 12)
        scale = 1.0 / np.sqrt(D)
        inp = {'Q': jax.random.normal(ks[0], (B, S, D), jnp.float32), 'K': jax.random.normal(ks[1], (B, S, D), jnp.float32), 'V': jax.random.normal(ks[2], (B, S, D), jnp.float32), 'Wq_w': jax.random.normal(ks[3], (D, D), jnp.float32) * scale, 'Wq_b': jax.random.normal(ks[4], (D,), jnp.float32) * scale, 'Wk_w': jax.random.normal(ks[5], (D, D), jnp.float32) * scale, 'Wk_b': jax.random.normal(ks[6], (D,), jnp.float32) * scale, 'Wv_w': jax.random.normal(ks[7], (D, D), jnp.float32) * scale, 'Wv_b': jax.random.normal(ks[8], (D,), jnp.float32) * scale, 'Wo_w': jax.random.normal(ks[9], (D, D), jnp.float32) * scale, 'Wo_b': jax.random.normal(ks[10], (D,), jnp.float32) * scale, 'mask': jnp.tril(jnp.ones((S, S), jnp.int32))[None, None, :, :]}
        return inp
    _L0_xattn_all = _L0_xattn_setup()
    _L0_xattn_in = {k: v for k, v in _L0_xattn_all.items() if k in ('Wq_w', 'Wq_b', 'Wk_w', 'Wk_b', 'Wv_w', 'Wv_b', 'Wo_w', 'Wo_b')}
    del _L0_xattn_all

    def _L0_ffn_setup():
        import jax, jax.numpy as jnp
        import numpy as np
        B, T, C, H, E, K = (4, 512, 512, 512, 8, 2)

        def _swiglu(x):
            a, b = jnp.split(x, 2, axis=-1)
            return jax.nn.silu(a) * b
        key = jax.random.key(seed)
        ks = jax.random.split(key, 6)
        s = 0.02
        x = jax.random.normal(ks[0], (B, T, C), jnp.float32)
        w_shared_in = jax.random.normal(ks[1], (C, 2 * H), jnp.float32) * s
        w_shared_out = jax.random.normal(ks[2], (H, C), jnp.float32) * s
        w1_shared = jax.random.normal(ks[3], (C, 2 * H), jnp.float32) * s
        w2 = jax.random.normal(ks[4], (E, H, C), jnp.float32) * s
        w_gate = jax.random.normal(ks[5], (C, E), jnp.float32) * s
        gate_bias = jnp.zeros((E,), jnp.float32)
        return {'x': x, 'w_shared_in': w_shared_in, 'w_shared_out': w_shared_out, 'w1_shared': w1_shared, 'w2': w2, 'w_gate': w_gate, 'gate_bias': gate_bias}
    _L0_ffn_all = _L0_ffn_setup()
    _L0_ffn_in = {k: v for k, v in _L0_ffn_all.items() if k in ('w_shared_in', 'w_shared_out', 'w1_shared', 'w2', 'w_gate', 'gate_bias')}
    del _L0_ffn_all
    return {'x': x, 'ctx_1024': ctx_1024, 'mask_1x1xSxS2_ik0': mask_1x1xSxS2_ik0, 'L0_attn_k': _L0_attn_in['k'], 'L0_attn_v': _L0_attn_in['v'], 'L0_attn_scale_factor': _L0_attn_in['scale_factor'], 'L0_attn_dropout_p': _L0_attn_in['dropout_p'], 'L0_xattn_Wq_w': _L0_xattn_in['Wq_w'], 'L0_xattn_Wq_b': _L0_xattn_in['Wq_b'], 'L0_xattn_Wk_w': _L0_xattn_in['Wk_w'], 'L0_xattn_Wk_b': _L0_xattn_in['Wk_b'], 'L0_xattn_Wv_w': _L0_xattn_in['Wv_w'], 'L0_xattn_Wv_b': _L0_xattn_in['Wv_b'], 'L0_xattn_Wo_w': _L0_xattn_in['Wo_w'], 'L0_xattn_Wo_b': _L0_xattn_in['Wo_b'], 'L0_ffn_w_shared_in': _L0_ffn_in['w_shared_in'], 'L0_ffn_w_shared_out': _L0_ffn_in['w_shared_out'], 'L0_ffn_w1_shared': _L0_ffn_in['w1_shared'], 'L0_ffn_w2': _L0_ffn_in['w2'], 'L0_ffn_w_gate': _L0_ffn_in['w_gate'], 'L0_ffn_gate_bias': _L0_ffn_in['gate_bias']}

def reference(x, ctx_1024, mask_1x1xSxS2_ik0, L0_attn_k, L0_attn_v, L0_attn_scale_factor, L0_attn_dropout_p, L0_xattn_Wq_w, L0_xattn_Wq_b, L0_xattn_Wk_w, L0_xattn_Wk_b, L0_xattn_Wv_w, L0_xattn_Wv_b, L0_xattn_Wo_w, L0_xattn_Wo_b, L0_ffn_w_shared_in, L0_ffn_w_shared_out, L0_ffn_w1_shared, L0_ffn_w2, L0_ffn_w_gate, L0_ffn_gate_bias):
    import jax
    import jax.numpy as jnp

    def _L0_attn_ref(q, k, v, scale_factor, dropout_p):
        import jax, jax.numpy as jnp
        import numpy as np
        B, S, D, DV = (1, 2048, 512, 512)
        b, s, d = q.shape
        step = s // 4
        scale = q[:, ::step].reshape(b, -1)
        qk = jnp.einsum('bsd,btd->bst', q, k)
        scaled_qk = qk * scale[:, None, :]
        softmax_qk = jax.nn.softmax(scaled_qk, axis=-1)
        return jnp.einsum('bst,btv->bsv', softmax_qk, v)

    def _L0_xattn_ref(Q, K, V, Wq_w, Wq_b, Wk_w, Wk_b, Wv_w, Wv_b, Wo_w, Wo_b, mask):
        import jax, jax.numpy as jnp
        import numpy as np
        D = 512
        H = 16
        DK = D // H
        B = 1
        S = 2048

        def _split_heads(x):
            b, s, _ = x.shape
            return x.reshape(b, s, H, DK).transpose(0, 2, 1, 3)
        q = _split_heads(Q @ Wq_w.T + Wq_b)
        k = _split_heads(K @ Wk_w.T + Wk_b)
        v = _split_heads(V @ Wv_w.T + Wv_b)
        scores = jnp.einsum('bhqd,bhkd->bhqk', q, k) / np.sqrt(DK).astype(np.float32)
        scores = jnp.where(mask == 0, jnp.float32(-1000000000.0), scores)
        attn = jax.nn.softmax(scores, axis=-1)
        out = jnp.einsum('bhqk,bhkd->bhqd', attn, v)
        out = out.transpose(0, 2, 1, 3).reshape(Q.shape[0], Q.shape[1], D)
        return out @ Wo_w.T + Wo_b

    def _L0_ffn_ref(x, w_shared_in, w_shared_out, w1_shared, w2, w_gate, gate_bias):
        import jax, jax.numpy as jnp
        import numpy as np
        B, T, C, H, E, K = (4, 512, 512, 512, 8, 2)

        def _swiglu(x):
            a, b = jnp.split(x, 2, axis=-1)
            return jax.nn.silu(a) * b
        Bx, Tx, Cx = x.shape
        S = Bx * Tx
        fx = x.reshape(S, Cx)
        shared_out = _swiglu(fx @ w_shared_in) @ w_shared_out
        logits = fx @ w_gate + gate_bias
        probs = jax.nn.softmax(logits, axis=-1)
        top_val, top_idx = jax.lax.top_k(probs, K)
        wdense = jnp.zeros((S, E), probs.dtype).at[jnp.arange(S)[:, None], top_idx].add(top_val)
        hid = _swiglu(fx @ w1_shared)
        routed_out = jnp.zeros_like(shared_out)
        for e in range(E):
            routed_out = routed_out + wdense[:, e:e + 1] * (hid @ w2[e])
        return (shared_out + routed_out).reshape(Bx, Tx, Cx)
    x = x + _L0_attn_ref(_layernorm(x, axis=-1), L0_attn_k, L0_attn_v, L0_attn_scale_factor, L0_attn_dropout_p)
    x = x + _L0_xattn_ref(_layernorm(x, axis=-1), ctx_1024, ctx_1024, L0_xattn_Wq_w, L0_xattn_Wq_b, L0_xattn_Wk_w, L0_xattn_Wk_b, L0_xattn_Wv_w, L0_xattn_Wv_b, L0_xattn_Wo_w, L0_xattn_Wo_b, mask_1x1xSxS2_ik0)
    x = x + _L0_ffn_ref(_layernorm(x, axis=-1), L0_ffn_w_shared_in, L0_ffn_w_shared_out, L0_ffn_w1_shared, L0_ffn_w2, L0_ffn_w_gate, L0_ffn_gate_bias)
    return x

_drawn_inputs = setup_inputs


def setup_inputs(seed=0):
    import zlib

    import numpy as np

    out = dict(_drawn_inputs(seed))
    spreads = {'L0_ffn_gate_bias': (0.0, 0.8)}
    factors = {'L0_xattn_Wq_b': 8.0,
     'L0_xattn_Wk_b': 64.0,
     'L0_ffn_w1_shared': 5.968,
     'L0_ffn_w2': 6.032,
     'L0_ffn_w_gate': 6.998,
     'L0_ffn_w_shared_in': 8.0,
     'L0_ffn_w_shared_out': 8.0}
    for name, (base, spread) in spreads.items():
        noise = np.random.default_rng([zlib.crc32(name.encode()), seed]).standard_normal(out[name].shape)
        drawn = base * np.exp(spread * noise) if base else spread * noise
        out[name] = jnp.asarray(drawn.astype(out[name].dtype))
    for name, factor in factors.items():
        out[name] = (out[name] * factor).astype(out[name].dtype)
    return out
```

```python
import concourse.bass as bass
from concourse import mybir
from concourse.alu_op_type import AluOpType as ALU
from contextlib import ExitStack
import itertools
import numpy as np

F32 = mybir.dt.float32
F32R = mybir.dt.float32r
BF16 = mybir.dt.bfloat16
I32 = mybir.dt.int32
U32 = mybir.dt.uint32
ACT = mybir.ActivationFunctionType
AX = mybir.AxisListType
ds = bass.ds

P = 128
B, S, D = 4, 1024, 512
TOK = B * S
DC = D // P
T1 = 2048
T1C = T1 // P
S2 = 1601
H, DK = 16, 32
E = 8
BANK = 512
EPS = 1e-5
LOWEST = -3.0e38


class Step:

    def __init__(self, ctx, nc, name, ahead=None, size=1):
        self.sem = ctx.enter_context(nc.semaphore(name))
        self.ahead, self.size = 0 if ahead is None else ahead + 1, size

    def open(self, eng):
        eng.sem_inc(self.sem, self.ahead * self.size)

    def done(self, instruction):
        instruction.then_inc(self.sem, self.size)

    def wait(self, eng, n):
        eng.wait_ge(self.sem, (n + self.ahead) * self.size)


class Chain:

    def __init__(self, step, eng, base):
        self.step, self.eng, self.n = step, eng, base

    def __call__(self, instruction):
        self.step.done(instruction)
        self.n = self.n + 1
        self.step.wait(self.eng, self.n)


def words(ap):
    return ap.bitcast(F32)


def matmul3(pe, out, left, right, start, stop):
    (lh, ll), (rh, rl) = left, right
    pe.matmul(out, lh, rh, start=start, stop=False)
    pe.matmul(out, lh, rl, start=False, stop=False)
    return pe.matmul(out, ll, rh, start=False, stop=stop)


def allocator(ctx, nc, tag):
    def sb(name, shape, dt=F32):
        return ctx.enter_context(nc.sbuf_tensor(f"{tag}_{name}", shape, dt))

    def ps(name, shape, dt=F32):
        return ctx.enter_context(nc.psum_tensor(f"{tag}_{name}", shape, dt))

    def step(name, **more):
        return Step(ctx, nc, f"{tag}_{name}", **more)

    return sb, ps, step


def make_identity(nc, ident, ident_b):
    with ExitStack() as ctx:
        _, _, step = allocator(ctx, nc, "id")
        made = step("made")
        with nc.Block() as block:
            @block.gpsimd
            def _(pool):
                made.done(pool.memset(ident[:, :], 0.0))
                made.wait(pool, 1)
                made.done(pool.affine_select(out=ident[:, :], in_=ident[:, :], compare_op=ALU.not_equal,
                                             fill=1.0, base=0, pattern=[[-1, P]], channel_multiplier=1))
                made.wait(pool, 2)
                made.done(pool.tensor_copy(ident_b[:, :], ident[:, :]))


def split_transposed(nc, ident, tag, items):
    with ExitStack() as ctx:
        sb, ps, step = allocator(ctx, nc, tag)
        rows = sb("rows", [P, 8, D])
        banks = ps("banks", [P, 8, DC, P])
        loaded, turned, high_done, low_done = step("loaded", size=16), step("turned"), step("high"), step("low")
        with nc.Block() as block:
            @block.sync
            def _(sp):
                for n, (src, _, _) in enumerate(items):
                    turned.wait(sp, 8 * n)
                    loaded.done(sp.dma_start(rows[:, :, :], src))

            @block.tensor
            def _(pe):
                for n in range(len(items)):
                    loaded.wait(pe, n + 1)
                    for r in range(8):
                        if n:
                            low_done.wait(pe, 8 * (n - 1) + r + 1)
                        for dc in range(DC):
                            last = pe.transpose(banks[:, r, dc, :], rows[:, r, dc * P:(dc + 1) * P], ident[:, :])
                        turned.done(last)

            @block.scalar
            def _(act):
                for n, (_, high, low) in enumerate(items):
                    for r in range(8):
                        turned.wait(act, 8 * n + r + 1)
                        high_done.done(act.activation(high[:, :, r * P:(r + 1) * P], banks[:, r, :, :], ACT.Copy))

            @block.vector
            def _(dve):
                for n, (_, high, low) in enumerate(items):
                    for r in range(8):
                        high_done.wait(dve, 8 * n + r + 1)
                        low_done.done(dve.tensor_tensor(low[:, :, r * P:(r + 1) * P], banks[:, r, :, :],
                                                        words(high[:, :, r * P:(r + 1) * P]), ALU.subtract))


def tokens(ap):
    return ap.rearrange("(t p) n -> t p n", p=P)


def one(ap, i):
    return ap[ds(i, 1)].squeeze(0)


def self_attention(nc, ident, x, k, v, x1):
    NB = T1 // BANK
    KB = BANK // P
    tiles = TOK // P
    with ExitStack() as keep:
        sb, _, _ = allocator(keep, nc, "sa")
        kT = [sb(f"kT_{part}", [P, DC, T1], F32R) for part in ("high", "low")]
        vs = [sb(f"v_{part}", [P, T1C, D], F32R) for part in ("high", "low")]
        scale = sb("scale", [P, B, NB, D])
        k_rows = k[0].rearrange("(n r p) d -> n p r d", p=P, r=8)
        split_transposed(nc, ident, "sak",
                         [(k_rows[n], *(t[:, :, n * 8 * P:(n + 1) * 8 * P] for t in kT)) for n in range(2)])
        self_attention_setup(nc, x, v, vs, scale)
        self_attention_loop(nc, ident, x, x1, kT, vs, scale, NB, KB, tiles)


def self_attention_setup(nc, x, v, vs, scale):
    G = B * 4
    rows_of_scale = x.rearrange("b (j r) n -> (b j) r n", j=4)[:, 0, :]
    v_rows = v[0].rearrange("(n r p) d -> n p r d", p=P, r=T1C // 2)
    with ExitStack() as ctx:
        sb, _, step = allocator(ctx, nc, "sas")
        v_in = sb("v_in", [P, T1C // 2, D])
        stats = sb("stats", [P, G, 6])
        mean_var = sb("mean_var", [P, G, 2])
        var, rstd, power = sb("var", [P, G]), sb("rstd", [P, G]), sb("power", [P, G])
        v_loaded, v_high, v_low, s_loaded = step("v_loaded", size=16), step("v_high"), step("v_low"), step("s_loaded", size=16)
        chain, pow_set, root = step("chain"), step("pow_set"), step("root")
        groups = scale[:, :, :, :].rearrange("p b j d -> p (b j) d")
        with nc.Block() as block:
            @block.sync
            def _(sp):
                s_loaded.done(sp.dma_start(groups, rows_of_scale.partition_broadcast(P)))
                for n in range(2):
                    v_low.wait(sp, n)
                    v_loaded.done(sp.dma_start(v_in[:, :, :], v_rows[n]))

            @block.scalar
            def _(act):
                for n in range(2):
                    v_loaded.wait(act, n + 1)
                    v_high.done(act.activation(vs[0][:, n * 8:(n + 1) * 8, :], v_in[:, :, :], ACT.Copy))

            @block.gpsimd
            def _(pool):
                pow_set.done(pool.memset(power[:, :], -0.5))
                pow_set.wait(pool, 1)
                chain.wait(pool, 2 * G + 1)
                root.done(pool.tensor_tensor(rstd[:, :], var[:, :], power[:, :], ALU.pow))

            @block.vector
            def _(dve):
                s_loaded.wait(dve, 1)
                for g in range(G):
                    chain.done(dve.bn_stats(stats[:, g, :], groups[:, g, :]))
                chain.wait(dve, G)
                for g in range(G):
                    chain.done(dve.bn_aggr(mean_var[:, g, :], stats[:, g, :]))
                chain.wait(dve, 2 * G)
                chain.done(dve.tensor_scalar_add(var[:, :], mean_var[:, :, 1], EPS))
                root.wait(dve, 1)
                for g in range(G):
                    chain.done(dve.tensor_scalar(groups[:, g, :], groups[:, g, :], mean_var[:, g, 0:1],
                                                 rstd[:, g:g + 1], ALU.subtract, ALU.mult))
                for n in range(2):
                    v_high.wait(dve, n + 1)
                    v_low.done(dve.tensor_tensor(vs[1][:, n * 8:(n + 1) * 8, :], v_in[:, :, :],
                                                 words(vs[0][:, n * 8:(n + 1) * 8, :]), ALU.subtract))


def self_attention_loop(nc, ident, x, x1, kT, vs, scale, NB, KB, tiles):
    x_t, x1_t = tokens(x.rearrange("b s n -> (b s) n")), tokens(x1)
    with ExitStack() as ctx:
        sb, ps, step = allocator(ctx, nc, "sal")
        x_norm, x_add = sb("x_norm", [P, D]), sb("x_add", [P, D])
        normed = sb("normed", [P, D])
        nT = [sb(f"nT_{part}", [P, DC, P], F32R) for part in ("high", "low")]
        scaled, prob = sb("scaled", [P, NB, BANK]), sb("prob", [P, NB, BANK])
        pT = [sb(f"pT_{part}", [P, T1C, P], F32R) for part in ("high", "low")]
        out = sb("out", [P, D])
        stats, mean_var, var, rstd, power = sb("stats", [P, 6]), sb("mean_var", [P, 2]), sb("var", [P, 1]), sb("rstd", [P, 1]), sb("power", [P, 1])
        neg_max, total, inv_total = sb("neg_max", [P, 1]), sb("total", [P, 1]), sb("inv_total", [P, 1])
        scores = ps("scores", [P, NB, BANK])
        nT_ps = ps("nT_ps", [P, DC, P])
        pT_ps = [ps(f"pT_ps{i}", [P, KB, P]) for i in range(2)]
        o_ps = ps("o_ps", [P, D])

        norm_in = step("norm_in", size=16)
        add_in = step("add_in", size=16)
        stored = step("stored", size=16, ahead=1)
        constant = step("constant")
        stat = step("stat")
        root = step("root", ahead=1)
        normal = step("normal", ahead=1)
        turned = step("turned", ahead=1)
        nT_high, nT_low = step("nT_high"), step("nT_low")
        scored = step("scored")
        scaled_to = step("scaled_to", ahead=NB)
        peak = step("peak", ahead=1)
        exped = step("exped", ahead=1)
        p_turned = step("p_turned", ahead=NB)
        pT_high, pT_low = step("pT_high"), step("pT_low", ahead=2)
        weighed = step("weighed", ahead=1)
        inverse = step("inverse")
        summed = step("summed", ahead=1)

        with nc.Block() as block:
            @block.sync
            def _(sp):
                def load_norm(t):
                    normal.wait(sp, t)
                    norm_in.done(sp.dma_start(x_norm[:, :], one(x_t, t)))

                def load_add(t):
                    summed.wait(sp, t)
                    add_in.done(sp.dma_start(x_add[:, :], one(x_t, t)))

                def store(t):
                    summed.wait(sp, t + 1)
                    stored.done(sp.dma_start(one(x1_t, t), out[:, :]))

                stored.open(sp)
                load_norm(0)
                load_norm(1)
                with sp.Fori(0, tiles - 2) as t:
                    load_norm(t + 2)
                    load_add(t)
                    store(t)
                for t in (tiles - 2, tiles - 1):
                    load_add(t)
                    store(t)
                stored.wait(sp, tiles)

            @block.gpsimd
            def _(pool):
                root.open(pool)
                constant.done(pool.memset(power[:, :], -0.5))
                constant.wait(pool, 1)
                with pool.Fori(0, tiles) as t:
                    stat.wait(pool, t + 1)
                    root.done(pool.tensor_tensor(rstd[:, :], var[:, :], power[:, :], ALU.pow))

            @block.tensor
            def _(pe):
                def turn(t):
                    normal.wait(pe, t + 1)
                    nT_low.wait(pe, t)
                    for dc in range(DC):
                        last = pe.transpose(nT_ps[:, dc, :], normed[:, dc * P:(dc + 1) * P], ident[:, :])
                    turned.done(last)

                def score(t, j):
                    if j == 0:
                        nT_low.wait(pe, t + 1)
                    scaled_to.wait(pe, NB * (t - 1) + j + 1)
                    for dc in range(DC):
                        last = matmul3(pe, scores[:, j, :], [n[:, dc, :] for n in nT],
                                       [kt[:, dc, j * BANK:(j + 1) * BANK] for kt in kT], dc == 0, dc == DC - 1)
                    scored.done(last)

                def turn_p(t, j):
                    if j == 0:
                        exped.wait(pe, t + 1)
                    pT_low.wait(pe, NB * t + j - 1)
                    for n in range(KB):
                        last = pe.transpose(pT_ps[j % 2][:, n, :], prob[:, j, n * P:(n + 1) * P], ident[:, :])
                    p_turned.done(last)

                def weigh(t, j):
                    if j == 0:
                        summed.wait(pe, t)
                    pT_low.wait(pe, NB * t + j + 1)
                    for n in range(j * KB, (j + 1) * KB):
                        last = matmul3(pe, o_ps[:, :], [p[:, n, :] for p in pT], [w[:, n, :] for w in vs],
                                       n == 0, n == T1C - 1)
                    if j == NB - 1:
                        weighed.done(last)

                def tile(t, ahead):
                    if ahead >= 1:
                        for j in range(NB - 1):
                            score(t + 1, j)
                    turn_p(t, 0)
                    turn_p(t, 1)
                    if ahead >= 1:
                        score(t + 1, NB - 1)
                    if ahead >= 2:
                        turn(t + 2)
                    for j in range(NB):
                        weigh(t, j)
                        if j + 2 < NB:
                            turn_p(t, j + 2)

                turned.open(pe)
                p_turned.open(pe)
                weighed.open(pe)
                turn(0)
                for j in range(NB):
                    score(0, j)
                turn(1)
                with pe.Fori(0, tiles - 2) as t:
                    tile(t, 2)
                tile(tiles - 2, 1)
                tile(tiles - 1, 0)

            @block.scalar
            def _(act):
                def high_n(t):
                    turned.wait(act, t + 1)
                    nT_high.done(act.activation(nT[0][:, :, :], nT_ps[:, :, :], ACT.Copy))

                def exp(t):
                    p_turned.wait(act, NB * t)
                    peak.wait(act, t + 1)
                    exped.done(act.activation(prob[:, :, :], scaled[:, :, :], ACT.Exp, bias=neg_max[:, 0:1],
                                              accum_out=total[:, 0:1]))

                def high_p(t, j):
                    if j == 0:
                        weighed.wait(act, t)
                    p_turned.wait(act, NB * t + j + 1)
                    pT_high.done(act.activation(pT[0][:, j * KB:(j + 1) * KB, :], pT_ps[j % 2][:, :, :], ACT.Copy))

                def tile(t, ahead):
                    high_p(t, 0)
                    high_p(t, 1)
                    if ahead >= 2:
                        high_n(t + 2)
                    high_p(t, 2)
                    high_p(t, 3)
                    if ahead >= 1:
                        exp(t + 1)

                exped.open(act)
                high_n(0)
                high_n(1)
                exp(0)
                with act.Fori(0, tiles - 2) as t:
                    tile(t, 2)
                tile(tiles - 2, 1)
                tile(tiles - 1, 0)

            @block.vector
            def _(dve):
                def normalize(t):
                    norm_in.wait(dve, t + 1)
                    root.wait(dve, t)
                    dve.bn_stats(stats[:, :], x_norm[:, :])
                    dve.drain()
                    dve.bn_aggr(mean_var[:, :], stats[:, :])
                    dve.drain()
                    stat.done(dve.tensor_scalar_add(var[:, :], mean_var[:, 1:2], EPS))
                    turned.wait(dve, t)
                    root.wait(dve, t + 1)
                    normal.done(dve.tensor_scalar(normed[:, :], x_norm[:, :], mean_var[:, 0:1], rstd[:, 0:1],
                                                  ALU.subtract, ALU.mult))

                def low_n(t):
                    nT_high.wait(dve, t + 1)
                    nT_low.done(dve.tensor_tensor(nT[1][:, :, :], nT_ps[:, :, :], words(nT[0][:, :, :]), ALU.subtract))

                def scale_block(t, j):
                    if j == 0:
                        exped.wait(dve, t)
                    scored.wait(dve, NB * t + j + 1)
                    batch = scale[:, ds(t // (S // P), 1), j, :].squeeze(1)
                    scaled_to.done(dve.tensor_tensor(scaled[:, j, :], scores[:, j, :], batch, ALU.mult))

                def row_max(t):
                    scaled_to.wait(dve, NB * (t + 1))
                    peak.done(dve.tensor_reduce(neg_max[:, 0:1], scaled[:, :, :], AX.XY, ALU.max, negate=True))

                def low_p(t, j):
                    pT_high.wait(dve, NB * t + j + 1)
                    pT_low.done(dve.tensor_tensor(pT[1][:, j * KB:(j + 1) * KB, :], pT_ps[j % 2][:, :, :],
                                                  words(pT[0][:, j * KB:(j + 1) * KB, :]), ALU.subtract))

                def invert(t):
                    summed.wait(dve, t)
                    exped.wait(dve, t + 1)
                    inverse.done(dve.reciprocal(inv_total[:, :], total[:, :]))

                def add(t):
                    weighed.wait(dve, t + 1)
                    inverse.wait(dve, t + 1)
                    add_in.wait(dve, t + 1)
                    stored.wait(dve, t)
                    summed.done(dve.scalar_tensor_tensor(out[:, :], o_ps[:, :], inv_total[:, 0:1], x_add[:, :],
                                                         ALU.mult, ALU.add))

                def tile(t, ahead):
                    invert(t)
                    if ahead >= 2:
                        normalize(t + 2)
                    if ahead >= 1:
                        for j in range(NB - 1):
                            scale_block(t + 1, j)
                    low_p(t, 0)
                    low_p(t, 1)
                    if ahead >= 1:
                        scale_block(t + 1, NB - 1)
                        row_max(t + 1)
                    if ahead >= 2:
                        low_n(t + 2)
                    low_p(t, 2)
                    low_p(t, 3)
                    add(t)

                for s in (normal, scaled_to, peak, pT_low, summed):
                    s.open(dve)
                normalize(0)
                low_n(0)
                normalize(1)
                for j in range(NB):
                    scale_block(0, j)
                row_max(0)
                low_n(1)
                with dve.Fori(0, tiles - 2) as t:
                    tile(t, 2)
                tile(tiles - 2, 1)
                tile(tiles - 1, 0)


BLOCKS = 4
ROWS = 100
KEYS = [4 * ROWS] * 3 + [4 * ROWS + 1]
assert sum(KEYS) == S2


def split_weights(nc, ident, tag, weights, outs):
    with ExitStack() as ctx:
        sb, ps, step = allocator(ctx, nc, tag)
        rows = sb("rows", [P, len(weights), DC, D])
        banks = ps("banks", [P, len(weights) * DC, DC, P])
        loaded, turned, high_done, low_done = step("loaded", size=16), step("turned"), step("high"), step("low")
        cases = [(w, r) for w in range(len(weights)) for r in range(DC)]
        with nc.Block() as block:
            @block.sync
            def _(sp):
                for w, weight in enumerate(weights):
                    loaded.done(sp.dma_start(rows[:, w, :, :], weight.rearrange("(r p) n -> p r n", p=P)))

            @block.tensor
            def _(pe):
                loaded.wait(pe, len(weights))
                for n, (w, r) in enumerate(cases):
                    for dc in range(DC):
                        last = pe.transpose(banks[:, n, dc, :], rows[:, w, r, dc * P:(dc + 1) * P], ident[:, :])
                    turned.done(last)

            @block.scalar
            def _(act):
                for n, (w, r) in enumerate(cases):
                    turned.wait(act, n + 1)
                    high_done.done(act.activation(outs[w][0][:, :, r * P:(r + 1) * P], banks[:, n, :, :], ACT.Copy))

            @block.vector
            def _(dve):
                for n, (w, r) in enumerate(cases):
                    high_done.wait(dve, n + 1)
                    low_done.done(dve.tensor_tensor(outs[w][1][:, :, r * P:(r + 1) * P], banks[:, n, :, :],
                                                    words(outs[w][0][:, :, r * P:(r + 1) * P]), ALU.subtract))


def context_keys_values(nc, ident, context, Wk, bk, Wv, bv, kT_out, v_out):
    steps = B * BLOCKS
    with ExitStack() as keep:
        sb, _, _ = allocator(keep, nc, "cx")
        wk = [sb(f"wk_{part}", [P, DC, D], F32R) for part in ("high", "low")]
        wv = [sb(f"wv_{part}", [P, DC, D], F32R) for part in ("high", "low")]
        split_weights(nc, ident, "cxw", [Wk, Wv], [wk, wv])
        with ExitStack() as ctx:
            sb, ps, step = allocator(ctx, nc, "cxl")
            k_bias, v_bias = sb("k_bias", [P, DC]), sb("v_bias", [P, D])
            rows = sb("rows", [P, 2, 4, D])
            WIDE = max(KEYS) + 1
            cT = [[sb(f"cT_{part}{i}", [P, DC, WIDE], F32R) for part in ("high", "low")] for i in range(2)]
            kT = [sb(f"kT_{part}", [P, DC, max(KEYS)], F32R) for part in ("high", "low")]
            v_sb = sb("v", [P, 4, D])
            banks = ps("banks", [P, 4, BANK])
            outs = ps("outs", [P, 4, BANK])

            bias_in = step("bias_in", size=16)
            rows_in = [step(f"rows_in{i}", size=16) for i in range(2)]
            turned = step("turned", ahead=8)
            cT_high, cT_low = step("cT_high"), step("cT_low", ahead=4)
            k_made, k_high, k_low = step("k_made", ahead=4), step("k_high"), step("k_low")
            v_made, v_done = step("v_made", ahead=4), step("v_done", ahead=4)
            k_stored, v_stored = step("k_stored", size=16, ahead=2), step("v_stored", size=16, ahead=2)

            padded = step("padded")

            def even(q):
                return KEYS[q] + KEYS[q] % 2

            def size(q, r):
                return ROWS + (q == BLOCKS - 1 and r == 3)

            def span(q):
                return slice(q * 4 * ROWS, q * 4 * ROWS + KEYS[q])

            def row_parts(dram, b, q, tile):
                first = q * 4 * ROWS
                yield (one(dram, b)[first:first + 4 * ROWS, :].rearrange("(r p) n -> p r n", p=ROWS), tile[0:ROWS, :, :])
                if q == BLOCKS - 1:
                    yield one(dram, b)[S2 - 1:S2, :], tile[ROWS:ROWS + 1, 3, :]

            def group_parts(b, q):
                first = q * 4 * ROWS
                for r in range(4):
                    yield (one(v_out, b)[:, first + r * ROWS:first + r * ROWS + size(q, r), :].rearrange("g p n -> p g n"),
                           v_sb[0:size(q, r), r, :].rearrange("p (g n) -> p g n", n=P))

            with nc.Block() as block:
                @block.sync
                def _(sp):
                    bias_in.done(sp.dma_start(k_bias[:, :], bk.rearrange("(c p) -> p c", p=P),
                                              allow_slow_non_contiguous=True))
                    bias_in.done(sp.dma_start(v_bias[:, :], bv.partition_broadcast(P)))

                    def load(b, q):
                        turned.wait(sp, 4 * (BLOCKS * b + q - 1))
                        for src, dst in row_parts(context, b, q, rows[:, q % 2, :, :]):
                            rows_in[q % 2].done(sp.dma_start(dst, src))

                    def store(b, q):
                        s = BLOCKS * b + q
                        k_low.wait(sp, 4 * (s + 1))
                        for part in range(2):
                            k_stored.done(sp.dma_start(
                                one(kT_out[part], b)[:, span(q)].rearrange("(c p) n -> p c n", p=P),
                                words(kT[part][:, :, 0:KEYS[q]])))
                        v_done.wait(sp, 4 * (s + 1))
                        for dst, src in group_parts(b, q):
                            v_stored.done(sp.dma_start(dst, src))

                    k_stored.open(sp)
                    v_stored.open(sp)
                    with sp.Fori(0, B) as b:
                        load(b, 0)
                        for q in range(BLOCKS):
                            if q + 1 < BLOCKS:
                                load(b, q + 1)
                            store(b, q)
                    k_stored.wait(sp, 2 * steps)
                    v_stored.wait(sp, 4 * steps)

                def rows_arrived(b, q):
                    return (2 + q % 2) * b + q // 2 + 1 + (q == BLOCKS - 1)

                @block.gpsimd
                def _(pool):
                    for n, part in enumerate(cT[(BLOCKS - 1) % 2]):
                        padded.done(pool.memset(words(part[:, :, WIDE - 1:WIDE]), 0.0))
                        padded.wait(pool, n + 1)

                @block.tensor
                def _(pe):
                    def turn(b, q):
                        s = BLOCKS * b + q
                        rows_in[q % 2].wait(pe, rows_arrived(b, q))
                        for r in range(4):
                            cT_low.wait(pe, 4 * (s - 1) + r + 1)
                            n = size(q, r)
                            for dc in range(DC):
                                last = pe.transpose(banks[:, r, dc * n:(dc + 1) * n],
                                                    rows[0:n, q % 2, r, dc * P:(dc + 1) * P], ident[0:n, 0:n])
                            turned.done(last)

                    def keys(b, q):
                        s = BLOCKS * b + q
                        for hd in range(DC):
                            v_done.wait(pe, 4 * (s - 1) + hd + 1)
                            for dc in range(DC):
                                last = matmul3(pe, outs[:, hd, 0:even(q)], [w[:, dc, hd * P:(hd + 1) * P] for w in wk],
                                               [c[:, dc, 0:even(q)] for c in cT[q % 2]], dc == 0, dc == DC - 1)
                            k_made.done(last)

                    def values(b, q):
                        s = BLOCKS * b + q
                        for r in range(4):
                            n, first = size(q, r), r * ROWS
                            k_low.wait(pe, 4 * s + r + 1)
                            for dc in range(DC):
                                last = matmul3(pe, outs[0:n, r, :], [c[:, dc, first:first + n] for c in cT[q % 2]],
                                               [w[:, dc, :] for w in wv], dc == 0, dc == DC - 1)
                            v_made.done(last)

                    padded.wait(pe, 2)
                    turned.open(pe)
                    k_made.open(pe)
                    v_made.open(pe)
                    with pe.Fori(0, B) as b:
                        turn(b, 0)
                        for q in range(BLOCKS):
                            if q + 1 < BLOCKS:
                                turn(b, q + 1)
                            cT_low.wait(pe, 4 * (BLOCKS * b + q + 1))
                            keys(b, q)
                            values(b, q)

                @block.scalar
                def _(act):
                    def high_c(b, q):
                        s = BLOCKS * b + q
                        v_made.wait(act, 4 * (s - 1))
                        for r in range(4):
                            n, first = size(q, r), r * ROWS
                            turned.wait(act, 4 * s + r + 1)
                            cT_high.done(act.activation(
                                cT[q % 2][0][:, :, first:first + n],
                                banks[:, r, 0:DC * n].rearrange("p (c n) -> p c n", c=DC), ACT.Copy))

                    def high_k(b, q):
                        s = BLOCKS * b + q
                        k_stored.wait(act, 2 * s)
                        for hd in range(DC):
                            k_made.wait(act, 4 * s + hd + 1)
                            k_high.done(act.activation(kT[0][:, hd, 0:KEYS[q]], outs[:, hd, 0:KEYS[q]], ACT.Identity,
                                                       bias=k_bias[:, hd:hd + 1]))

                    bias_in.wait(act, 2)
                    with act.Fori(0, B) as b:
                        high_c(b, 0)
                        for q in range(BLOCKS):
                            if q + 1 < BLOCKS:
                                high_c(b, q + 1)
                            high_k(b, q)

                @block.vector
                def _(dve):
                    def low_c(b, q):
                        s = BLOCKS * b + q
                        for r in range(4):
                            n, first = size(q, r), r * ROWS
                            cT_high.wait(dve, 4 * s + r + 1)
                            cT_low.done(dve.tensor_tensor(
                                cT[q % 2][1][:, :, first:first + n],
                                banks[:, r, 0:DC * n].rearrange("p (c n) -> p c n", c=DC),
                                words(cT[q % 2][0][:, :, first:first + n]), ALU.subtract))

                    def low_k(b, q):
                        s = BLOCKS * b + q
                        for hd in range(DC):
                            k_high.wait(dve, 4 * s + hd + 1)
                            k_low.done(dve.scalar_tensor_tensor(
                                kT[1][:, hd, 0:KEYS[q]], outs[:, hd, 0:KEYS[q]], k_bias[:, hd:hd + 1],
                                words(kT[0][:, hd, 0:KEYS[q]]), ALU.add, ALU.subtract))

                    def finish_v(b, q):
                        s = BLOCKS * b + q
                        v_stored.wait(dve, 4 * s)
                        for r in range(4):
                            n = size(q, r)
                            v_made.wait(dve, 4 * s + r + 1)
                            v_done.done(dve.tensor_tensor(v_sb[0:n, r, :], outs[0:n, r, :], v_bias[0:n, :], ALU.add))

                    bias_in.wait(dve, 2)
                    cT_low.open(dve)
                    v_done.open(dve)
                    with dve.Fori(0, B) as b:
                        low_c(b, 0)
                        for q in range(BLOCKS):
                            if q + 1 < BLOCKS:
                                low_c(b, q + 1)
                            low_k(b, q)
                            finish_v(b, q)


MASKED = -1e9
QT = S // P
KT = (S2 + P - 1) // P
LAST = S2 - (KT - 1) * P


def prepare_mask(nc, ident_b, mask, mask_q, mask_t, any_key):
    rows = mask[0, 0].rearrange("(t p) n -> t p n", p=P)
    with ExitStack() as ctx:
        sb, ps, step = allocator(ctx, nc, "mk")
        raw = sb("raw", [P, S2], I32)
        zero = sb("zero", [P, S2], BF16)
        tile = sb("tile", [P, S2], BF16)
        none, some, weight = sb("none", [P, 1]), sb("some", [P, 1]), sb("weight", [P, 1])
        some_b = sb("some_b", [P, P], BF16)
        turned_ps = ps("turned_ps", [P, 2 * 8, P], BF16)
        some_ps = ps("some_ps", [P, BANK])
        raw_in, zeroed, found = step("raw_in", size=16), step("zeroed", ahead=1), step("found", ahead=1)
        weighted, turned, copied, kept = step("weighted"), step("turned", ahead=1), step("copied", ahead=3), step("kept", ahead=1)
        with nc.Block() as block:
            @block.sync
            def _(sp):
                with sp.Fori(0, QT) as t:
                    zeroed.wait(sp, t)
                    raw_in.done(sp.dma_start(raw[:, :], one(rows, t)))

            @block.vector
            def _(dve):
                zeroed.open(dve)
                found.open(dve)
                copied.open(dve)
                with dve.Fori(0, QT) as t:
                    raw_in.wait(dve, t + 1)
                    zeroed.done(dve.tensor_scalar(zero[:, :], raw[:, :], 0.0, None, ALU.is_equal))
                    zeroed.wait(dve, t + 1)
                    dve.tensor_reduce(none[:, :], zero[:, :], AX.X, ALU.min)
                    dve.drain()
                    dve.tensor_scalar(some[:, :], none[:, :], -1.0, 1.0, ALU.mult, ALU.add)
                    dve.tensor_scalar(weight[:, :], none[:, :], -MASKED, MASKED, ALU.mult, ALU.add)
                    dve.drain()
                    turned.wait(dve, t)
                    found.done(dve.tensor_copy(some_b[:, :], some[:, :].broadcast_to([P, P])))
                    kept.wait(dve, t)
                    weighted.done(dve.tensor_scalar(tile[:, :], zero[:, :], weight[:, 0:1], None, ALU.mult))
                    turned.wait(dve, t + 1)
                    here = ds(t * P, P)
                    copied.done(dve.tensor_copy(mask_t[:, 0:KT - 1, here], turned_ps[:, 0:KT - 1, :]))
                    copied.done(dve.tensor_copy(mask_t[0:LAST, KT - 1, here], turned_ps[0:LAST, KT - 1, :]))
                    copied.done(dve.tensor_copy(any_key[:, here], some_ps[:, 0:P]))

            @block.tensor
            def _(pe):
                turned.open(pe)
                with pe.Fori(0, QT) as t:
                    copied.wait(pe, 3 * t)
                    found.wait(pe, t + 1)
                    pe.matmul(some_ps[:, 0:P], some_b[:, :], ident_b[:, :], start=True, stop=True)
                    weighted.wait(pe, t + 1)
                    for n in range(KT):
                        keys = min(P, S2 - n * P)
                        last = pe.transpose(turned_ps[0:keys, n, :], tile[:, n * P:n * P + keys], ident_b[:, :])
                    turned.done(last)

            @block.scalar
            def _(act):
                kept.open(act)
                with act.Fori(0, QT) as t:
                    weighted.wait(act, t + 1)
                    kept.done(act.activation(mask_q[:, ds(t, 1), :].squeeze(1), tile[:, :], ACT.Copy))


class LayerNorm:

    def __init__(self, sb, step, R):
        self.R = R
        self.stats, self.mean_var = sb("ln_stats", [P, R, 6]), sb("ln_mean_var", [P, R, 2])
        self.var, self.rstd, self.power = sb("ln_var", [P, R]), sb("ln_rstd", [P, R]), sb("ln_power", [P, R])
        self.constant, self.stat, self.root = step("ln_constant"), step("ln_stat"), step("ln_root", ahead=1)

    def pool_setup(self, pool):
        self.root.open(pool)
        self.constant.done(pool.memset(self.power[:, :], -0.5))
        self.constant.wait(pool, 1)

    def pool_step(self, pool, s):
        self.stat.wait(pool, s + 1)
        self.root.done(pool.tensor_tensor(self.rstd[:, :], self.var[:, :], self.power[:, :], ALU.pow))

    def statistics(self, dve, rows, s):
        self.root.wait(dve, s)
        for r in range(self.R):
            dve.bn_stats(self.stats[:, r, :], rows[:, r, :])
        dve.drain()
        for r in range(self.R):
            dve.bn_aggr(self.mean_var[:, r, :], self.stats[:, r, :])
        dve.drain()
        self.stat.done(dve.tensor_scalar_add(self.var[:, :], self.mean_var[:, :, 1], EPS))

    def normalize(self, dve, out, rows, s):
        self.root.wait(dve, s + 1)
        for r in range(self.R):
            last = dve.tensor_scalar(out[:, r, :], rows[:, r, :], self.mean_var[:, r, 0:1], self.rstd[:, r:r + 1],
                                     ALU.subtract, ALU.mult)
        return last


def project_queries(nc, ident, x1, Wq, bq, any_key, qT_out):
    steps = TOK // BANK
    R = BANK // P
    x_rows = x1.rearrange("(s r p) n -> s p r n", p=P, r=R)
    with ExitStack() as keep:
        sb, _, _ = allocator(keep, nc, "pq")
        wq = [sb(f"wq_{part}", [P, DC, D], F32R) for part in ("high", "low")]
        split_weights(nc, ident, "pqw", [Wq], [wq])
        with ExitStack() as ctx:
            sb, ps, step = allocator(ctx, nc, "pql")
            q_bias = sb("q_bias", [P, DC])
            rows = sb("rows", [P, R, D])
            normed = sb("normed", [P, R, D])
            norm = LayerNorm(sb, step, R)
            nT = [[sb(f"nT_{part}{i}", [P, DC, BANK], F32R) for part in ("high", "low")] for i in range(2)]
            q = sb("q", [P, DC, BANK])
            qT = [sb(f"qT_{part}", [P, DC, BANK], F32R) for part in ("high", "low")]
            banks, outs = ps("banks", [P, R, DC, P]), ps("outs", [P, DC, BANK])
            bias_in, rows_in = step("bias_in", size=16), step("rows_in", size=16)
            normal = step("normal", ahead=1)
            turned = step("turned", ahead=R)
            high_n, low_n = step("high_n"), step("low_n", ahead=R)
            made = step("made", ahead=2 * DC)
            q_done = step("q_done", ahead=DC)
            high_q, low_q, stored = step("high_q"), step("low_q", ahead=DC), step("stored", size=16, ahead=2)

            with nc.Block() as block:
                @block.sync
                def _(sp):
                    bias_in.done(sp.dma_start(q_bias[:, :], bq.rearrange("(c p) -> p c", p=P),
                                              allow_slow_non_contiguous=True))
                    stored.open(sp)
                    with sp.Fori(0, B) as b:
                        for half in range(2):
                            normal.wait(sp, 2 * b + half)
                            rows_in.done(sp.dma_start(rows[:, :, :], one(x_rows, 2 * b + half)))
                        for half in range(2):
                            low_q.wait(sp, DC * (2 * b + half + 1))
                            for part in range(2):
                                dst = one(qT_out[part], b).rearrange("(c p) n -> p c n", p=P)
                                stored.done(sp.dma_start(dst[:, :, half * BANK:(half + 1) * BANK],
                                                         words(qT[part][:, :, :])))
                    stored.wait(sp, 2 * steps)

                @block.gpsimd
                def _(pool):
                    norm.pool_setup(pool)
                    with pool.Fori(0, steps) as s:
                        norm.pool_step(pool, s)

                @block.tensor
                def _(pe):
                    turned.open(pe)
                    made.open(pe)
                    with pe.Fori(0, B) as b:
                        for half in range(2):
                            s = 2 * b + half
                            normal.wait(pe, s + 1)
                            for r in range(R):
                                low_n.wait(pe, R * (s - 1) + r + 1)
                                for dc in range(DC):
                                    last = pe.transpose(banks[:, r, dc, :], normed[:, r, dc * P:(dc + 1) * P], ident[:, :])
                                turned.done(last)
                        for half in range(2):
                            s = 2 * b + half
                            low_n.wait(pe, R * (s + 1))
                            for hd in range(DC):
                                q_done.wait(pe, DC * (s - 1) + hd + 1)
                                for dc in range(DC):
                                    last = matmul3(pe, outs[:, hd, :], [w[:, dc, hd * P:(hd + 1) * P] for w in wq],
                                                   [n[:, dc, :] for n in nT[half]], dc == 0, dc == DC - 1)
                                made.done(last)

                @block.scalar
                def _(act):
                    with act.Fori(0, B) as b:
                        for half in range(2):
                            s = 2 * b + half
                            made.wait(act, DC * (s - 1))
                            for r in range(R):
                                turned.wait(act, R * s + r + 1)
                                high_n.done(act.activation(nT[half][0][:, :, r * P:(r + 1) * P], banks[:, r, :, :],
                                                           ACT.Copy))
                        for half in range(2):
                            s = 2 * b + half
                            stored.wait(act, 2 * s)
                            for hd in range(DC):
                                q_done.wait(act, DC * s + hd + 1)
                                high_q.done(act.activation(qT[0][:, hd, :], q[:, hd, :], ACT.Copy))

                @block.vector
                def _(dve):
                    for s in (normal, low_n, q_done, low_q):
                        s.open(dve)
                    bias_in.wait(dve, 1)
                    with dve.Fori(0, B) as b:
                        for half in range(2):
                            s = 2 * b + half
                            rows_in.wait(dve, s + 1)
                            norm.statistics(dve, rows, s)
                            turned.wait(dve, R * s)
                            normal.done(norm.normalize(dve, normed, rows, s))
                            for r in range(R):
                                high_n.wait(dve, R * s + r + 1)
                                low_n.done(dve.tensor_tensor(nT[half][1][:, :, r * P:(r + 1) * P], banks[:, r, :, :],
                                                             words(nT[half][0][:, :, r * P:(r + 1) * P]), ALU.subtract))
                        for half in range(2):
                            s = 2 * b + half
                            for hd in range(DC):
                                made.wait(dve, DC * s + hd + 1)
                                low_q.wait(dve, DC * (s - 1) + hd + 1)
                                q_done.done(dve.scalar_tensor_tensor(
                                    q[:, hd, :], outs[:, hd, :], q_bias[:, hd:hd + 1],
                                    any_key[:, half * BANK:(half + 1) * BANK], ALU.add, ALU.mult))
                            stored.wait(dve, 2 * s)
                            for hd in range(DC):
                                high_q.wait(dve, DC * s + hd + 1)
                                low_q.done(dve.tensor_tensor(qT[1][:, hd, :], q[:, hd, :], words(qT[0][:, hd, :]),
                                                             ALU.subtract))


GROUPS = D // P
GH = H // GROUPS
PAIRS = GH // 2


def cross_attention(nc, ident, ident_b, kT, qT, v, mask_q, mask_t, row, oT):
    HALF = S // BANK
    units = B * GROUPS * HALF
    QB = BANK // P
    MB, MKEYS = 4, 402
    MFIRST = [0, 400, 800, S2 - MKEYS]
    SLOTS = GH * QB * MB
    SLOTS_OF = [2, 8, 8, 6, 8, 8, 7, 9, 8] + [0] * (KT - 9)
    SLOT_OF = [sum(SLOTS_OF[:n]) for n in range(KT + 1)]
    assert SLOT_OF[KT] == SLOTS
    TURN = 9
    OWN = {"dve": (3, 6, 10), "pool": (0, 1, 2, 4, 5, 7, 8, 9, 11)}
    POOL_ADDS, DVE_ADDS = len(OWN["pool"]) - 1, len(OWN["dve"])
    RING = 4
    LOADS = 8
    SCALE = float(1.0 / np.sqrt(np.float32(DK)))
    MAXROW = 3 * DK
    ROWS97 = MAXROW + 1

    with ExitStack() as ctx:
        sb, ps, step = allocator(ctx, nc, "xa")
        kp = [sb(f"kp{i}", [P, GH, S2], F32R) for i in range(2)]
        qp = [sb(f"qp{i}", [P, GH, S], F32R) for i in range(2)]
        vg = [sb(f"vg{i}", [P, KT, P]) for i in range(2)]
        prob = [[sb(f"prob{i}{pr}", [P, 2, BANK]) for pr in range(PAIRS)] for i in range(RING)]
        sums = {who: [sb(f"sums_{who}{pr}", [P, 2, BANK]) for pr in range(PAIRS)] for who in OWN}
        ones = sb("ones", [P, DK])
        unread = [sb(f"unread{i}", [P, MKEYS], BF16) for i in range(2)]
        maxima, neg_max = sb("maxima", [P, GH * QB, MB]), sb("neg_max", [P, GH * QB])
        max_row = sb("max_row", [GH * QB, P], F32R)
        o_sb, sum_sb, out = sb("o_sb", [P, BANK]), sb("sum_sb", [P, BANK]), sb("out", [P, BANK])
        scores = [ps(f"scores{pr}", [P, 2, BANK]) for pr in range(PAIRS)]
        o_ps = ps("o_ps", [P, BANK])
        mx_ps = [ps(f"mx_ps{i}", [P, BANK]) for i in range(3)]
        peak_ps, sum_ps = mx_ps[0], mx_ps[1]

        loaded = step("loaded", size=16)
        const = step("const")
        mx_made, mx_read = step("mx_made"), step("mx_read", ahead=3)
        carried = step("carried")
        peaks = step("peaks", ahead=1)
        row_made = step("row_made")
        row_kept = step("row_kept", ahead=1)
        row_out, row_in = step("row_out", size=16, ahead=1), step("row_in", size=16)
        scored, exped = step("scored"), step("exped", ahead=PAIRS)
        weighed = step("weighed", ahead=RING)
        pool_added = step("pool_added", ahead=PAIRS * POOL_ADDS)
        dve_added = step("dve_added", ahead=PAIRS * DVE_ADDS)
        total_made = step("total_made", ahead=1)
        o_kept, sum_kept = step("o_kept", ahead=1), step("sum_kept", ahead=1)
        inverted, finished = step("inverted", ahead=1), step("finished", ahead=1)
        stored = step("stored", size=16, ahead=1)

        def keys_of(kt):
            return LAST if kt == KT - 1 else P

        def wait_added(eng, u, kt):
            if kt < 0:
                u, kt = u - 1, kt + KT
            if kt == KT - 1:
                return
            if kt in OWN["dve"]:
                dve_added.wait(eng, PAIRS * (DVE_ADDS * u + OWN["dve"].index(kt) + 1))
            else:
                pool_added.wait(eng, PAIRS * (POOL_ADDS * u + max(OWN["pool"].index(kt), 1)))

        def loops(eng, unit):
            def four(first, last):
                for n in range(2 * HALF):
                    unit(first + n, n // HALF, n % HALF, (KT * n) % RING, not (last and n == 2 * HALF - 1))

            with eng.Fori(0, units // (2 * HALF) - 1) as it:
                four(it * (2 * HALF), False)
            four(units - 2 * HALF, True)

        with nc.Block() as block:
            @block.sync
            def _(sp):
                def load(i, par):
                    for dst, (high_or_low, first) in enumerate(((0, 0), (0, DK), (1, 2 * DK))):
                        loaded.done(sp.dma_start(words(kp[par][first:first + DK, :, :]),
                                                 one(kT[high_or_low], i).rearrange("(j p) n -> p j n", p=DK)))
                    for dst, (high_or_low, first) in enumerate(((0, 0), (1, DK), (0, 2 * DK))):
                        loaded.done(sp.dma_start(words(qp[par][first:first + DK, :, :]),
                                                 one(qT[high_or_low], i).rearrange("(j p) n -> p j n", p=DK)))
                    whole = (KT - 1) * P
                    loaded.done(sp.dma_start(vg[par][:, 0:KT - 1, :],
                                             one(v, i)[0:whole, :].rearrange("(t p) n -> p t n", p=P)))
                    loaded.done(sp.dma_start(vg[par][0:LAST, KT - 1, :], one(v, i)[whole:S2, :]))

                def set_row(u, par, half):
                    row_kept.wait(sp, u + 1)
                    row_out.done(sp.dma_start(row, words(max_row[:, :])))
                    row_out.wait(sp, u + 1)
                    row_in.done(sp.dma_start(words(qp[par][MAXROW:ROWS97, :, half * BANK:(half + 1) * BANK]),
                                             row.rearrange("(o j t) n -> o j (t n)", o=1, j=GH)))

                def unit(u, par, half, _, more):
                    if half == 0 and not (isinstance(u, int) and u == units - HALF):
                        weighed.wait(sp, u * KT)
                        load_index = (u // HALF) + 1
                        load(load_index, 1 - par)
                    if more:
                        set_row(u + 1, par if half == 0 else 1 - par, 1 - half)
                    finished.wait(sp, u + 1)
                    stored.done(sp.dma_start(one(oT, u // HALF)[:, half * BANK:(half + 1) * BANK], out[:, :]))

                row_out.open(sp)
                stored.open(sp)
                load(0, 0)
                set_row(0, 0, 0)
                loops(sp, unit)
                stored.wait(sp, units)

            @block.gpsimd
            def _(pool):
                const.done(pool.memset(ones[:, :], 1.0))
                for i in range(2):
                    const.wait(pool, i + 1)
                    const.done(pool.memset(words(kp[i][MAXROW:ROWS97, :, :]), 1.0))

                def add(u, kt, left, right):
                    for pr in range(PAIRS):
                        exped.wait(pool, PAIRS * (KT * u + kt) + pr + 1)
                        pool_added.done(pool.tensor_tensor(sums["pool"][pr][:, :, :], left[pr][:, :, :],
                                                           right[pr][:, :, :], ALU.add))

                def unit(u, par, half, at, more):
                    total_made.wait(pool, u)
                    add(u, 1, prob[at], prob[(at + 1) % RING])
                    for n, kt in enumerate(OWN["pool"][2:]):
                        pool_added.wait(pool, PAIRS * (POOL_ADDS * u + n + 1))
                        add(u, kt, sums["pool"], prob[(at + kt) % RING])

                pool_added.open(pool)
                loops(pool, unit)

            @block.tensor
            def _(pe):
                def mx(u, par, half, slot):
                    j, qt, kb = slot // (QB * MB), slot // MB % QB, slot % MB
                    m = SLOTS * u + slot
                    mx_read.wait(pe, m - 2)
                    first = half * BANK + qt * P
                    mx_made.done(pe.matmul(mx_ps[slot % 3][:, 0:MKEYS], qp[par][0:MAXROW, j, first:first + P],
                                           kp[par][0:MAXROW, j, MFIRST[kb]:MFIRST[kb] + MKEYS], start=True, stop=True))

                def turn_peaks(u):
                    peaks.wait(pe, u + 1)
                    row_made.done(pe.transpose(peak_ps[0:GH * QB, 0:P], neg_max[:, :], ident[:, :]))

                def score(u, par, half, kt, pr, between):
                    keys = keys_of(kt)
                    if kt == 0 and pr == 0:
                        row_in.wait(pe, u + 1)
                    queries = slice(half * BANK, (half + 1) * BANK)
                    exped.wait(pe, PAIRS * (KT * u + kt - 1) + pr + 1)
                    for jj in range(2):
                        j = 2 * pr + jj
                        pe.matmul(scores[pr][0:keys, jj, :], kp[par][0:ROWS97, j, kt * P:kt * P + keys],
                                  qp[par][0:ROWS97, j, queries], start=True, stop=False)
                        last = pe.matmul(scores[pr][0:keys, jj, :], ident_b[0:keys, 0:keys],
                                         mask_t[0:keys, kt, queries], start=False, stop=True)
                        if jj == 1:
                            scored.done(last)
                        between()

                def four_heads(total, left, right, start, stop):
                    for j in range(GH):
                        mine = slice(j * DK, (j + 1) * DK)
                        last = pe.matmul(total[mine, :], left(mine), right[j // 2][0:left(mine).shape[0], j % 2, :],
                                         start=start, stop=stop, tile_position=(0, j * DK))
                    return last

                def weigh(u, par, kt, ring):
                    keys = keys_of(kt)
                    if kt == 0:
                        o_kept.wait(pe, u)
                    exped.wait(pe, PAIRS * (KT * u + kt + 1))
                    if kt == KT - 1:
                        sum_kept.wait(pe, u)
                        four_heads(sum_ps, lambda mine: ones[0:keys, :], prob[ring], True, False)
                    weighed.done(four_heads(o_ps, lambda mine: vg[par][0:keys, kt, mine], prob[ring],
                                            kt == 0, kt == KT - 1))

                def add_up(u):
                    wait_added(pe, u, OWN["dve"][-1])
                    four_heads(sum_ps, lambda mine: ones[:, :], sums["dve"], False, False)
                    wait_added(pe, u, OWN["pool"][-1])
                    total_made.done(four_heads(sum_ps, lambda mine: ones[:, :], sums["pool"], False, True))

                def unit(u, par, half, at, more):
                    nxt = (par if half == 0 else 1 - par, 1 - half)
                    for kt in range(KT):
                        if more and kt == 0:
                            row_kept.wait(pe, u + 1)
                            sum_kept.wait(pe, u)
                            if half == 1:
                                loaded.wait(pe, LOADS * (u // HALF + 2))
                        slots = iter(range(SLOT_OF[kt], SLOT_OF[kt + 1]) if more else ())

                        def maximum():
                            for slot in itertools.islice(slots, 1):
                                mx(u + 1, *nxt, slot)

                        for pr in range(PAIRS):
                            if kt + 1 < KT:
                                score(u, par, half, kt + 1, pr, maximum)
                            elif more:
                                score(u + 1, *nxt, 0, pr, maximum)
                        if more and kt == TURN:
                            turn_peaks(u + 1)
                        if SLOTS_OF[kt] > 6:
                            maximum()
                        weigh(u, par, kt, (at + kt) % RING)
                        for _ in range(SLOTS_OF[kt]):
                            maximum()
                    add_up(u)

                weighed.open(pe)
                total_made.open(pe)
                const.wait(pe, 3)
                loaded.wait(pe, LOADS)
                for slot in range(SLOTS):
                    mx(0, 0, 0, slot)
                turn_peaks(0)
                for pr in range(PAIRS):
                    score(0, 0, 0, 0, pr, lambda: None)
                loops(pe, unit)

            @block.scalar
            def _(act):
                def keep_row(u):
                    row_made.wait(act, u + 1)
                    row_out.wait(act, u)
                    row_kept.done(act.activation(max_row[:, :], peak_ps[0:GH * QB, 0:P], ACT.Copy))

                def exp(u, kt, ring):
                    n, keys = KT * u + kt, keys_of(kt)
                    weighed.wait(act, n - RING + 1)
                    wait_added(act, u, kt - RING)
                    for pr in range(PAIRS):
                        scored.wait(act, PAIRS * n + pr + 1)
                        exped.done(act.activation(prob[ring][pr][0:keys, :, :], scores[pr][0:keys, :, :], ACT.Exp,
                                                  scale=SCALE))

                def unit(u, par, half, at, more):
                    for kt in range(KT):
                        if kt + 1 < KT:
                            exp(u, kt + 1, (at + kt + 1) % RING)
                        elif more:
                            exp(u + 1, 0, (at + KT) % RING)
                        if more and kt == TURN:
                            keep_row(u + 1)
                    weighed.wait(act, KT * (u + 1))
                    finished.wait(act, u)
                    o_kept.done(act.activation(o_sb[:, :], o_ps[:, :], ACT.Copy))
                    total_made.wait(act, u + 1)
                    sum_kept.done(act.activation(sum_sb[:, :], sum_ps[:, :], ACT.Copy))

                for s in (row_kept, exped, o_kept, sum_kept):
                    s.open(act)
                keep_row(0)
                exp(0, 0, 0)
                loops(act, unit)

            @block.vector
            def _(dve):
                def read(u, half, slot):
                    j_qt, kb, qt = slot // MB, slot % MB, slot // MB % QB
                    m = SLOTS * u + slot
                    mx_read.wait(dve, m - 1)
                    mx_made.wait(dve, m + 1)
                    dve.sem_inc(carried.sem, 1)
                    mx_read.done(dve.tensor_tensor_reduce(
                        out=unread[slot % 2][:, :], in0=mx_ps[slot % 3][:, 0:MKEYS],
                        in1=mask_q[:, half * QB + qt, MFIRST[kb]:MFIRST[kb] + MKEYS], scale=1.0, scalar=LOWEST,
                        op0=ALU.add, op1=ALU.max, accum_out=maxima[:, j_qt, kb:kb + 1]))

                def peak(u):
                    mx_read.wait(dve, SLOTS * (u + 1))
                    row_made.wait(dve, u)
                    peaks.done(dve.tensor_reduce(neg_max[:, :], maxima[:, :, :], AX.X, ALU.max, negate=True))

                def add(u, kt, ring, i, pr):
                    if i == 0:
                        total_made.wait(dve, u)
                    else:
                        dve_added.wait(dve, PAIRS * (DVE_ADDS * u + i))
                    exped.wait(dve, PAIRS * (KT * u + kt) + pr + 1)
                    mine, new = sums["dve"][pr][:, :, :], prob[ring][pr][:, :, :]
                    dve_added.done(dve.tensor_tensor(mine, mine, new, ALU.add) if i else dve.tensor_copy(mine, new))

                def unit(u, par, half, at, more):
                    for kt in range(KT):
                        for pr in range(PAIRS):
                            middle = (SLOT_OF[kt] + SLOT_OF[kt + 1]) // 2
                            mine = (SLOT_OF[kt], middle) if pr == 0 else (middle, SLOT_OF[kt + 1])
                            for slot in range(*mine) if more else ():
                                read(u + 1, 1 - half, slot)
                            if kt in OWN["dve"]:
                                add(u, kt, (at + kt) % RING, OWN["dve"].index(kt), pr)
                        if more and kt == TURN - 1:
                            peak(u + 1)
                    sum_kept.wait(dve, u + 1)
                    inverted.done(dve.reciprocal(sum_sb[:, :], sum_sb[:, :]))
                    inverted.wait(dve, u + 1)
                    o_kept.wait(dve, u + 1)
                    stored.wait(dve, u)
                    finished.done(dve.tensor_tensor(out[:, :], o_sb[:, :], sum_sb[:, :], ALU.mult))

                for s in (mx_read, peaks, dve_added, finished, inverted):
                    s.open(dve)
                for slot in range(SLOTS):
                    read(0, 0, slot)
                peak(0)
                loops(dve, unit)


def split_plain(nc, tag, pieces):
    with ExitStack() as ctx:
        sb, _, step = allocator(ctx, nc, tag)
        widest = max(high.shape[1] for _, high, _ in pieces)
        stage = [sb(f"stage{i}", [P, widest]) for i in range(2)]
        loaded = [step(f"loaded{i}", size=16) for i in range(2)]
        high_done, low_done = step("high"), step("low", ahead=2)

        def staged(n):
            return stage[n % 2][:, 0:pieces[n][1].shape[1]]

        with nc.Block() as block:
            @block.sync
            def _(sp):
                for n, (src, _, _) in enumerate(pieces):
                    low_done.wait(sp, n - 1)
                    loaded[n % 2].done(sp.dma_start(staged(n), src))

            @block.scalar
            def _(act):
                for n, (_, high, _) in enumerate(pieces):
                    loaded[n % 2].wait(act, n // 2 + 1)
                    high_done.done(act.activation(high, staged(n), ACT.Copy))

            @block.vector
            def _(dve):
                low_done.open(dve)
                for n, (_, high, low) in enumerate(pieces):
                    high_done.wait(dve, n + 1)
                    low_done.done(dve.tensor_tensor(low, staged(n), words(high), ALU.subtract))


def hidden_layers(nc, ident, oT, Wo, bo, x1, w_in, w_gate, gate_bias, x2, hT, weights):
    R = BANK // P
    steps = TOK // BANK
    NH = 2 * DC
    x_rows = x1.rearrange("(s r p) n -> s p r n", p=P, r=R)
    x2_rows = x2.rearrange("(s r p) n -> s p r n", p=P, r=R)
    oT_half = oT.rearrange("(b g) p n -> b p g n", g=GROUPS)
    hT_rows = hT.rearrange("(s r) p w c n -> s w p c r n", r=R)
    with ExitStack() as keep:
        sb, _, _ = allocator(keep, nc, "hd")
        parts = ("high", "low")
        wo = [sb(f"wo_{part}", [P, DC, D], F32R) for part in parts]
        wi = [[sb(f"wi{w}_{part}", [P, DC, 2 * D], F32R) for part in parts] for w in range(2)]
        wg = [sb(f"wg_{part}", [P, DC, E], F32R) for part in parts]
        split_weights(nc, ident, "hdo", [Wo], [wo])
        split_plain(nc, "hdi", [(w_in[w][dc * P:(dc + 1) * P, :], wi[w][0][:, dc, :], wi[w][1][:, dc, :])
                                for w in range(2) for dc in range(DC)]
                    + [(w_gate[dc * P:(dc + 1) * P, :], wg[0][:, dc, :], wg[1][:, dc, :]) for dc in range(DC)])
        with ExitStack() as ctx:
            sb, ps, step = allocator(ctx, nc, "hdl")
            o_bias, g_bias = sb("o_bias", [P, D]), sb("g_bias", [P, E])
            o_in = sb("o_in", [P, GROUPS, BANK])
            o_parts = [sb(f"o_{part}", [P, GROUPS, BANK], F32R) for part in parts]
            rows, rows2 = sb("rows", [P, R, D]), sb("rows2", [P, R, D])
            norm = LayerNorm(sb, step, R)
            nT = [[sb(f"nT_{part}{i}", [P, DC, BANK], F32R) for part in parts] for i in range(2)]
            gated = [sb(f"gated{i}", [P, BANK]) for i in range(2)]
            hidden = [sb(f"hidden{w}", [P, DC, BANK]) for w in range(2)]
            logits_t = sb("logits_t", [P, BANK])
            logits, probs = sb("logits", [P, R, E]), sb("probs", [P, R, E])
            top, sums, inv_sums = sb("top", [P, R]), sb("sums", [P, R]), sb("inv_sums", [P, R])
            best, best_at, best_at_f = sb("best", [P, R, 8]), sb("best_at", [P, R, 8], U32), sb("best_at_f", [P, R, 8])
            number = sb("number", [P, E])
            second = sb("second", [P, R, E])
            proj_ps = [ps(f"proj_ps{i}", [P, BANK]) for i in range(2)]
            turn_ps = ps("turn_ps", [P, DC, P])
            pair_ps = [ps(f"pair_ps{i}", [P, 2, BANK]) for i in range(2)]
            gate_ps = ps("gate_ps", [P, BANK])

            setup_in, const = step("setup_in", size=16), step("const")
            o_loaded, x_loaded = step("o_loaded", size=16), step("x_loaded", size=16)
            o_high, o_low = step("o_high", ahead=1), step("o_low", ahead=1)
            biased = step("biased")
            projected, added = step("projected", ahead=R), step("added", ahead=2)
            x2_stored = step("x2_stored", size=16, ahead=1)
            normal, turned = step("normal", ahead=1), step("turned")
            high_n, low_n = step("high_n"), step("low_n", ahead=1)
            paired, silu, hid = step("paired"), step("silu"), step("hid", ahead=2)
            h_stored = [step(f"h_stored{w}", size=16, ahead=R) for w in range(2)]
            gated_t, gate_kept, gate_turned = step("gated_t", ahead=1), step("gate_kept", ahead=1), step("gate_turned", ahead=1)
            shifted, gate_exp, routed = step("shifted"), step("gate_exp"), step("routed", ahead=1)

            def loops(eng, body):
                with eng.Fori(0, B - 1) as b:
                    for half in range(2):
                        body(2 * b + half, half, True)
                body(steps - 2, 0, True)
                body(steps - 1, 1, False)

            with nc.Block() as block:
                @block.sync
                def _(sp):
                    setup_in.done(sp.dma_start(o_bias[:, :], bo.partition_broadcast(P)))
                    setup_in.done(sp.dma_start(g_bias[:, :], gate_bias.partition_broadcast(P)))

                    def load(s, half):
                        o_low.wait(sp, s)
                        b = s // 2
                        o_loaded.done(sp.dma_start(o_in[:, :, :], one(oT_half, b)[:, :, half * BANK:(half + 1) * BANK]))
                        x2_stored.wait(sp, s)
                        normal.wait(sp, s)
                        x_loaded.done(sp.dma_start(rows[:, :, :], one(x_rows, s)))

                    def store_x2(s):
                        added.wait(sp, R * (s + 1))
                        x2_stored.done(sp.dma_start(one(x2_rows, s), rows[:, :, :]))

                    def body(s, half, more):
                        if more:
                            load(s + 1, 1 - half)
                            store_x2(s + 1)
                        for w in range(2):
                            hid.wait(sp, NH * s + DC * (w + 1))
                            for r in range(R):
                                h_stored[w].done(sp.dma_start(one(hT_rows, s)[w, :, :, r, :],
                                                              hidden[w][:, :, r * P:(r + 1) * P]))

                    x2_stored.open(sp)
                    for w in range(2):
                        h_stored[w].open(sp)
                    load(0, 0)
                    store_x2(0)
                    loops(sp, body)
                    x2_stored.wait(sp, steps)
                    for w in range(2):
                        h_stored[w].wait(sp, R * steps)

                @block.gpsimd
                def _(pool):
                    norm.pool_setup(pool)
                    for e in range(E):
                        const.done(pool.memset(number[:, e:e + 1], float(e)))
                        const.wait(pool, e + 1)
                    const.done(pool.memset(logits_t[:, :], 0.0))
                    setup_in.wait(pool, 2)
                    with pool.Fori(0, steps) as s:
                        x_loaded.wait(pool, s + 1)
                        for r in range(R):
                            last = pool.tensor_tensor(rows[:, r, :], rows[:, r, :], o_bias[:, :], ALU.add)
                            biased.done(last)
                            biased.wait(pool, R * s + r + 1)
                        norm.pool_step(pool, s)

                @block.tensor
                def _(pe):
                    def project(s):
                        o_low.wait(pe, s + 1)
                        for r in range(R):
                            added.wait(pe, R * s + r - 1)
                            for g in range(GROUPS):
                                last = matmul3(pe, proj_ps[r % 2][:, :], [o[:, g, r * P:(r + 1) * P] for o in o_parts],
                                               [w[:, g, :] for w in wo], g == 0, g == GROUPS - 1)
                            projected.done(last)

                    def turn(s):
                        normal.wait(pe, s + 1)
                        for r in range(R):
                            low_n.wait(pe, R * s + r)
                            for dc in range(DC):
                                last = pe.transpose(turn_ps[:, dc, :], rows2[:, r, dc * P:(dc + 1) * P], ident[:, :])
                            turned.done(last)

                    def pair(s, half, n):
                        w, c = n // DC, n % DC
                        hid.wait(pe, NH * s + n - 1)
                        for side in range(2):
                            cols = slice(side * D + c * P, side * D + (c + 1) * P)
                            for dc in range(DC):
                                last = matmul3(pe, pair_ps[n % 2][:, side, :], [x[:, dc, cols] for x in wi[w]],
                                               [x[:, dc, :] for x in nT[half]], dc == 0, dc == DC - 1)
                        paired.done(last)

                    def gate(s, half):
                        routed.wait(pe, s)
                        for dc in range(DC):
                            last = matmul3(pe, gate_ps[0:E, :], [x[:, dc, :] for x in wg],
                                           [x[:, dc, :] for x in nT[half]], dc == 0, dc == DC - 1)
                        gated_t.done(last)

                    def turn_gate(s):
                        gate_kept.wait(pe, s + 1)
                        for r in range(R):
                            last = pe.transpose(gate_ps[:, r * P:(r + 1) * P], logits_t[:, r * P:(r + 1) * P], ident[:, :])
                        gate_turned.done(last)

                    def body(s, half, more):
                        if more:
                            project(s + 1)
                        low_n.wait(pe, R * (s + 1))
                        for n in range(NH // 2):
                            pair(s, half, n)
                        if more:
                            turn(s + 1)
                        gate(s, half)
                        for n in range(NH // 2, NH):
                            pair(s, half, n)
                        turn_gate(s)

                    for st in (projected, gated_t, gate_turned):
                        st.open(pe)
                    project(0)
                    turn(0)
                    loops(pe, body)

                @block.scalar
                def _(act):
                    def split_o(s):
                        o_loaded.wait(act, s + 1)
                        projected.wait(act, R * s)
                        o_high.done(act.activation(o_parts[0][:, :, :], o_in[:, :, :], ACT.Copy))

                    def split_n(s, half):
                        for r in range(R):
                            turned.wait(act, R * s + r + 1)
                            high_n.done(act.activation(nT[half][0][:, :, r * P:(r + 1) * P], turn_ps[:, :, :], ACT.Copy))

                    def activate(s, n):
                        hid.wait(act, NH * s + n - 1)
                        paired.wait(act, NH * s + n + 1)
                        silu.done(act.activation(gated[n % 2][:, :], pair_ps[n % 2][:, 0, :], ACT.Silu))

                    def body(s, half, more):
                        if more:
                            split_o(s + 1)
                        for n in range(NH // 2):
                            activate(s, n)
                        if more:
                            split_n(s + 1, 1 - half)
                        gated_t.wait(act, s + 1)
                        gate_turned.wait(act, s)
                        gate_kept.done(act.activation(logits_t[0:E, :], gate_ps[0:E, :], ACT.Copy))
                        for n in range(NH // 2, NH):
                            activate(s, n)
                        shifted.wait(act, s + 1)
                        gate_exp.done(act.activation(probs[:, :, :], logits[:, :, :], ACT.Exp))

                    o_high.open(act)
                    gate_kept.open(act)
                    const.wait(act, E + 1)
                    split_o(0)
                    split_n(0, 0)
                    loops(act, body)

                @block.vector
                def _(dve):
                    def split_o(s):
                        o_high.wait(dve, s + 1)
                        projected.wait(dve, R * s)
                        o_low.done(dve.tensor_tensor(o_parts[1][:, :, :], o_in[:, :, :], words(o_parts[0][:, :, :]),
                                                     ALU.subtract))

                    def add(s):
                        for r in range(R):
                            biased.wait(dve, R * s + r + 1)
                            projected.wait(dve, R * s + r + 1)
                            added.done(dve.tensor_tensor(rows[:, r, :], proj_ps[r % 2][:, :], rows[:, r, :], ALU.add))
                        added.wait(dve, R * (s + 1))
                        norm.statistics(dve, rows, s)
                        turned.wait(dve, R * s)
                        normal.done(norm.normalize(dve, rows2, rows, s))

                    def split_n(s, half):
                        for r in range(R):
                            high_n.wait(dve, R * s + r + 1)
                            low_n.done(dve.tensor_tensor(nT[half][1][:, :, r * P:(r + 1) * P], turn_ps[:, :, :],
                                                         words(nT[half][0][:, :, r * P:(r + 1) * P]), ALU.subtract))

                    def multiply(s, n):
                        w, c = n // DC, n % DC
                        if c == 0:
                            h_stored[w].wait(dve, R * s)
                        silu.wait(dve, NH * s + n + 1)
                        hid.done(dve.tensor_tensor(hidden[w][:, c, :], gated[n % 2][:, :], pair_ps[n % 2][:, 1, :],
                                                   ALU.mult))

                    def route(s):
                        gate_turned.wait(dve, s + 1)
                        for r in range(R):
                            last = dve.tensor_tensor(logits[:, r, :], gate_ps[:, r * P:r * P + E], g_bias[:, :], ALU.add)
                        dve.drain()
                        dve.tensor_reduce(top[:, :], logits[:, :, :], AX.X, ALU.max)
                        dve.drain()
                        for r in range(R):
                            last = dve.tensor_scalar(logits[:, r, :], logits[:, r, :], top[:, r:r + 1], None,
                                                     ALU.subtract)
                        shifted.done(last)
                        gate_exp.wait(dve, s + 1)
                        dve.tensor_reduce(sums[:, :], probs[:, :, :], AX.X, ALU.add)
                        dve.drain()
                        dve.reciprocal(inv_sums[:, :], sums[:, :])
                        dve.drain()
                        for r in range(R):
                            dve.tensor_scalar(probs[:, r, :], probs[:, r, :], inv_sums[:, r:r + 1], None, ALU.mult)
                        dve.drain()
                        for r in range(R):
                            dve.max(best[:, r, :], probs[:, r, :])
                        dve.drain()
                        for r in range(R):
                            dve.max_index(best_at[:, r, :], best[:, r, :], probs[:, r, :])
                        dve.drain()
                        dve.tensor_copy(best_at_f[:, :, :], best_at[:, :, :])
                        dve.drain()
                        first = [probs, second]
                        for r in range(R):
                            for k in range(2):
                                dve.tensor_scalar(first[k][:, r, :], number[:, :], best_at_f[:, r, k:k + 1],
                                                  best[:, r, k:k + 1], ALU.is_equal, ALU.mult)
                        dve.drain()
                        routed.done(dve.tensor_tensor(weights[:, ds(R * s, R), :], probs[:, :, :], second[:, :, :],
                                                      ALU.add))

                    def body(s, half, more):
                        if more:
                            split_o(s + 1)
                            add(s + 1)
                        for n in range(NH // 2):
                            multiply(s, n)
                        if more:
                            split_n(s + 1, 1 - half)
                        for n in range(NH // 2, NH):
                            multiply(s, n)
                        route(s)

                    for st in (o_low, added, normal, low_n, hid, routed):
                        st.open(dve)
                    setup_in.wait(dve, 2)
                    const.wait(dve, E)
                    split_o(0)
                    add(0)
                    split_n(0, 0)
                    loops(dve, body)


def experts(nc, hT, x2, w_out, w2, weights, y):
    tiles = TOK // P
    OUTS = E + 1
    BANKS = 6
    parts = ("high", "low")
    x_t, y_t = tokens(x2), tokens(y)
    with ExitStack() as keep:
        sb, _, _ = allocator(keep, nc, "ex")
        wo = [sb(f"wo_{part}", [P, DC, D], F32R) for part in parts]
        wx = [sb(f"wx_{part}", [P, E, DC, D], F32R) for part in parts]
        chunk = [(w_out.rearrange("(c p) n -> p c n", p=P)[:, c, :], wo[0][:, c, :], wo[1][:, c, :]) for c in range(DC)]
        chunk += [(w2[e].rearrange("(c p) n -> p c n", p=P)[:, c, :], wx[0][:, e, c, :], wx[1][:, e, c, :])
                  for e in range(E) for c in range(DC)]
        split_plain(nc, "exw", chunk)
        with ExitStack() as ctx:
            sb, ps, step = allocator(ctx, nc, "exl")
            h_in = [sb(f"h_in{i}", [P, 2, DC, P]) for i in range(2)]
            h = [[sb(f"h_{part}{i}", [P, 2, DC, P], F32R) for part in parts] for i in range(2)]
            rows = [sb(f"rows{i}", [P, D]) for i in range(2)]
            banks = [ps(f"banks{i}", [P, D]) for i in range(BANKS)]
            h_loaded = [step(f"h_loaded{i}", size=16) for i in range(2)]
            x_loaded = [step(f"x_loaded{i}", size=16) for i in range(2)]
            high, low = step("high", ahead=2), step("low", ahead=2)
            made, summed = step("made", ahead=2 * OUTS), step("summed", ahead=max(BANKS, OUTS))
            stored = [step(f"stored{i}", size=16, ahead=1) for i in range(2)]

            def loops(eng, body):
                with eng.Fori(0, tiles // 2) as n:
                    for odd in range(2):
                        body(n, 2 * n + odd, odd)

            with nc.Block() as block:
                @block.sync
                def _(sp):
                    def load(n, t, odd):
                        low.wait(sp, t - 1)
                        h_loaded[odd].done(sp.dma_start(h_in[odd][:, :, :, :], one(hT, t)))
                        stored[odd].wait(sp, n)
                        x_loaded[odd].done(sp.dma_start(rows[odd][:, :], one(x_t, t)))

                    def body(n, t, odd, more=True):
                        if more:
                            load(n + odd, t + 1, 1 - odd)
                        summed.wait(sp, OUTS * (t + 1))
                        stored[odd].done(sp.dma_start(one(y_t, t), rows[odd][:, :]))

                    for st in stored:
                        st.open(sp)
                    load(0, 0, 0)
                    with sp.Fori(0, tiles // 2 - 1) as n:
                        for odd in range(2):
                            body(n, 2 * n + odd, odd)
                    body(tiles // 2 - 1, tiles - 2, 0)
                    body(tiles // 2 - 1, tiles - 1, 1, False)
                    for st in stored:
                        st.wait(sp, tiles // 2)

                @block.scalar
                def _(act):
                    def body(n, t, odd):
                        h_loaded[odd].wait(act, n + 1)
                        made.wait(act, OUTS * (t - 1))
                        high.done(act.activation(h[odd][0][:, :, :, :], h_in[odd][:, :, :, :], ACT.Copy))

                    high.open(act)
                    loops(act, body)

                @block.tensor
                def _(pe):
                    def body(n, t, odd):
                        low.wait(pe, t + 1)
                        for o in range(OUTS):
                            which = min(o, 1)
                            summed.wait(pe, OUTS * t + o - BANKS + 1)
                            out = banks[(OUTS * odd + o) % BANKS]
                            right = wo if o == 0 else [w[:, o - 1, :, :] for w in wx]
                            for c in range(DC):
                                last = matmul3(pe, out[:, :], [x[:, which, c, :] for x in h[odd]],
                                               [w[:, c, :] for w in right], c == 0, c == DC - 1)
                            made.done(last)

                    made.open(pe)
                    loops(pe, body)

                @block.vector
                def _(dve):
                    def split(n, t, odd):
                        high.wait(dve, t + 1)
                        low.done(dve.tensor_tensor(h[odd][1][:, :, :, :], h_in[odd][:, :, :, :],
                                                   words(h[odd][0][:, :, :, :]), ALU.subtract))

                    def body(n, t, odd):
                        split(n, t, odd)
                        x_loaded[odd].wait(dve, n + 1)
                        for o in range(OUTS):
                            made.wait(dve, OUTS * t + o + 1)
                            out = banks[(OUTS * odd + o) % BANKS]
                            if o == 0:
                                summed.done(dve.tensor_tensor(rows[odd][:, :], out[:, :], rows[odd][:, :], ALU.add))
                            else:
                                summed.wait(dve, OUTS * t + o)
                                summed.done(dve.scalar_tensor_tensor(
                                    rows[odd][:, :], out[:, :], weights[:, ds(t, 1), o - 1:o].squeeze(1), rows[odd][:, :],
                                    ALU.mult, ALU.add))

                    low.open(dve)
                    summed.open(dve)
                    loops(dve, body)


def decoder_layer(nc, x, context, mask, k, v, Wq, bq, Wk, bk, Wv, bv, Wo, bo, w_shared_in, w_shared_out, w1, w2,
                  w_gate, gate_bias, y):
    def dram(name, shape, dt=F32):
        return nc.dram_tensor(name, shape, dt).ap()

    x1, x2 = dram("x1", [TOK, D]), dram("x2", [TOK, D])
    kT = [dram(f"kT_{part}", [B, D, S2]) for part in ("high", "low")]
    qT = [dram(f"qT_{part}", [B, D, S]) for part in ("high", "low")]
    values = dram("values", [B, GROUPS, S2, P])
    row = dram("row", [H, P])
    oT = dram("oT", [B * GROUPS, P, S])
    hT = dram("hT", [TOK // P, P, 2, DC, P])
    by_group = "b (g p) n -> (b g) p n"
    with ExitStack() as ctx:
        def sb(name, shape, dt=F32):
            return ctx.enter_context(nc.sbuf_tensor(name, shape, dt))

        ident, ident_b = sb("ident", [P, P]), sb("ident_b", [P, P], BF16)
        make_identity(nc, ident, ident_b)
        self_attention(nc, ident, x, k, v, x1)
        context_keys_values(nc, ident, context, Wk, bk, Wv, bv, kT, values)
        with ExitStack() as masks:
            mask_q = masks.enter_context(nc.sbuf_tensor("mask_q", [P, QT, S2], BF16))
            mask_t = masks.enter_context(nc.sbuf_tensor("mask_t", [P, KT, S], BF16))
            with nc.sbuf_tensor("any_key", [P, S], F32) as any_key:
                prepare_mask(nc, ident_b, mask, mask_q, mask_t, any_key)
                project_queries(nc, ident, x1, Wq, bq, any_key, qT)
            cross_attention(nc, ident, ident_b, [a.rearrange(by_group, p=P) for a in kT],
                            [a.rearrange(by_group, p=P) for a in qT], values.rearrange("b g n p -> (b g) n p"),
                            mask_q, mask_t, row, oT)
        weights = sb("weights", [P, TOK // P, E])
        hidden_layers(nc, ident, oT, Wo, bo, x1, [w_shared_in, w1], w_gate, gate_bias, x2, hT, weights)
        experts(nc, hT, x2, w_shared_out, w2, weights, y)


INPUTS = ["x", "ctx_1024", "mask_1x1xSxS2_ik0", "L0_attn_k", "L0_attn_v", "L0_xattn_Wq_w", "L0_xattn_Wq_b",
          "L0_xattn_Wk_w", "L0_xattn_Wk_b", "L0_xattn_Wv_w", "L0_xattn_Wv_b", "L0_xattn_Wo_w", "L0_xattn_Wo_b",
          "L0_ffn_w_shared_in", "L0_ffn_w_shared_out", "L0_ffn_w1_shared", "L0_ffn_w2", "L0_ffn_w_gate",
          "L0_ffn_gate_bias"]


def kernel(**inputs):
    import concourse.bacc as bacc
    from concourse.bass_utils import run_bass_kernel_spmd

    nc = bacc.Bacc("TRN2", target_bir_lowering=False, num_devices=1)
    arrays, args = {}, []
    for name in INPUTS:
        a = np.ascontiguousarray(inputs[name])
        arrays[f"in_{name}"] = a
        args.append(nc.dram_tensor(f"in_{name}", a.shape, mybir.dt.from_np(a.dtype), kind="ExternalInput").ap())
    y = nc.dram_tensor("out_y", [TOK, D], F32, kind="ExternalOutput").ap()
    decoder_layer(nc, *args, y)
    result = run_bass_kernel_spmd(nc, [arrays], core_ids=[0])
    return result.results[0]["out_y"].reshape(B, S, D)
```

```python
import concourse.bass as bass
from concourse import mybir
from concourse.alu_op_type import AluOpType as ALU
from contextlib import ExitStack
import itertools
import numpy as np

F32 = mybir.dt.float32
F32R = mybir.dt.float32r
BF16 = mybir.dt.bfloat16
I32 = mybir.dt.int32
U32 = mybir.dt.uint32
ACT = mybir.ActivationFunctionType
AX = mybir.AxisListType
ds = bass.ds

P = 128
B, S, D = 4, 1024, 512
TOK = B * S
DC = D // P
T1 = 2048
T1C = T1 // P
S2 = 1601
H, DK = 16, 32
E = 8
BANK = 512
EPS = 1e-5
LOWEST = -3.0e38


class Step:

    def __init__(self, ctx, nc, name, ahead=None, size=1):
        self.sem = ctx.enter_context(nc.semaphore(name))
        self.ahead, self.size = 0 if ahead is None else ahead + 1, size

    def open(self, eng):
        eng.sem_inc(self.sem, self.ahead * self.size)

    def done(self, instruction):
        instruction.then_inc(self.sem, self.size)

    def wait(self, eng, n):
        eng.wait_ge(self.sem, (n + self.ahead) * self.size)


class Chain:

    def __init__(self, step, eng, base):
        self.step, self.eng, self.n = step, eng, base

    def __call__(self, instruction):
        self.step.done(instruction)
        self.n = self.n + 1
        self.step.wait(self.eng, self.n)


def words(ap):
    return ap.bitcast(F32)


def matmul3(pe, out, left, right, start, stop):
    (lh, ll), (rh, rl) = left, right
    pe.matmul(out, lh, rh, start=start, stop=False)
    pe.matmul(out, lh, rl, start=False, stop=False)
    return pe.matmul(out, ll, rh, start=False, stop=stop)


def allocator(ctx, nc, tag):
    def sb(name, shape, dt=F32):
        return ctx.enter_context(nc.sbuf_tensor(f"{tag}_{name}", shape, dt))

    def ps(name, shape, dt=F32):
        return ctx.enter_context(nc.psum_tensor(f"{tag}_{name}", shape, dt))

    def step(name, **more):
        return Step(ctx, nc, f"{tag}_{name}", **more)

    return sb, ps, step


def make_identity(nc, ident, ident_b):
    with ExitStack() as ctx:
        _, _, step = allocator(ctx, nc, "id")
        made = step("made")
        with nc.Block() as block:
            @block.gpsimd
            def _(pool):
                made.done(pool.memset(ident[:, :], 0.0))
                made.wait(pool, 1)
                made.done(pool.affine_select(out=ident[:, :], in_=ident[:, :], compare_op=ALU.not_equal,
                                             fill=1.0, base=0, pattern=[[-1, P]], channel_multiplier=1))
                made.wait(pool, 2)
                made.done(pool.tensor_copy(ident_b[:, :], ident[:, :]))


def split_transposed(nc, ident, tag, items):
    with ExitStack() as ctx:
        sb, ps, step = allocator(ctx, nc, tag)
        rows = sb("rows", [P, 8, D])
        banks = ps("banks", [P, 8, DC, P])
        loaded, turned, high_done, low_done = step("loaded", size=16), step("turned"), step("high"), step("low")
        with nc.Block() as block:
            @block.sync
            def _(sp):
                for n, (src, _, _) in enumerate(items):
                    turned.wait(sp, 8 * n)
                    loaded.done(sp.dma_start(rows[:, :, :], src))

            @block.tensor
            def _(pe):
                for n in range(len(items)):
                    loaded.wait(pe, n + 1)
                    for r in range(8):
                        if n:
                            low_done.wait(pe, 8 * (n - 1) + r + 1)
                        for dc in range(DC):
                            last = pe.transpose(banks[:, r, dc, :], rows[:, r, dc * P:(dc + 1) * P], ident[:, :])
                        turned.done(last)

            @block.scalar
            def _(act):
                for n, (_, high, low) in enumerate(items):
                    for r in range(8):
                        turned.wait(act, 8 * n + r + 1)
                        high_done.done(act.activation(high[:, :, r * P:(r + 1) * P], banks[:, r, :, :], ACT.Copy))

            @block.vector
            def _(dve):
                for n, (_, high, low) in enumerate(items):
                    for r in range(8):
                        high_done.wait(dve, 8 * n + r + 1)
                        low_done.done(dve.tensor_tensor(low[:, :, r * P:(r + 1) * P], banks[:, r, :, :],
                                                        words(high[:, :, r * P:(r + 1) * P]), ALU.subtract))


def tokens(ap):
    return ap.rearrange("(t p) n -> t p n", p=P)


def one(ap, i):
    return ap[ds(i, 1)].squeeze(0)


def self_attention(nc, ident, x, k, v, x1):
    NB = T1 // BANK
    KB = BANK // P
    tiles = TOK // P
    with ExitStack() as keep:
        sb, _, _ = allocator(keep, nc, "sa")
        kT = [sb(f"kT_{part}", [P, DC, T1], F32R) for part in ("high", "low")]
        vs = [sb(f"v_{part}", [P, T1C, D], F32R) for part in ("high", "low")]
        scale = sb("scale", [P, B, NB, D])
        k_rows = k[0].rearrange("(n r p) d -> n p r d", p=P, r=8)
        split_transposed(nc, ident, "sak",
                         [(k_rows[n], *(t[:, :, n * 8 * P:(n + 1) * 8 * P] for t in kT)) for n in range(2)])
        self_attention_setup(nc, x, v, vs, scale)
        self_attention_loop(nc, ident, x, x1, kT, vs, scale, NB, KB, tiles)


def self_attention_setup(nc, x, v, vs, scale):
    G = B * 4
    rows_of_scale = x.rearrange("b (j r) n -> (b j) r n", j=4)[:, 0, :]
    v_rows = v[0].rearrange("(n r p) d -> n p r d", p=P, r=T1C // 2)
    with ExitStack() as ctx:
        sb, _, step = allocator(ctx, nc, "sas")
        v_in = sb("v_in", [P, T1C // 2, D])
        stats = sb("stats", [P, G, 6])
        mean_var = sb("mean_var", [P, G, 2])
        var, rstd, power = sb("var", [P, G]), sb("rstd", [P, G]), sb("power", [P, G])
        v_loaded, v_high, v_low, s_loaded = step("v_loaded", size=16), step("v_high"), step("v_low"), step("s_loaded", size=16)
        chain, pow_set, root = step("chain"), step("pow_set"), step("root")
        groups = scale[:, :, :, :].rearrange("p b j d -> p (b j) d")
        with nc.Block() as block:
            @block.sync
            def _(sp):
                s_loaded.done(sp.dma_start(groups, rows_of_scale.partition_broadcast(P)))
                for n in range(2):
                    v_low.wait(sp, n)
                    v_loaded.done(sp.dma_start(v_in[:, :, :], v_rows[n]))

            @block.scalar
            def _(act):
                for n in range(2):
                    v_loaded.wait(act, n + 1)
                    v_high.done(act.activation(vs[0][:, n * 8:(n + 1) * 8, :], v_in[:, :, :], ACT.Copy))

            @block.gpsimd
            def _(pool):
                pow_set.done(pool.memset(power[:, :], -0.5))
                pow_set.wait(pool, 1)
                chain.wait(pool, 2 * G + 1)
                root.done(pool.tensor_tensor(rstd[:, :], var[:, :], power[:, :], ALU.pow))

            @block.vector
            def _(dve):
                s_loaded.wait(dve, 1)
                for g in range(G):
                    chain.done(dve.bn_stats(stats[:, g, :], groups[:, g, :]))
                chain.wait(dve, G)
                for g in range(G):
                    chain.done(dve.bn_aggr(mean_var[:, g, :], stats[:, g, :]))
                chain.wait(dve, 2 * G)
                chain.done(dve.tensor_scalar_add(var[:, :], mean_var[:, :, 1], EPS))
                root.wait(dve, 1)
                for g in range(G):
                    chain.done(dve.tensor_scalar(groups[:, g, :], groups[:, g, :], mean_var[:, g, 0:1],
                                                 rstd[:, g:g + 1], ALU.subtract, ALU.mult))
                for n in range(2):
                    v_high.wait(dve, n + 1)
                    v_low.done(dve.tensor_tensor(vs[1][:, n * 8:(n + 1) * 8, :], v_in[:, :, :],
                                                 words(vs[0][:, n * 8:(n + 1) * 8, :]), ALU.subtract))


def self_attention_loop(nc, ident, x, x1, kT, vs, scale, NB, KB, tiles):
    x_t, x1_t = tokens(x.rearrange("b s n -> (b s) n")), tokens(x1)
    with ExitStack() as ctx:
        sb, ps, step = allocator(ctx, nc, "sal")
        x_norm, x_add = sb("x_norm", [P, D]), sb("x_add", [P, D])
        normed = sb("normed", [P, D])
        nT = [sb(f"nT_{part}", [P, DC, P], F32R) for part in ("high", "low")]
        scaled, prob = sb("scaled", [P, NB, BANK]), sb("prob", [P, NB, BANK])
        pT = [sb(f"pT_{part}", [P, T1C, P], F32R) for part in ("high", "low")]
        out = sb("out", [P, D])
        stats, mean_var, var, rstd, power = sb("stats", [P, 6]), sb("mean_var", [P, 2]), sb("var", [P, 1]), sb("rstd", [P, 1]), sb("power", [P, 1])
        neg_max, total, inv_total = sb("neg_max", [P, 1]), sb("total", [P, 1]), sb("inv_total", [P, 1])
        scores = ps("scores", [P, NB, BANK])
        nT_ps = ps("nT_ps", [P, DC, P])
        pT_ps = [ps(f"pT_ps{i}", [P, KB, P]) for i in range(2)]
        o_ps = ps("o_ps", [P, D])

        norm_in = step("norm_in", size=16)
        add_in = step("add_in", size=16)
        stored = step("stored", size=16, ahead=1)
        constant = step("constant")
        stat = step("stat")
        root = step("root", ahead=1)
        normal = step("normal", ahead=1)
        turned = step("turned", ahead=1)
        nT_high, nT_low = step("nT_high"), step("nT_low")
        scored = step("scored")
        scaled_to = step("scaled_to", ahead=NB)
        peak = step("peak", ahead=1)
        exped = step("exped", ahead=1)
        p_turned = step("p_turned", ahead=NB)
        pT_high, pT_low = step("pT_high"), step("pT_low", ahead=2)
        weighed = step("weighed", ahead=1)
        inverse = step("inverse")
        summed = step("summed", ahead=1)

        with nc.Block() as block:
            @block.sync
            def _(sp):
                def load_norm(t):
                    normal.wait(sp, t)
                    norm_in.done(sp.dma_start(x_norm[:, :], one(x_t, t)))

                def load_add(t):
                    summed.wait(sp, t)
                    add_in.done(sp.dma_start(x_add[:, :], one(x_t, t)))

                def store(t):
                    summed.wait(sp, t + 1)
                    stored.done(sp.dma_start(one(x1_t, t), out[:, :]))

                stored.open(sp)
                load_norm(0)
                load_norm(1)
                with sp.Fori(0, tiles - 2) as t:
                    load_norm(t + 2)
                    load_add(t)
                    store(t)
                for t in (tiles - 2, tiles - 1):
                    load_add(t)
                    store(t)
                stored.wait(sp, tiles)

            @block.gpsimd
            def _(pool):
                root.open(pool)
                constant.done(pool.memset(power[:, :], -0.5))
                constant.wait(pool, 1)
                with pool.Fori(0, tiles) as t:
                    stat.wait(pool, t + 1)
                    root.done(pool.tensor_tensor(rstd[:, :], var[:, :], power[:, :], ALU.pow))

            @block.tensor
            def _(pe):
                def turn(t):
                    normal.wait(pe, t + 1)
                    nT_low.wait(pe, t)
                    for dc in range(DC):
                        last = pe.transpose(nT_ps[:, dc, :], normed[:, dc * P:(dc + 1) * P], ident[:, :])
                    turned.done(last)

                def score(t, j):
                    if j == 0:
                        nT_low.wait(pe, t + 1)
                    scaled_to.wait(pe, NB * (t - 1) + j + 1)
                    for dc in range(DC):
                        last = matmul3(pe, scores[:, j, :], [n[:, dc, :] for n in nT],
                                       [kt[:, dc, j * BANK:(j + 1) * BANK] for kt in kT], dc == 0, dc == DC - 1)
                    scored.done(last)

                def turn_p(t, j):
                    if j == 0:
                        exped.wait(pe, t + 1)
                    pT_low.wait(pe, NB * t + j - 1)
                    for n in range(KB):
                        last = pe.transpose(pT_ps[j % 2][:, n, :], prob[:, j, n * P:(n + 1) * P], ident[:, :])
                    p_turned.done(last)

                def weigh(t, j):
                    if j == 0:
                        summed.wait(pe, t)
                    pT_low.wait(pe, NB * t + j + 1)
                    for n in range(j * KB, (j + 1) * KB):
                        last = matmul3(pe, o_ps[:, :], [p[:, n, :] for p in pT], [w[:, n, :] for w in vs],
                                       n == 0, n == T1C - 1)
                    if j == NB - 1:
                        weighed.done(last)

                def tile(t, ahead):
                    if ahead >= 1:
                        for j in range(NB - 1):
                            score(t + 1, j)
                    turn_p(t, 0)
                    turn_p(t, 1)
                    if ahead >= 1:
                        score(t + 1, NB - 1)
                    if ahead >= 2:
                        turn(t + 2)
                    for j in range(NB):
                        weigh(t, j)
                        if j + 2 < NB:
                            turn_p(t, j + 2)

                turned.open(pe)
                p_turned.open(pe)
                weighed.open(pe)
                turn(0)
                for j in range(NB):
                    score(0, j)
                turn(1)
                with pe.Fori(0, tiles - 2) as t:
                    tile(t, 2)
                tile(tiles - 2, 1)
                tile(tiles - 1, 0)

            @block.scalar
            def _(act):
                def high_n(t):
                    turned.wait(act, t + 1)
                    nT_high.done(act.activation(nT[0][:, :, :], nT_ps[:, :, :], ACT.Copy))

                def exp(t):
                    p_turned.wait(act, NB * t)
                    peak.wait(act, t + 1)
                    exped.done(act.activation(prob[:, :, :], scaled[:, :, :], ACT.Exp, bias=neg_max[:, 0:1],
                                              accum_out=total[:, 0:1]))

                def high_p(t, j):
                    if j == 0:
                        weighed.wait(act, t)
                    p_turned.wait(act, NB * t + j + 1)
                    pT_high.done(act.activation(pT[0][:, j * KB:(j + 1) * KB, :], pT_ps[j % 2][:, :, :], ACT.Copy))

                def tile(t, ahead):
                    high_p(t, 0)
                    high_p(t, 1)
                    if ahead >= 2:
                        high_n(t + 2)
                    high_p(t, 2)
                    high_p(t, 3)
                    if ahead >= 1:
                        exp(t + 1)

                exped.open(act)
                high_n(0)
                high_n(1)
                exp(0)
                with act.Fori(0, tiles - 2) as t:
                    tile(t, 2)
                tile(tiles - 2, 1)
                tile(tiles - 1, 0)

            @block.vector
            def _(dve):
                def normalize(t):
                    norm_in.wait(dve, t + 1)
                    root.wait(dve, t)
                    dve.bn_stats(stats[:, :], x_norm[:, :])
                    dve.drain()
                    dve.bn_aggr(mean_var[:, :], stats[:, :])
                    dve.drain()
                    stat.done(dve.tensor_scalar_add(var[:, :], mean_var[:, 1:2], EPS))
                    turned.wait(dve, t)
                    root.wait(dve, t + 1)
                    normal.done(dve.tensor_scalar(normed[:, :], x_norm[:, :], mean_var[:, 0:1], rstd[:, 0:1],
                                                  ALU.subtract, ALU.mult))

                def low_n(t):
                    nT_high.wait(dve, t + 1)
                    nT_low.done(dve.tensor_tensor(nT[1][:, :, :], nT_ps[:, :, :], words(nT[0][:, :, :]), ALU.subtract))

                def scale_block(t, j):
                    if j == 0:
                        exped.wait(dve, t)
                    scored.wait(dve, NB * t + j + 1)
                    batch = scale[:, ds(t // (S // P), 1), j, :].squeeze(1)
                    scaled_to.done(dve.tensor_tensor(scaled[:, j, :], scores[:, j, :], batch, ALU.mult))

                def row_max(t):
                    scaled_to.wait(dve, NB * (t + 1))
                    peak.done(dve.tensor_reduce(neg_max[:, 0:1], scaled[:, :, :], AX.XY, ALU.max, negate=True))

                def low_p(t, j):
                    pT_high.wait(dve, NB * t + j + 1)
                    pT_low.done(dve.tensor_tensor(pT[1][:, j * KB:(j + 1) * KB, :], pT_ps[j % 2][:, :, :],
                                                  words(pT[0][:, j * KB:(j + 1) * KB, :]), ALU.subtract))

                def invert(t):
                    summed.wait(dve, t)
                    exped.wait(dve, t + 1)
                    inverse.done(dve.reciprocal(inv_total[:, :], total[:, :]))

                def add(t):
                    weighed.wait(dve, t + 1)
                    inverse.wait(dve, t + 1)
                    add_in.wait(dve, t + 1)
                    stored.wait(dve, t)
                    summed.done(dve.scalar_tensor_tensor(out[:, :], o_ps[:, :], inv_total[:, 0:1], x_add[:, :],
                                                         ALU.mult, ALU.add))

                def tile(t, ahead):
                    invert(t)
                    if ahead >= 2:
                        normalize(t + 2)
                    if ahead >= 1:
                        for j in range(NB - 1):
                            scale_block(t + 1, j)
                    low_p(t, 0)
                    low_p(t, 1)
                    if ahead >= 1:
                        scale_block(t + 1, NB - 1)
                        row_max(t + 1)
                    if ahead >= 2:
                        low_n(t + 2)
                    low_p(t, 2)
                    low_p(t, 3)
                    add(t)

                for s in (normal, scaled_to, peak, pT_low, summed):
                    s.open(dve)
                normalize(0)
                low_n(0)
                normalize(1)
                for j in range(NB):
                    scale_block(0, j)
                row_max(0)
                low_n(1)
                with dve.Fori(0, tiles - 2) as t:
                    tile(t, 2)
                tile(tiles - 2, 1)
                tile(tiles - 1, 0)


BLOCKS = 4
ROWS = 100
KEYS = [4 * ROWS] * 3 + [4 * ROWS + 1]
assert sum(KEYS) == S2


MASKED = -1e9
QT = S // P
KT = (S2 + P - 1) // P
LAST = S2 - (KT - 1) * P


class MaskPreparation:

    ROUNDS = [(0, 8), (8, KT)]

    def __init__(self, sb, ps, step, ident_b, mask, mask_q, mask_t, any_key):
        self.rows = mask[0, 0].rearrange("(t p) n -> t p n", p=P)
        self.ident_b, self.mask_q, self.mask_t, self.any_key = ident_b, mask_q, mask_t, any_key
        self.raw, self.zero, self.tile = sb("mk_raw", [P, S2], I32), sb("mk_zero", [P, S2], BF16), sb("mk_tile", [P, S2], BF16)
        self.none, self.some, self.weight = sb("mk_none", [P, 1]), sb("mk_some", [P, 1]), sb("mk_weight", [P, 1])
        self.some_b = sb("mk_some_b", [P, P], BF16)
        self.turned_ps, self.some_ps = ps("mk_turned_ps", [P, 8, P], BF16), ps("mk_some_ps", [P, BANK])
        self.raw_in, self.zeroed = step("mk_raw_in", size=16), step("mk_zeroed", ahead=1)
        self.weighted, self.turned = step("mk_weighted"), step("mk_turned", ahead=2)
        self.copied, self.kept = step("mk_copied", ahead=2), step("mk_kept", ahead=1)

    def load(self, sp, t):
        source = one(self.rows, t)
        self.zeroed.wait(sp, t)
        self.raw_in.done(sp.dma_start(self.raw[:, :], source))

    def vector(self, dve, t):
        self.raw_in.wait(dve, t + 1)
        self.zeroed.done(dve.tensor_scalar(self.zero[:, :], self.raw[:, :], 0.0, None, ALU.is_equal))
        self.zeroed.wait(dve, t + 1)
        dve.tensor_reduce(self.none[:, :], self.zero[:, :], AX.X, ALU.min)
        dve.drain()
        dve.tensor_scalar(self.some[:, :], self.none[:, :], -1.0, 1.0, ALU.mult, ALU.add)
        dve.tensor_scalar(self.weight[:, :], self.none[:, :], -MASKED, MASKED, ALU.mult, ALU.add)
        dve.drain()
        self.turned.wait(dve, 2 * t)
        dve.tensor_copy(self.some_b[:, :], self.some[:, :].broadcast_to([P, P]))
        dve.drain()
        self.kept.wait(dve, t)
        self.weighted.done(dve.tensor_scalar(self.tile[:, :], self.zero[:, :], self.weight[:, 0:1], None, ALU.mult))

    def transposes(self, pe, t, part):
        self.weighted.wait(pe, t + 1)
        self.copied.wait(pe, 2 * t + part)
        if part == 0:
            pe.matmul(self.some_ps[:, 0:P], self.some_b[:, :], self.ident_b[:, :], start=True, stop=True)
        first, end = self.ROUNDS[part]
        for n in range(first, end):
            keys = min(P, S2 - n * P)
            last = pe.transpose(self.turned_ps[0:keys, n - first, :], self.tile[:, n * P:n * P + keys], self.ident_b[:, :])
        self.turned.done(last)

    def copies(self, act, t, part):
        self.turned.wait(act, 2 * t + part + 1)
        here = ds(t * P, P)
        first, end = self.ROUNDS[part]
        whole = min(end, KT - 1)
        if part == 0:
            act.activation(self.any_key[:, here], self.some_ps[:, 0:P], ACT.Copy)
            self.kept.done(act.activation(self.mask_q[:, ds(t, 1), :].squeeze(1), self.tile[:, :], ACT.Copy))
        else:
            act.activation(self.mask_t[0:LAST, KT - 1, here], self.turned_ps[0:LAST, KT - 1 - first, :], ACT.Copy)
        act.drain()
        self.copied.done(act.activation(self.mask_t[:, first:whole, here], self.turned_ps[:, 0:whole - first, :], ACT.Copy))


def split_weights(nc, ident, tag, weights, outs):
    with ExitStack() as ctx:
        sb, ps, step = allocator(ctx, nc, tag)
        rows = sb("rows", [P, len(weights), DC, D])
        banks = ps("banks", [P, len(weights) * DC, DC, P])
        loaded, turned, high_done, low_done = step("loaded", size=16), step("turned"), step("high"), step("low")
        cases = [(w, r) for w in range(len(weights)) for r in range(DC)]
        with nc.Block() as block:
            @block.sync
            def _(sp):
                for w, weight in enumerate(weights):
                    loaded.done(sp.dma_start(rows[:, w, :, :], weight.rearrange("(r p) n -> p r n", p=P)))

            @block.tensor
            def _(pe):
                loaded.wait(pe, len(weights))
                for n, (w, r) in enumerate(cases):
                    for dc in range(DC):
                        last = pe.transpose(banks[:, n, dc, :], rows[:, w, r, dc * P:(dc + 1) * P], ident[:, :])
                    turned.done(last)

            @block.scalar
            def _(act):
                for n, (w, r) in enumerate(cases):
                    turned.wait(act, n + 1)
                    high_done.done(act.activation(outs[w][0][:, :, r * P:(r + 1) * P], banks[:, n, :, :], ACT.Copy))

            @block.vector
            def _(dve):
                for n, (w, r) in enumerate(cases):
                    high_done.wait(dve, n + 1)
                    low_done.done(dve.tensor_tensor(outs[w][1][:, :, r * P:(r + 1) * P], banks[:, n, :, :],
                                                    words(outs[w][0][:, :, r * P:(r + 1) * P]), ALU.subtract))


def context_keys_values(nc, ident, ident_b, context, Wk, bk, Wv, bv, mask, masks, kT_out, v_out):
    steps = B * BLOCKS
    with ExitStack() as keep:
        sb, _, _ = allocator(keep, nc, "cx")
        wk = [sb(f"wk_{part}", [P, DC, D], F32R) for part in ("high", "low")]
        wv = [sb(f"wv_{part}", [P, DC, D], F32R) for part in ("high", "low")]
        split_weights(nc, ident, "cxw", [Wk, Wv], [wk, wv])
        with ExitStack() as ctx:
            sb, ps, step = allocator(ctx, nc, "cxl")
            k_bias, v_bias = sb("k_bias", [P, DC]), sb("v_bias", [P, D])
            rows = sb("rows", [P, 2, 4, D])
            WIDE = max(KEYS) + 1
            cT = [[sb(f"cT_{part}{i}", [P, DC, WIDE], F32R) for part in ("high", "low")] for i in range(2)]
            kT = [sb(f"kT_{part}", [P, DC, max(KEYS)], F32R) for part in ("high", "low")]
            v_sb = sb("v", [P, 4, D])
            banks = ps("banks", [P, 2, BANK])
            outs = ps("outs", [P, 4, BANK])

            bias_in = step("bias_in", size=16)
            rows_in = [step(f"rows_in{i}", size=16) for i in range(2)]
            turned = step("turned", ahead=8)
            cT_high, cT_low = step("cT_high"), step("cT_low", ahead=2)
            k_made, k_high, k_low = step("k_made", ahead=4), step("k_high"), step("k_low")
            v_made, v_done = step("v_made", ahead=4), step("v_done", ahead=4)
            k_stored, v_stored = step("k_stored", size=16, ahead=2), step("v_stored", size=16, ahead=2)

            padded, carried = step("padded"), step("carried")
            preparation = MaskPreparation(sb, ps, step, ident_b, mask, *masks)

            def even(q):
                return KEYS[q] + KEYS[q] % 2

            def size(q, r):
                return ROWS + (q == BLOCKS - 1 and r == 3)

            def span(q):
                return slice(q * 4 * ROWS, q * 4 * ROWS + KEYS[q])

            def row_parts(dram, b, q, tile):
                first = q * 4 * ROWS
                yield (one(dram, b)[first:first + 4 * ROWS, :].rearrange("(r p) n -> p r n", p=ROWS), tile[0:ROWS, :, :])
                if q == BLOCKS - 1:
                    yield one(dram, b)[S2 - 1:S2, :], tile[ROWS:ROWS + 1, 3, :]

            def group_parts(b, q):
                first = q * 4 * ROWS
                for r in range(4):
                    yield (one(v_out, b)[:, first + r * ROWS:first + r * ROWS + size(q, r), :].rearrange("g p n -> p g n"),
                           v_sb[0:size(q, r), r, :].rearrange("p (g n) -> p g n", n=P))

            def loops(eng, body):
                def batch(b, last):
                    for q in range(BLOCKS):
                        def following(n):
                            return (b, q + n) if q + n < BLOCKS else None if last else (b + 1, q + n - BLOCKS)

                        body(b, q, following)

                with eng.Fori(0, B - 1) as b:
                    batch(b, False)
                batch(B - 1, True)

            with nc.Block() as block:
                @block.sync
                def _(sp):
                    bias_in.done(sp.dma_start(k_bias[:, :], bk.rearrange("(c p) -> p c", p=P),
                                              allow_slow_non_contiguous=True))
                    bias_in.done(sp.dma_start(v_bias[:, :], bv.partition_broadcast(P)))

                    def load(b, q):
                        parts = list(row_parts(context, b, q, rows[:, q % 2, :, :]))
                        turned.wait(sp, 4 * (BLOCKS * b + q - 1))
                        for src, dst in parts:
                            rows_in[q % 2].done(sp.dma_start(dst, src))

                    def store(b, q):
                        s = BLOCKS * b + q
                        places = [one(out, b)[:, span(q)].rearrange("(c p) n -> p c n", p=P) for out in kT_out]
                        parts = list(group_parts(b, q))
                        k_low.wait(sp, 4 * (s + 1))
                        sp.sem_inc(carried.sem, 1)
                        for part, dst in enumerate(places):
                            k_stored.done(sp.dma_start(dst, words(kT[part][:, :, 0:KEYS[q]])))
                        v_done.wait(sp, 4 * (s + 1))
                        for dst, src in parts:
                            v_stored.done(sp.dma_start(dst, src))

                    k_stored.open(sp)
                    v_stored.open(sp)
                    load(0, 0)
                    load(0, 1)

                    def body(b, q, following):
                        if following(2):
                            load(*following(2))
                        if q % 2 == 0:
                            preparation.load(sp, 2 * b + q // 2)
                        store(b, q)

                    loops(sp, body)
                    k_stored.wait(sp, 2 * steps)
                    v_stored.wait(sp, 4 * steps)

                def rows_arrived(b, q):
                    return (2 + q % 2) * b + q // 2 + 1 + (q == BLOCKS - 1)

                @block.gpsimd
                def _(pool):
                    for n, part in enumerate(cT[(BLOCKS - 1) % 2]):
                        padded.done(pool.memset(words(part[:, :, WIDE - 1:WIDE]), 0.0))
                        padded.wait(pool, n + 1)

                @block.tensor
                def _(pe):
                    def turn(b, q, r):
                        if r == 0:
                            rows_in[q % 2].wait(pe, rows_arrived(b, q))
                        cT_low.wait(pe, 4 * (BLOCKS * b + q) + r - 1)
                        n = size(q, r)
                        for dc in range(DC):
                            last = pe.transpose(banks[:, r % 2, dc * n:(dc + 1) * n],
                                                rows[0:n, q % 2, r, dc * P:(dc + 1) * P], ident[0:n, 0:n])
                        turned.done(last)

                    def keys(b, q, following):
                        s = BLOCKS * b + q
                        for hd in range(DC):
                            if following:
                                turn(*following, hd)
                            v_done.wait(pe, 4 * (s - 1) + hd + 1)
                            for dc in range(DC):
                                last = matmul3(pe, outs[:, hd, 0:even(q)], [w[:, dc, hd * P:(hd + 1) * P] for w in wk],
                                               [c[:, dc, 0:even(q)] for c in cT[q % 2]], dc == 0, dc == DC - 1)
                            k_made.done(last)

                    def values(b, q):
                        s = BLOCKS * b + q
                        for r in range(4):
                            n, first = size(q, r), r * ROWS
                            k_low.wait(pe, 4 * s + r + 1)
                            for dc in range(DC):
                                last = matmul3(pe, outs[0:n, r, :], [c[:, dc, first:first + n] for c in cT[q % 2]],
                                               [w[:, dc, :] for w in wv], dc == 0, dc == DC - 1)
                            v_made.done(last)

                    padded.wait(pe, 2)
                    turned.open(pe)
                    k_made.open(pe)
                    v_made.open(pe)
                    preparation.turned.open(pe)
                    for r in range(4):
                        turn(0, 0, r)

                    def body(b, q, following):
                        cT_low.wait(pe, 4 * (BLOCKS * b + q + 1))
                        keys(b, q, following(1))
                        if q % 2 == 1:
                            preparation.transposes(pe, 2 * b + q // 2, 0)
                        values(b, q)
                        if q % 2 == 1:
                            preparation.transposes(pe, 2 * b + q // 2, 1)

                    loops(pe, body)

                @block.scalar
                def _(act):
                    def high_c(b, q, r):
                        s = BLOCKS * b + q
                        v_made.wait(act, 4 * (s - 1))
                        n, first = size(q, r), r * ROWS
                        turned.wait(act, 4 * s + r + 1)
                        cT_high.done(act.activation(
                            cT[q % 2][0][:, :, first:first + n],
                            banks[:, r % 2, 0:DC * n].rearrange("p (c n) -> p c n", c=DC), ACT.Copy))

                    def high_k(b, q, following):
                        s = BLOCKS * b + q
                        for hd in range(DC):
                            if following:
                                high_c(*following, hd)
                            k_stored.wait(act, 2 * s)
                            k_made.wait(act, 4 * s + hd + 1)
                            k_high.done(act.activation(kT[0][:, hd, 0:KEYS[q]], outs[:, hd, 0:KEYS[q]], ACT.Identity,
                                                       bias=k_bias[:, hd:hd + 1]))

                    bias_in.wait(act, 2)
                    preparation.copied.open(act)
                    preparation.kept.open(act)
                    for r in range(4):
                        high_c(0, 0, r)

                    def body(b, q, following):
                        high_k(b, q, following(1))
                        if q % 2 == 1:
                            for part in range(2):
                                preparation.copies(act, 2 * b + q // 2, part)

                    loops(act, body)

                @block.vector
                def _(dve):
                    def low_c(b, q, r):
                        s = BLOCKS * b + q
                        n, first = size(q, r), r * ROWS
                        cT_high.wait(dve, 4 * s + r + 1)
                        cT_low.done(dve.tensor_tensor(
                            cT[q % 2][1][:, :, first:first + n],
                            banks[:, r % 2, 0:DC * n].rearrange("p (c n) -> p c n", c=DC),
                            words(cT[q % 2][0][:, :, first:first + n]), ALU.subtract))

                    def low_k(b, q, following):
                        s = BLOCKS * b + q
                        for hd in range(DC):
                            if following:
                                low_c(*following, hd)
                            k_high.wait(dve, 4 * s + hd + 1)
                            k_low.done(dve.scalar_tensor_tensor(
                                kT[1][:, hd, 0:KEYS[q]], outs[:, hd, 0:KEYS[q]], k_bias[:, hd:hd + 1],
                                words(kT[0][:, hd, 0:KEYS[q]]), ALU.add, ALU.subtract))

                    def finish_v(b, q):
                        s = BLOCKS * b + q
                        v_stored.wait(dve, 4 * s)
                        for r in range(4):
                            n = size(q, r)
                            v_made.wait(dve, 4 * s + r + 1)
                            v_done.done(dve.tensor_tensor(v_sb[0:n, r, :], outs[0:n, r, :], v_bias[0:n, :], ALU.add))

                    bias_in.wait(dve, 2)
                    cT_low.open(dve)
                    v_done.open(dve)
                    preparation.zeroed.open(dve)
                    for r in range(4):
                        low_c(0, 0, r)

                    def body(b, q, following):
                        low_k(b, q, following(1))
                        finish_v(b, q)
                        if q % 2 == 0:
                            preparation.vector(dve, 2 * b + q // 2)

                    loops(dve, body)


class LayerNorm:

    def __init__(self, sb, step, R):
        self.R = R
        self.stats, self.mean_var = sb("ln_stats", [P, R, 6]), sb("ln_mean_var", [P, R, 2])
        self.var, self.rstd, self.power = sb("ln_var", [P, R]), sb("ln_rstd", [P, R]), sb("ln_power", [P, R])
        self.constant, self.stat, self.root = step("ln_constant"), step("ln_stat"), step("ln_root", ahead=1)

    def pool_setup(self, pool):
        self.root.open(pool)
        self.constant.done(pool.memset(self.power[:, :], -0.5))
        self.constant.wait(pool, 1)

    def pool_step(self, pool, s):
        self.stat.wait(pool, s + 1)
        self.root.done(pool.tensor_tensor(self.rstd[:, :], self.var[:, :], self.power[:, :], ALU.pow))

    def statistics(self, dve, rows, s):
        self.root.wait(dve, s)
        for r in range(self.R):
            dve.bn_stats(self.stats[:, r, :], rows[:, r, :])
        dve.drain()
        for r in range(self.R):
            dve.bn_aggr(self.mean_var[:, r, :], self.stats[:, r, :])
        dve.drain()
        self.stat.done(dve.tensor_scalar_add(self.var[:, :], self.mean_var[:, :, 1], EPS))

    def normalize(self, dve, out, rows, s):
        self.root.wait(dve, s + 1)
        for r in range(self.R):
            last = dve.tensor_scalar(out[:, r, :], rows[:, r, :], self.mean_var[:, r, 0:1], self.rstd[:, r:r + 1],
                                     ALU.subtract, ALU.mult)
        return last


def project_queries(nc, ident, x1, Wq, bq, any_key, qT_out):
    steps = TOK // BANK
    R = BANK // P
    x_rows = x1.rearrange("(s r p) n -> s p r n", p=P, r=R)
    with ExitStack() as keep:
        sb, _, _ = allocator(keep, nc, "pq")
        wq = [sb(f"wq_{part}", [P, DC, D], F32R) for part in ("high", "low")]
        split_weights(nc, ident, "pqw", [Wq], [wq])
        with ExitStack() as ctx:
            sb, ps, step = allocator(ctx, nc, "pql")
            q_bias = sb("q_bias", [P, DC])
            rows = [sb(f"rows{i}", [P, R, D]) for i in range(2)]
            normed = sb("normed", [P, R, D])
            norm = LayerNorm(sb, step, R)
            nT = [[sb(f"nT_{part}{i}", [P, DC, BANK], F32R) for part in ("high", "low")] for i in range(2)]
            q = sb("q", [P, DC, BANK])
            qT = [[sb(f"qT_{part}{i}", [P, DC, BANK], F32R) for part in ("high", "low")] for i in range(2)]
            banks, outs = ps("banks", [P, R, DC, P]), ps("outs", [P, DC, BANK])
            bias_in, rows_in = step("bias_in", size=16), [step(f"rows_in{half}", size=16) for half in range(2)]
            normal = step("normal", ahead=2)
            turned = step("turned", ahead=R)
            high_n, low_n = step("high_n"), step("low_n", ahead=R)
            made = step("made", ahead=2 * DC)
            q_done = step("q_done", ahead=DC)
            high_q, low_q, carried = step("high_q"), step("low_q", ahead=DC), step("carried")
            stored = [step(f"stored{half}", size=16, ahead=2) for half in range(2)]

            def loops(eng, body):
                with eng.Fori(0, B - 1) as b:
                    for half in range(2):
                        body(b, half, 2)
                for half in range(2):
                    body(B - 1, half, 1 - half)

            with nc.Block() as block:
                @block.sync
                def _(sp):
                    bias_in.done(sp.dma_start(q_bias[:, :], bq.rearrange("(c p) -> p c", p=P),
                                              allow_slow_non_contiguous=True))

                    def load(s, half):
                        source = one(x_rows, s)
                        normal.wait(sp, s - 1)
                        rows_in[half].done(sp.dma_start(rows[half][:, :, :], source))

                    def body(b, half, more):
                        if more:
                            load(2 * b + half + 3, 1 - half)
                        places = [one(out, b).rearrange("(c p) n -> p c n", p=P)[:, :, half * BANK:(half + 1) * BANK]
                                  for out in qT_out]
                        low_q.wait(sp, DC * (2 * b + half + 1))
                        sp.sem_inc(carried.sem, 1)
                        for part, dst in enumerate(places):
                            stored[half].done(sp.dma_start(dst, words(qT[half][part][:, :, :])))

                    for st in stored:
                        st.open(sp)
                    load(0, 0)
                    load(1, 1)
                    load(2, 0)
                    with sp.Fori(0, B - 2) as b:
                        for half in range(2):
                            body(b, half, True)
                    for s in range(steps - 4, steps):
                        body(s // 2, s % 2, s + 3 < steps)
                    for st in stored:
                        st.wait(sp, 2 * B)

                @block.gpsimd
                def _(pool):
                    norm.pool_setup(pool)
                    with pool.Fori(0, steps) as s:
                        norm.pool_step(pool, s)

                @block.tensor
                def _(pe):
                    def turn(s, r):
                        normal.wait(pe, s + 1)
                        low_n.wait(pe, R * (s - 1) + r + 1)
                        for dc in range(DC):
                            last = pe.transpose(banks[:, r, dc, :], normed[:, r, dc * P:(dc + 1) * P], ident[:, :])
                        turned.done(last)

                    def body(b, half, more):
                        s = 2 * b + half
                        low_n.wait(pe, R * (s + 1))
                        for hd in range(DC):
                            if more:
                                turn(s + 1, hd)
                            q_done.wait(pe, DC * (s - 1) + hd + 1)
                            for dc in range(DC):
                                last = matmul3(pe, outs[:, hd, :], [w[:, dc, hd * P:(hd + 1) * P] for w in wq],
                                               [n[:, dc, :] for n in nT[half]], dc == 0, dc == DC - 1)
                            made.done(last)

                    turned.open(pe)
                    made.open(pe)
                    for r in range(R):
                        turn(0, r)
                    loops(pe, body)

                @block.scalar
                def _(act):
                    def high(s, half, r):
                        made.wait(act, DC * (s - 1))
                        turned.wait(act, R * s + r + 1)
                        high_n.done(act.activation(nT[half][0][:, :, r * P:(r + 1) * P], banks[:, r, :, :], ACT.Copy))

                    def body(b, half, more):
                        s = 2 * b + half
                        stored[half].wait(act, 2 * b)
                        for hd in range(DC):
                            if more:
                                high(s + 1, 1 - half, hd)
                            q_done.wait(act, DC * s + hd + 1)
                            high_q.done(act.activation(qT[half][0][:, hd, :], q[:, hd, :], ACT.Copy))

                    for r in range(R):
                        high(0, 0, r)
                    loops(act, body)

                @block.vector
                def _(dve):
                    def statistics(b, half):
                        rows_in[half].wait(dve, b + 1)
                        norm.statistics(dve, rows[half], 2 * b + half)

                    def normalize(b, half):
                        s = 2 * b + half
                        turned.wait(dve, R * s)
                        normal.done(norm.normalize(dve, normed, rows[half], s))

                    def low(s, half, r):
                        high_n.wait(dve, R * s + r + 1)
                        low_n.done(dve.tensor_tensor(nT[half][1][:, :, r * P:(r + 1) * P], banks[:, r, :, :],
                                                     words(nT[half][0][:, :, r * P:(r + 1) * P]), ALU.subtract))

                    def split_q(s, half, hd):
                        high_q.wait(dve, DC * s + hd + 1)
                        low_q.done(dve.tensor_tensor(qT[half][1][:, hd, :], q[:, hd, :],
                                                     words(qT[half][0][:, hd, :]), ALU.subtract))

                    def body(b, half, more):
                        s = 2 * b + half
                        stored[half].wait(dve, 2 * b)
                        for hd in range(DC):
                            if more:
                                low(s + 1, 1 - half, hd)
                            if hd == 2 and more == 2:
                                statistics(b + 1, half)
                            if hd == 3 and more == 2:
                                normalize(b + 1, half)
                            made.wait(dve, DC * s + hd + 1)
                            low_q.wait(dve, DC * (s - 1) + hd + 1)
                            q_done.done(dve.scalar_tensor_tensor(
                                q[:, hd, :], outs[:, hd, :], q_bias[:, hd:hd + 1],
                                any_key[:, half * BANK:(half + 1) * BANK], ALU.add, ALU.mult))
                            if hd > 0:
                                split_q(s, half, hd - 1)
                        split_q(s, half, DC - 1)

                    for s in (normal, low_n, q_done, low_q):
                        s.open(dve)
                    bias_in.wait(dve, 1)
                    statistics(0, 0)
                    normalize(0, 0)
                    for r in range(R):
                        low(0, 0, r)
                    statistics(0, 1)
                    normalize(0, 1)
                    loops(dve, body)


GROUPS = D // P
GH = H // GROUPS
PAIRS = GH // 2


def cross_attention(nc, ident, ident_b, kT, qT, v, mask_q, mask_t, row, oT):
    HALF = S // BANK
    units = B * GROUPS * HALF
    QB = BANK // P
    MB, MKEYS = 4, 402
    MFIRST = [0, 400, 800, S2 - MKEYS]
    SLOTS = GH * QB * MB
    SLOTS_OF = [2, 8, 8, 6, 8, 8, 7, 9, 8] + [0] * (KT - 9)
    SLOT_OF = [sum(SLOTS_OF[:n]) for n in range(KT + 1)]
    assert SLOT_OF[KT] == SLOTS
    TURN = 9
    OWN = {"dve": (3, 6, 10), "pool": (0, 1, 2, 4, 5, 7, 8, 9, 11)}
    POOL_ADDS, DVE_ADDS = len(OWN["pool"]) - 1, len(OWN["dve"])
    RING = 4
    LOADS = 8
    SCALE = float(1.0 / np.sqrt(np.float32(DK)))
    MAXROW = 3 * DK
    ROWS97 = MAXROW + 1

    with ExitStack() as ctx:
        sb, ps, step = allocator(ctx, nc, "xa")
        kp = [sb(f"kp{i}", [P, GH, S2], F32R) for i in range(2)]
        qp = [sb(f"qp{i}", [P, GH, S], F32R) for i in range(2)]
        vg = [sb(f"vg{i}", [P, KT, P]) for i in range(2)]
        prob = [[sb(f"prob{i}{pr}", [P, 2, BANK]) for pr in range(PAIRS)] for i in range(RING)]
        sums = {who: [sb(f"sums_{who}{pr}", [P, 2, BANK]) for pr in range(PAIRS)] for who in OWN}
        ones = sb("ones", [P, DK])
        unread = [sb(f"unread{i}", [P, MKEYS], BF16) for i in range(2)]
        maxima, neg_max = sb("maxima", [P, GH * QB, MB]), sb("neg_max", [P, GH * QB])
        max_row = sb("max_row", [GH * QB, P], F32R)
        o_sb, sum_sb, out = sb("o_sb", [P, BANK]), sb("sum_sb", [P, BANK]), sb("out", [P, BANK])
        scores = [ps(f"scores{pr}", [P, 2, BANK]) for pr in range(PAIRS)]
        o_ps = ps("o_ps", [P, BANK])
        mx_ps = [ps(f"mx_ps{i}", [P, BANK]) for i in range(3)]
        peak_ps, sum_ps = mx_ps[0], mx_ps[1]

        loaded = step("loaded", size=16)
        const = step("const")
        mx_made, mx_read = step("mx_made"), step("mx_read", ahead=3)
        carried = step("carried")
        peaks = step("peaks", ahead=1)
        row_made = step("row_made")
        row_kept = step("row_kept", ahead=1)
        row_out, row_in = step("row_out", size=16, ahead=1), step("row_in", size=16)
        scored, exped = step("scored"), step("exped", ahead=PAIRS)
        weighed = step("weighed", ahead=RING)
        pool_added = step("pool_added", ahead=PAIRS * POOL_ADDS)
        dve_added = step("dve_added", ahead=PAIRS * DVE_ADDS)
        total_made = step("total_made", ahead=1)
        o_kept, sum_kept = step("o_kept", ahead=1), step("sum_kept", ahead=1)
        inverted, finished = step("inverted", ahead=1), step("finished", ahead=1)
        stored = step("stored", size=16, ahead=1)

        def keys_of(kt):
            return LAST if kt == KT - 1 else P

        def wait_added(eng, u, kt):
            if kt < 0:
                u, kt = u - 1, kt + KT
            if kt == KT - 1:
                return
            if kt in OWN["dve"]:
                dve_added.wait(eng, PAIRS * (DVE_ADDS * u + OWN["dve"].index(kt) + 1))
            else:
                pool_added.wait(eng, PAIRS * (POOL_ADDS * u + max(OWN["pool"].index(kt), 1)))

        def loops(eng, unit):
            def four(first, last):
                for n in range(2 * HALF):
                    unit(first + n, n // HALF, n % HALF, (KT * n) % RING, not (last and n == 2 * HALF - 1))

            with eng.Fori(0, units // (2 * HALF) - 1) as it:
                four(it * (2 * HALF), False)
            four(units - 2 * HALF, True)

        with nc.Block() as block:
            @block.sync
            def _(sp):
                def load(i, par):
                    for dst, (high_or_low, first) in enumerate(((0, 0), (0, DK), (1, 2 * DK))):
                        loaded.done(sp.dma_start(words(kp[par][first:first + DK, :, :]),
                                                 one(kT[high_or_low], i).rearrange("(j p) n -> p j n", p=DK)))
                    for dst, (high_or_low, first) in enumerate(((0, 0), (1, DK), (0, 2 * DK))):
                        loaded.done(sp.dma_start(words(qp[par][first:first + DK, :, :]),
                                                 one(qT[high_or_low], i).rearrange("(j p) n -> p j n", p=DK)))
                    whole = (KT - 1) * P
                    loaded.done(sp.dma_start(vg[par][:, 0:KT - 1, :],
                                             one(v, i)[0:whole, :].rearrange("(t p) n -> p t n", p=P)))
                    loaded.done(sp.dma_start(vg[par][0:LAST, KT - 1, :], one(v, i)[whole:S2, :]))

                def set_row(u, par, half):
                    row_kept.wait(sp, u + 1)
                    row_out.done(sp.dma_start(row, words(max_row[:, :])))
                    row_out.wait(sp, u + 1)
                    row_in.done(sp.dma_start(words(qp[par][MAXROW:ROWS97, :, half * BANK:(half + 1) * BANK]),
                                             row.rearrange("(o j t) n -> o j (t n)", o=1, j=GH)))

                def unit(u, par, half, _, more):
                    if half == 0 and not (isinstance(u, int) and u == units - HALF):
                        weighed.wait(sp, u * KT)
                        load_index = (u // HALF) + 1
                        load(load_index, 1 - par)
                    if more:
                        set_row(u + 1, par if half == 0 else 1 - par, 1 - half)
                    finished.wait(sp, u + 1)
                    stored.done(sp.dma_start(one(oT, u // HALF)[:, half * BANK:(half + 1) * BANK], out[:, :]))

                row_out.open(sp)
                stored.open(sp)
                load(0, 0)
                set_row(0, 0, 0)
                loops(sp, unit)
                stored.wait(sp, units)

            @block.gpsimd
            def _(pool):
                const.done(pool.memset(ones[:, :], 1.0))
                for i in range(2):
                    const.wait(pool, i + 1)
                    const.done(pool.memset(words(kp[i][MAXROW:ROWS97, :, :]), 1.0))

                def add(u, kt, left, right):
                    for pr in range(PAIRS):
                        exped.wait(pool, PAIRS * (KT * u + kt) + pr + 1)
                        pool_added.done(pool.tensor_tensor(sums["pool"][pr][:, :, :], left[pr][:, :, :],
                                                           right[pr][:, :, :], ALU.add))

                def unit(u, par, half, at, more):
                    total_made.wait(pool, u)
                    add(u, 1, prob[at], prob[(at + 1) % RING])
                    for n, kt in enumerate(OWN["pool"][2:]):
                        pool_added.wait(pool, PAIRS * (POOL_ADDS * u + n + 1))
                        add(u, kt, sums["pool"], prob[(at + kt) % RING])

                pool_added.open(pool)
                loops(pool, unit)

            @block.tensor
            def _(pe):
                def mx(u, par, half, slot):
                    j, qt, kb = slot // (QB * MB), slot // MB % QB, slot % MB
                    m = SLOTS * u + slot
                    mx_read.wait(pe, m - 2)
                    first = half * BANK + qt * P
                    mx_made.done(pe.matmul(mx_ps[slot % 3][:, 0:MKEYS], qp[par][0:MAXROW, j, first:first + P],
                                           kp[par][0:MAXROW, j, MFIRST[kb]:MFIRST[kb] + MKEYS], start=True, stop=True))

                def turn_peaks(u):
                    peaks.wait(pe, u + 1)
                    row_made.done(pe.transpose(peak_ps[0:GH * QB, 0:P], neg_max[:, :], ident[:, :]))

                def score(u, par, half, kt, pr, between):
                    keys = keys_of(kt)
                    if kt == 0 and pr == 0:
                        row_in.wait(pe, u + 1)
                    queries = slice(half * BANK, (half + 1) * BANK)
                    exped.wait(pe, PAIRS * (KT * u + kt - 1) + pr + 1)
                    for jj in range(2):
                        j = 2 * pr + jj
                        pe.matmul(scores[pr][0:keys, jj, :], kp[par][0:ROWS97, j, kt * P:kt * P + keys],
                                  qp[par][0:ROWS97, j, queries], start=True, stop=False)
                        last = pe.matmul(scores[pr][0:keys, jj, :], ident_b[0:keys, 0:keys],
                                         mask_t[0:keys, kt, queries], start=False, stop=True)
                        if jj == 1:
                            scored.done(last)
                        between()

                def four_heads(total, left, right, start, stop):
                    for j in range(GH):
                        mine = slice(j * DK, (j + 1) * DK)
                        last = pe.matmul(total[mine, :], left(mine), right[j // 2][0:left(mine).shape[0], j % 2, :],
                                         start=start, stop=stop, tile_position=(0, j * DK))
                    return last

                def weigh(u, par, kt, ring):
                    keys = keys_of(kt)
                    if kt == 0:
                        o_kept.wait(pe, u)
                    exped.wait(pe, PAIRS * (KT * u + kt + 1))
                    if kt == KT - 1:
                        sum_kept.wait(pe, u)
                        four_heads(sum_ps, lambda mine: ones[0:keys, :], prob[ring], True, False)
                    weighed.done(four_heads(o_ps, lambda mine: vg[par][0:keys, kt, mine], prob[ring],
                                            kt == 0, kt == KT - 1))

                def add_up(u):
                    wait_added(pe, u, OWN["dve"][-1])
                    four_heads(sum_ps, lambda mine: ones[:, :], sums["dve"], False, False)
                    wait_added(pe, u, OWN["pool"][-1])
                    total_made.done(four_heads(sum_ps, lambda mine: ones[:, :], sums["pool"], False, True))

                def unit(u, par, half, at, more):
                    nxt = (par if half == 0 else 1 - par, 1 - half)
                    for kt in range(KT):
                        if more and kt == 0:
                            row_kept.wait(pe, u + 1)
                            sum_kept.wait(pe, u)
                            if half == 1:
                                loaded.wait(pe, LOADS * (u // HALF + 2))
                        slots = iter(range(SLOT_OF[kt], SLOT_OF[kt + 1]) if more else ())

                        def maximum():
                            for slot in itertools.islice(slots, 1):
                                mx(u + 1, *nxt, slot)

                        for pr in range(PAIRS):
                            if kt + 1 < KT:
                                score(u, par, half, kt + 1, pr, maximum)
                            elif more:
                                score(u + 1, *nxt, 0, pr, maximum)
                        if more and kt == TURN:
                            turn_peaks(u + 1)
                        if SLOTS_OF[kt] > 6:
                            maximum()
                        weigh(u, par, kt, (at + kt) % RING)
                        for _ in range(SLOTS_OF[kt]):
                            maximum()
                    add_up(u)

                weighed.open(pe)
                total_made.open(pe)
                const.wait(pe, 3)
                loaded.wait(pe, LOADS)
                for slot in range(SLOTS):
                    mx(0, 0, 0, slot)
                turn_peaks(0)
                for pr in range(PAIRS):
                    score(0, 0, 0, 0, pr, lambda: None)
                loops(pe, unit)

            @block.scalar
            def _(act):
                def keep_row(u):
                    row_made.wait(act, u + 1)
                    row_out.wait(act, u)
                    row_kept.done(act.activation(max_row[:, :], peak_ps[0:GH * QB, 0:P], ACT.Copy))

                def exp(u, kt, ring):
                    n, keys = KT * u + kt, keys_of(kt)
                    weighed.wait(act, n - RING + 1)
                    wait_added(act, u, kt - RING)
                    for pr in range(PAIRS):
                        scored.wait(act, PAIRS * n + pr + 1)
                        exped.done(act.activation(prob[ring][pr][0:keys, :, :], scores[pr][0:keys, :, :], ACT.Exp,
                                                  scale=SCALE))

                def unit(u, par, half, at, more):
                    for kt in range(KT):
                        if kt + 1 < KT:
                            exp(u, kt + 1, (at + kt + 1) % RING)
                        elif more:
                            exp(u + 1, 0, (at + KT) % RING)
                        if more and kt == TURN:
                            keep_row(u + 1)
                    weighed.wait(act, KT * (u + 1))
                    finished.wait(act, u)
                    o_kept.done(act.activation(o_sb[:, :], o_ps[:, :], ACT.Copy))
                    total_made.wait(act, u + 1)
                    sum_kept.done(act.activation(sum_sb[:, :], sum_ps[:, :], ACT.Copy))

                for s in (row_kept, exped, o_kept, sum_kept):
                    s.open(act)
                keep_row(0)
                exp(0, 0, 0)
                loops(act, unit)

            @block.vector
            def _(dve):
                def read(u, half, slot):
                    j_qt, kb, qt = slot // MB, slot % MB, slot // MB % QB
                    m = SLOTS * u + slot
                    mx_read.wait(dve, m - 1)
                    mx_made.wait(dve, m + 1)
                    dve.sem_inc(carried.sem, 1)
                    mx_read.done(dve.tensor_tensor_reduce(
                        out=unread[slot % 2][:, :], in0=mx_ps[slot % 3][:, 0:MKEYS],
                        in1=mask_q[:, half * QB + qt, MFIRST[kb]:MFIRST[kb] + MKEYS], scale=1.0, scalar=LOWEST,
                        op0=ALU.add, op1=ALU.max, accum_out=maxima[:, j_qt, kb:kb + 1]))

                def peak(u):
                    mx_read.wait(dve, SLOTS * (u + 1))
                    row_made.wait(dve, u)
                    peaks.done(dve.tensor_reduce(neg_max[:, :], maxima[:, :, :], AX.X, ALU.max, negate=True))

                def add(u, kt, ring, i, pr):
                    if i == 0:
                        total_made.wait(dve, u)
                    else:
                        dve_added.wait(dve, PAIRS * (DVE_ADDS * u + i))
                    exped.wait(dve, PAIRS * (KT * u + kt) + pr + 1)
                    mine, new = sums["dve"][pr][:, :, :], prob[ring][pr][:, :, :]
                    dve_added.done(dve.tensor_tensor(mine, mine, new, ALU.add) if i else dve.tensor_copy(mine, new))

                def unit(u, par, half, at, more):
                    for kt in range(KT):
                        for pr in range(PAIRS):
                            middle = (SLOT_OF[kt] + SLOT_OF[kt + 1]) // 2
                            mine = (SLOT_OF[kt], middle) if pr == 0 else (middle, SLOT_OF[kt + 1])
                            for slot in range(*mine) if more else ():
                                read(u + 1, 1 - half, slot)
                            if kt in OWN["dve"]:
                                add(u, kt, (at + kt) % RING, OWN["dve"].index(kt), pr)
                        if more and kt == TURN - 1:
                            peak(u + 1)
                    sum_kept.wait(dve, u + 1)
                    inverted.done(dve.reciprocal(sum_sb[:, :], sum_sb[:, :]))
                    inverted.wait(dve, u + 1)
                    o_kept.wait(dve, u + 1)
                    stored.wait(dve, u)
                    finished.done(dve.tensor_tensor(out[:, :], o_sb[:, :], sum_sb[:, :], ALU.mult))

                for s in (mx_read, peaks, dve_added, finished, inverted):
                    s.open(dve)
                for slot in range(SLOTS):
                    read(0, 0, slot)
                peak(0)
                loops(dve, unit)


def split_plain(nc, tag, pieces):
    with ExitStack() as ctx:
        sb, _, step = allocator(ctx, nc, tag)
        STAGES = 3
        widest = max(high.shape[1] * high.shape[2] for _, high, _ in pieces)
        stage = [sb(f"stage{i}", [P, widest]) for i in range(STAGES)]
        loaded = [step(f"loaded{i}", size=16) for i in range(STAGES)]
        high_done, low_done = step("high"), step("low", ahead=STAGES)

        def staged(n):
            m, width = pieces[n][1].shape[1:]
            return stage[n % STAGES][:, 0:m * width].rearrange("p (m n) -> p m n", m=m)

        with nc.Block() as block:
            @block.sync
            def _(sp):
                for n, (src, _, _) in enumerate(pieces):
                    low_done.wait(sp, n - STAGES + 1)
                    loaded[n % STAGES].done(sp.dma_start(staged(n), src))

            @block.scalar
            def _(act):
                for n, (_, high, _) in enumerate(pieces):
                    loaded[n % STAGES].wait(act, n // STAGES + 1)
                    high_done.done(act.activation(high, staged(n), ACT.Copy))

            @block.vector
            def _(dve):
                low_done.open(dve)
                for n, (_, high, low) in enumerate(pieces):
                    high_done.wait(dve, n + 1)
                    low_done.done(dve.tensor_tensor(low, staged(n), words(high), ALU.subtract))


def hidden_layers(nc, ident, oT, Wo, bo, x1, w_in, w_gate, gate_bias, x2, hT, weights):
    R = BANK // P
    steps = TOK // BANK
    NH = 2 * DC
    x_rows = x1.rearrange("(s r p) n -> s p r n", p=P, r=R)
    x2_rows = x2.rearrange("(s r p) n -> s p r n", p=P, r=R)
    oT_half = oT.rearrange("(b g) p n -> b p g n", g=GROUPS)
    hT_rows = hT.rearrange("(s r) p w c n -> s w p c r n", r=R)
    with ExitStack() as keep:
        sb, _, _ = allocator(keep, nc, "hd")
        parts = ("high", "low")
        wo = [sb(f"wo_{part}", [P, DC, D], F32R) for part in parts]
        wi = [[sb(f"wi{w}_{part}", [P, DC, 2 * D], F32R) for part in parts] for w in range(2)]
        wg = [sb(f"wg_{part}", [P, DC, E], F32R) for part in parts]
        split_weights(nc, ident, "hdo", [Wo], [wo])
        by_chunk = "(c p) n -> p c n"
        split_plain(nc, "hdi", [(w_in[w].rearrange(by_chunk, p=P)[:, part, :], wi[w][0][:, part, :], wi[w][1][:, part, :])
                                for w in range(2) for part in (slice(0, DC // 2), slice(DC // 2, DC))]
                    + [(w_gate.rearrange(by_chunk, p=P), wg[0][:, :, :], wg[1][:, :, :])])
        with ExitStack() as ctx:
            sb, ps, step = allocator(ctx, nc, "hdl")
            o_bias, g_bias = sb("o_bias", [P, D]), sb("g_bias", [P, E])
            o_in = sb("o_in", [P, GROUPS, BANK])
            o_parts = [sb(f"o_{part}", [P, GROUPS, BANK], F32R) for part in parts]
            rows, rows2 = sb("rows", [P, R, D]), sb("rows2", [P, R, D])
            norm = LayerNorm(sb, step, R)
            nT = [[sb(f"nT_{part}{i}", [P, DC, BANK], F32R) for part in parts] for i in range(2)]
            gated = [sb(f"gated{i}", [P, BANK]) for i in range(2)]
            hidden = [sb(f"hidden{w}", [P, DC, BANK]) for w in range(2)]
            logits_t = sb("logits_t", [P, BANK])
            logits, probs = sb("logits", [P, R, E]), sb("probs", [P, R, E])
            top, sums, inv_sums = sb("top", [P, R]), sb("sums", [P, R]), sb("inv_sums", [P, R])
            best, best_at, best_at_f = sb("best", [P, R, 8]), sb("best_at", [P, R, 8], U32), sb("best_at_f", [P, R, 8])
            number = sb("number", [P, E])
            second = sb("second", [P, R, E])
            proj_ps = [ps(f"proj_ps{i}", [P, BANK]) for i in range(2)]
            turn_ps = ps("turn_ps", [P, DC, P])
            pair_ps = [ps(f"pair_ps{i}", [P, 2, BANK]) for i in range(2)]
            gate_ps = ps("gate_ps", [P, BANK])

            setup_in, const = step("setup_in", size=16), step("const")
            o_loaded, x_loaded = step("o_loaded", size=16), step("x_loaded", size=16)
            o_high, o_low = step("o_high", ahead=1), step("o_low", ahead=1)
            biased = step("biased")
            projected, added = step("projected", ahead=R), step("added", ahead=2)
            x2_stored = step("x2_stored", size=16, ahead=1)
            normal, turned = step("normal", ahead=1), step("turned")
            high_n, low_n = step("high_n"), step("low_n", ahead=1)
            paired, silu, hid = step("paired"), step("silu"), step("hid", ahead=2)
            h_stored = [step(f"h_stored{w}", size=16, ahead=R) for w in range(2)]
            gated_t, gate_kept, gate_turned = step("gated_t", ahead=1), step("gate_kept", ahead=1), step("gate_turned", ahead=1)
            shifted, gate_exp, routed = step("shifted"), step("gate_exp"), step("routed", ahead=1)

            def loops(eng, body):
                with eng.Fori(0, B - 1) as b:
                    for half in range(2):
                        body(2 * b + half, half, 2)
                body(steps - 2, 0, 1)
                body(steps - 1, 1, 0)

            with nc.Block() as block:
                @block.sync
                def _(sp):
                    setup_in.done(sp.dma_start(o_bias[:, :], bo.partition_broadcast(P)))
                    setup_in.done(sp.dma_start(g_bias[:, :], gate_bias.partition_broadcast(P)))

                    def load(s, half):
                        o_low.wait(sp, s)
                        b = s // 2
                        o_loaded.done(sp.dma_start(o_in[:, :, :], one(oT_half, b)[:, :, half * BANK:(half + 1) * BANK]))
                        x2_stored.wait(sp, s)
                        normal.wait(sp, s)
                        x_loaded.done(sp.dma_start(rows[:, :, :], one(x_rows, s)))

                    def store_x2(s):
                        added.wait(sp, R * (s + 1))
                        x2_stored.done(sp.dma_start(one(x2_rows, s), rows[:, :, :]))

                    def body(s, half, more):
                        if more:
                            store_x2(s + 1)
                        if more == 2:
                            load(s + 2, half)
                        for w in range(2):
                            hid.wait(sp, NH * s + DC * (w + 1))
                            for r in range(R):
                                h_stored[w].done(sp.dma_start(one(hT_rows, s)[w, :, :, r, :],
                                                              hidden[w][:, :, r * P:(r + 1) * P]))

                    x2_stored.open(sp)
                    for w in range(2):
                        h_stored[w].open(sp)
                    load(0, 0)
                    store_x2(0)
                    load(1, 1)
                    loops(sp, body)
                    x2_stored.wait(sp, steps)
                    for w in range(2):
                        h_stored[w].wait(sp, R * steps)

                @block.gpsimd
                def _(pool):
                    norm.pool_setup(pool)
                    for e in range(E):
                        const.done(pool.memset(number[:, e:e + 1], float(e)))
                        const.wait(pool, e + 1)
                    const.done(pool.memset(logits_t[:, :], 0.0))
                    setup_in.wait(pool, 2)
                    with pool.Fori(0, steps) as s:
                        x_loaded.wait(pool, s + 1)
                        for r in range(R):
                            last = pool.tensor_tensor(rows[:, r, :], rows[:, r, :], o_bias[:, :], ALU.add)
                            biased.done(last)
                            biased.wait(pool, R * s + r + 1)
                        norm.pool_step(pool, s)

                @block.tensor
                def _(pe):
                    def project(s):
                        o_low.wait(pe, s + 1)
                        for r in range(R):
                            added.wait(pe, R * s + r - 1)
                            for g in range(GROUPS):
                                last = matmul3(pe, proj_ps[r % 2][:, :], [o[:, g, r * P:(r + 1) * P] for o in o_parts],
                                               [w[:, g, :] for w in wo], g == 0, g == GROUPS - 1)
                            projected.done(last)

                    def turn(s, r):
                        normal.wait(pe, s + 1)
                        low_n.wait(pe, R * s + r)
                        for dc in range(DC):
                            last = pe.transpose(turn_ps[:, dc, :], rows2[:, r, dc * P:(dc + 1) * P], ident[:, :])
                        turned.done(last)

                    def pair(s, half, n):
                        w, c = n // DC, n % DC
                        hid.wait(pe, NH * s + n - 1)
                        for side in range(2):
                            cols = slice(side * D + c * P, side * D + (c + 1) * P)
                            for dc in range(DC):
                                last = matmul3(pe, pair_ps[n % 2][:, side, :], [x[:, dc, cols] for x in wi[w]],
                                               [x[:, dc, :] for x in nT[half]], dc == 0, dc == DC - 1)
                        paired.done(last)

                    def gate(s, half):
                        routed.wait(pe, s)
                        for dc in range(DC):
                            last = matmul3(pe, gate_ps[0:E, :], [x[:, dc, :] for x in wg],
                                           [x[:, dc, :] for x in nT[half]], dc == 0, dc == DC - 1)
                        gated_t.done(last)

                    def turn_gate(s):
                        gate_kept.wait(pe, s + 1)
                        for r in range(R):
                            last = pe.transpose(gate_ps[:, r * P:(r + 1) * P], logits_t[:, r * P:(r + 1) * P], ident[:, :])
                        gate_turned.done(last)

                    def body(s, half, more):
                        if more:
                            project(s + 1)
                        low_n.wait(pe, R * (s + 1))
                        for n in range(NH // 2):
                            pair(s, half, n)
                        gate(s, half)
                        for n in range(NH // 2, NH):
                            if more:
                                turn(s + 1, n - NH // 2)
                            pair(s, half, n)
                            if n == NH // 2:
                                turn_gate(s)

                    for st in (projected, gated_t, gate_turned):
                        st.open(pe)
                    project(0)
                    for r in range(R):
                        turn(0, r)
                    loops(pe, body)

                @block.scalar
                def _(act):
                    def split_o(s):
                        o_loaded.wait(act, s + 1)
                        projected.wait(act, R * s)
                        o_high.done(act.activation(o_parts[0][:, :, :], o_in[:, :, :], ACT.Copy))

                    def split_n(s, half, r):
                        turned.wait(act, R * s + r + 1)
                        high_n.done(act.activation(nT[half][0][:, :, r * P:(r + 1) * P], turn_ps[:, :, :], ACT.Copy))

                    def activate(s, n):
                        hid.wait(act, NH * s + n - 1)
                        paired.wait(act, NH * s + n + 1)
                        silu.done(act.activation(gated[n % 2][:, :], pair_ps[n % 2][:, 0, :], ACT.Silu))

                    def body(s, half, more):
                        for n in range(NH // 2):
                            activate(s, n)
                        if more == 2:
                            split_o(s + 2)
                        gated_t.wait(act, s + 1)
                        gate_turned.wait(act, s)
                        gate_kept.done(act.activation(logits_t[0:E, :], gate_ps[0:E, :], ACT.Copy))
                        for n in range(NH // 2, NH):
                            if more:
                                split_n(s + 1, 1 - half, n - NH // 2)
                            activate(s, n)
                            if n == NH // 2 + 1:
                                shifted.wait(act, s + 1)
                                gate_exp.done(act.activation(probs[:, :, :], logits[:, :, :], ACT.Exp))

                    o_high.open(act)
                    gate_kept.open(act)
                    const.wait(act, E + 1)
                    split_o(0)
                    for r in range(R):
                        split_n(0, 0, r)
                    split_o(1)
                    loops(act, body)

                @block.vector
                def _(dve):
                    def split_o(s):
                        o_high.wait(dve, s + 1)
                        projected.wait(dve, R * s)
                        o_low.done(dve.tensor_tensor(o_parts[1][:, :, :], o_in[:, :, :], words(o_parts[0][:, :, :]),
                                                     ALU.subtract))

                    def add(s):
                        for r in range(R):
                            biased.wait(dve, R * s + r + 1)
                            projected.wait(dve, R * s + r + 1)
                            added.done(dve.tensor_tensor(rows[:, r, :], proj_ps[r % 2][:, :], rows[:, r, :], ALU.add))
                        added.wait(dve, R * (s + 1))
                        norm.statistics(dve, rows, s)
                        turned.wait(dve, R * s)
                        normal.done(norm.normalize(dve, rows2, rows, s))

                    def split_n(s, half, r):
                        high_n.wait(dve, R * s + r + 1)
                        low_n.done(dve.tensor_tensor(nT[half][1][:, :, r * P:(r + 1) * P], turn_ps[:, :, :],
                                                     words(nT[half][0][:, :, r * P:(r + 1) * P]), ALU.subtract))

                    def multiply(s, n):
                        w, c = n // DC, n % DC
                        if c == 0:
                            h_stored[w].wait(dve, R * s)
                        silu.wait(dve, NH * s + n + 1)
                        hid.done(dve.tensor_tensor(hidden[w][:, c, :], gated[n % 2][:, :], pair_ps[n % 2][:, 1, :],
                                                   ALU.mult))

                    def shift(s):
                        gate_turned.wait(dve, s + 1)
                        for r in range(R):
                            last = dve.tensor_tensor(logits[:, r, :], gate_ps[:, r * P:r * P + E], g_bias[:, :], ALU.add)
                        dve.drain()
                        dve.tensor_reduce(top[:, :], logits[:, :, :], AX.X, ALU.max)
                        dve.drain()
                        for r in range(R):
                            last = dve.tensor_scalar(logits[:, r, :], logits[:, r, :], top[:, r:r + 1], None,
                                                     ALU.subtract)
                        shifted.done(last)

                    def route(s):
                        gate_exp.wait(dve, s + 1)
                        dve.tensor_reduce(sums[:, :], probs[:, :, :], AX.X, ALU.add)
                        dve.drain()
                        dve.reciprocal(inv_sums[:, :], sums[:, :])
                        dve.drain()
                        for r in range(R):
                            dve.tensor_scalar(probs[:, r, :], probs[:, r, :], inv_sums[:, r:r + 1], None, ALU.mult)
                        dve.drain()
                        for r in range(R):
                            dve.max(best[:, r, :], probs[:, r, :])
                        dve.drain()
                        for r in range(R):
                            dve.max_index(best_at[:, r, :], best[:, r, :], probs[:, r, :])
                        dve.drain()
                        dve.tensor_copy(best_at_f[:, :, :], best_at[:, :, :])
                        dve.drain()
                        first = [probs, second]
                        for r in range(R):
                            for k in range(2):
                                dve.tensor_scalar(first[k][:, r, :], number[:, :], best_at_f[:, r, k:k + 1],
                                                  best[:, r, k:k + 1], ALU.is_equal, ALU.mult)
                        dve.drain()
                        routed.done(dve.tensor_tensor(weights[:, ds(R * s, R), :], probs[:, :, :], second[:, :, :],
                                                      ALU.add))

                    def body(s, half, more):
                        if more:
                            add(s + 1)
                        for n in range(NH // 2):
                            multiply(s, n)
                        if more == 2:
                            split_o(s + 2)
                        for n in range(NH // 2, NH):
                            if more:
                                split_n(s + 1, 1 - half, n - NH // 2)
                            multiply(s, n)
                            if n == NH // 2:
                                shift(s)
                            if n == NH // 2 + 1:
                                route(s)

                    for st in (o_low, added, normal, low_n, hid, routed):
                        st.open(dve)
                    setup_in.wait(dve, 2)
                    const.wait(dve, E)
                    split_o(0)
                    add(0)
                    for r in range(R):
                        split_n(0, 0, r)
                    split_o(1)
                    loops(dve, body)


def experts(nc, hT, x2, w_out, w2, weights, y):
    tiles = TOK // P
    OUTS = E + 1
    BANKS = 6
    parts = ("high", "low")
    x_t, y_t = tokens(x2), tokens(y)
    with ExitStack() as keep:
        sb, _, _ = allocator(keep, nc, "ex")
        wo = [sb(f"wo_{part}", [P, DC, D], F32R) for part in parts]
        wx = [sb(f"wx_{part}", [P, E, DC, D], F32R) for part in parts]
        by_chunk = "(c p) n -> p c n"
        split_plain(nc, "exw", [(w_out.rearrange(by_chunk, p=P), wo[0][:, :, :], wo[1][:, :, :])]
                    + [(w2[e].rearrange(by_chunk, p=P), wx[0][:, e, :, :], wx[1][:, e, :, :]) for e in range(E)])
        with ExitStack() as ctx:
            sb, ps, step = allocator(ctx, nc, "exl")
            h_in = [sb(f"h_in{i}", [P, 2, DC, P]) for i in range(2)]
            h = [[sb(f"h_{part}{i}", [P, 2, DC, P], F32R) for part in parts] for i in range(2)]
            rows = [sb(f"rows{i}", [P, D]) for i in range(2)]
            banks = [ps(f"banks{i}", [P, D]) for i in range(BANKS)]
            h_loaded = [step(f"h_loaded{i}", size=16) for i in range(2)]
            x_loaded = [step(f"x_loaded{i}", size=16) for i in range(2)]
            high, low = step("high", ahead=2), step("low", ahead=2)
            made, summed = step("made", ahead=2 * OUTS), step("summed", ahead=max(BANKS, OUTS))
            stored = [step(f"stored{i}", size=16, ahead=1) for i in range(2)]

            def loops(eng, body):
                with eng.Fori(0, tiles // 2) as n:
                    for odd in range(2):
                        body(n, 2 * n + odd, odd)

            with nc.Block() as block:
                @block.sync
                def _(sp):
                    def load(n, t, odd):
                        low.wait(sp, t - 1)
                        h_loaded[odd].done(sp.dma_start(h_in[odd][:, :, :, :], one(hT, t)))
                        stored[odd].wait(sp, n)
                        x_loaded[odd].done(sp.dma_start(rows[odd][:, :], one(x_t, t)))

                    def body(n, t, odd, more=True):
                        if more:
                            load(n + odd, t + 1, 1 - odd)
                        summed.wait(sp, OUTS * (t + 1))
                        stored[odd].done(sp.dma_start(one(y_t, t), rows[odd][:, :]))

                    for st in stored:
                        st.open(sp)
                    load(0, 0, 0)
                    with sp.Fori(0, tiles // 2 - 1) as n:
                        for odd in range(2):
                            body(n, 2 * n + odd, odd)
                    body(tiles // 2 - 1, tiles - 2, 0)
                    body(tiles // 2 - 1, tiles - 1, 1, False)
                    for st in stored:
                        st.wait(sp, tiles // 2)

                @block.scalar
                def _(act):
                    def body(n, t, odd):
                        h_loaded[odd].wait(act, n + 1)
                        made.wait(act, OUTS * (t - 1))
                        high.done(act.activation(h[odd][0][:, :, :, :], h_in[odd][:, :, :, :], ACT.Copy))

                    high.open(act)
                    loops(act, body)

                @block.tensor
                def _(pe):
                    def body(n, t, odd):
                        low.wait(pe, t + 1)
                        for o in range(OUTS):
                            which = min(o, 1)
                            summed.wait(pe, OUTS * t + o - BANKS + 1)
                            out = banks[(OUTS * odd + o) % BANKS]
                            right = wo if o == 0 else [w[:, o - 1, :, :] for w in wx]
                            for c in range(DC):
                                last = matmul3(pe, out[:, :], [x[:, which, c, :] for x in h[odd]],
                                               [w[:, c, :] for w in right], c == 0, c == DC - 1)
                            made.done(last)

                    made.open(pe)
                    loops(pe, body)

                @block.vector
                def _(dve):
                    def split(t, odd):
                        high.wait(dve, t + 1)
                        low.done(dve.tensor_tensor(h[odd][1][:, :, :, :], h_in[odd][:, :, :, :],
                                                   words(h[odd][0][:, :, :, :]), ALU.subtract))

                    def body(n, t, odd, more=True):
                        x_loaded[odd].wait(dve, n + 1)
                        for o in range(OUTS):
                            made.wait(dve, OUTS * t + o + 1)
                            out = banks[(OUTS * odd + o) % BANKS]
                            if o == 0:
                                summed.done(dve.tensor_tensor(rows[odd][:, :], out[:, :], rows[odd][:, :], ALU.add))
                            else:
                                summed.wait(dve, OUTS * t + o)
                                summed.done(dve.scalar_tensor_tensor(
                                    rows[odd][:, :], out[:, :], weights[:, ds(t, 1), o - 1:o].squeeze(1), rows[odd][:, :],
                                    ALU.mult, ALU.add))
                            if o == OUTS // 2 and more:
                                split(t + 1, 1 - odd)

                    low.open(dve)
                    summed.open(dve)
                    split(0, 0)
                    with dve.Fori(0, tiles // 2 - 1) as n:
                        for odd in range(2):
                            body(n, 2 * n + odd, odd)
                    body(tiles // 2 - 1, tiles - 2, 0)
                    body(tiles // 2 - 1, tiles - 1, 1, False)


def decoder_layer(nc, x, context, mask, k, v, Wq, bq, Wk, bk, Wv, bv, Wo, bo, w_shared_in, w_shared_out, w1, w2,
                  w_gate, gate_bias, y):
    def dram(name, shape, dt=F32):
        return nc.dram_tensor(name, shape, dt).ap()

    x1, x2 = dram("x1", [TOK, D]), dram("x2", [TOK, D])
    kT = [dram(f"kT_{part}", [B, D, S2]) for part in ("high", "low")]
    qT = [dram(f"qT_{part}", [B, D, S]) for part in ("high", "low")]
    values = dram("values", [B, GROUPS, S2, P])
    row = dram("row", [H, P])
    oT = dram("oT", [B * GROUPS, P, S])
    hT = dram("hT", [TOK // P, P, 2, DC, P])
    by_group = "b (g p) n -> (b g) p n"
    with ExitStack() as ctx:
        def sb(name, shape, dt=F32):
            return ctx.enter_context(nc.sbuf_tensor(name, shape, dt))

        ident, ident_b = sb("ident", [P, P]), sb("ident_b", [P, P], BF16)
        make_identity(nc, ident, ident_b)
        self_attention(nc, ident, x, k, v, x1)
        with ExitStack() as masks:
            mask_q = masks.enter_context(nc.sbuf_tensor("mask_q", [P, QT, S2], BF16))
            mask_t = masks.enter_context(nc.sbuf_tensor("mask_t", [P, KT, S], BF16))
            with nc.sbuf_tensor("any_key", [P, S], F32) as any_key:
                context_keys_values(nc, ident, ident_b, context, Wk, bk, Wv, bv, mask, (mask_q, mask_t, any_key), kT, values)
                project_queries(nc, ident, x1, Wq, bq, any_key, qT)
            cross_attention(nc, ident, ident_b, [a.rearrange(by_group, p=P) for a in kT],
                            [a.rearrange(by_group, p=P) for a in qT], values.rearrange("b g n p -> (b g) n p"),
                            mask_q, mask_t, row, oT)
        weights = sb("weights", [P, TOK // P, E])
        hidden_layers(nc, ident, oT, Wo, bo, x1, [w_shared_in, w1], w_gate, gate_bias, x2, hT, weights)
        experts(nc, hT, x2, w_shared_out, w2, weights, y)


INPUTS = ["x", "ctx_1024", "mask_1x1xSxS2_ik0", "L0_attn_k", "L0_attn_v", "L0_xattn_Wq_w", "L0_xattn_Wq_b",
          "L0_xattn_Wk_w", "L0_xattn_Wk_b", "L0_xattn_Wv_w", "L0_xattn_Wv_b", "L0_xattn_Wo_w", "L0_xattn_Wo_b",
          "L0_ffn_w_shared_in", "L0_ffn_w_shared_out", "L0_ffn_w1_shared", "L0_ffn_w2", "L0_ffn_w_gate",
          "L0_ffn_gate_bias"]


def kernel(**inputs):
    import concourse.bacc as bacc
    from concourse.bass_utils import run_bass_kernel_spmd

    nc = bacc.Bacc("TRN2", target_bir_lowering=False, num_devices=1)
    arrays, args = {}, []
    for name in INPUTS:
        a = np.ascontiguousarray(inputs[name])
        arrays[f"in_{name}"] = a
        args.append(nc.dram_tensor(f"in_{name}", a.shape, mybir.dt.from_np(a.dtype), kind="ExternalInput").ap())
    y = nc.dram_tensor("out_y", [TOK, D], F32, kind="ExternalOutput").ap()
    decoder_layer(nc, *args, y)
    result = run_bass_kernel_spmd(nc, [arrays], core_ids=[0])
    return result.results[0]["out_y"].reshape(B, S, D)
```

```python
import concourse.bass as bass
from concourse import mybir
from concourse.alu_op_type import AluOpType as ALU
from contextlib import ExitStack
import itertools
import numpy as np

F32 = mybir.dt.float32
F32R = mybir.dt.float32r
BF16 = mybir.dt.bfloat16
I32 = mybir.dt.int32
U32 = mybir.dt.uint32
ACT = mybir.ActivationFunctionType
AX = mybir.AxisListType
ds = bass.ds

P = 128
B, S, D = 4, 1024, 512
TOK = B * S
DC = D // P
T1 = 2048
T1C = T1 // P
S2 = 1601
H, DK = 16, 32
E = 8
BANK = 512
EPS = 1e-5
LOWEST = -3.0e38


class Step:

    def __init__(self, ctx, nc, name, ahead=None, size=1):
        self.sem = ctx.enter_context(nc.semaphore(name))
        self.ahead, self.size = 0 if ahead is None else ahead + 1, size

    def open(self, eng):
        eng.sem_inc(self.sem, self.ahead * self.size)

    def done(self, instruction):
        instruction.then_inc(self.sem, self.size)

    def wait(self, eng, n):
        eng.wait_ge(self.sem, (n + self.ahead) * self.size)


def words(ap):
    return ap.bitcast(F32)


def matmul3(pe, out, left, right, start, stop):
    (lh, ll), (rh, rl) = left, right
    pe.matmul(out, lh, rh, start=start, stop=False)
    pe.matmul(out, lh, rl, start=False, stop=False)
    return pe.matmul(out, ll, rh, start=False, stop=stop)


def allocator(ctx, nc, tag):
    def sb(name, shape, dt=F32):
        return ctx.enter_context(nc.sbuf_tensor(f"{tag}_{name}", shape, dt))

    def ps(name, shape, dt=F32):
        return ctx.enter_context(nc.psum_tensor(f"{tag}_{name}", shape, dt))

    def step(name, **more):
        return Step(ctx, nc, f"{tag}_{name}", **more)

    return sb, ps, step


def make_identity(nc, ident, ident_b):
    with ExitStack() as ctx:
        _, _, step = allocator(ctx, nc, "id")
        made = step("made")
        with nc.Block() as block:
            @block.gpsimd
            def _(pool):
                made.done(pool.memset(ident[:, :], 0.0))
                made.wait(pool, 1)
                made.done(pool.affine_select(out=ident[:, :], in_=ident[:, :], compare_op=ALU.not_equal,
                                             fill=1.0, base=0, pattern=[[-1, P]], channel_multiplier=1))
                made.wait(pool, 2)
                made.done(pool.tensor_copy(ident_b[:, :], ident[:, :]))


def tokens(ap):
    return ap.rearrange("(t p) n -> t p n", p=P)


def one(ap, i):
    return ap[ds(i, 1)].squeeze(0)


def self_attention(nc, ident, x, k, v, x1):
    NB = T1 // BANK
    KB = BANK // P
    tiles = TOK // P
    with ExitStack() as keep:
        sb, _, _ = allocator(keep, nc, "sa")
        kT = [sb(f"kT_{part}", [P, DC, T1], F32R) for part in ("high", "low")]
        vs = [sb(f"v_{part}", [P, T1C, D], F32R) for part in ("high", "low")]
        scale = sb("scale", [P, B, NB, D])
        self_attention_setup(nc, ident, x, k, v, kT, vs, scale)
        self_attention_loop(nc, ident, x, x1, kT, vs, scale, NB, KB, tiles)


def self_attention_setup(nc, ident, x, k, v, kT, vs, scale):
    G, TILES, V_TILES, BANKS = B * 4, 4, 4, 8
    K_PARTS, V_PARTS = T1C // TILES, T1C // V_TILES
    rows_of_scale = x.rearrange("b (j r) n -> (b j) r n", j=4)[:, 0, :]
    k_rows = k[0].rearrange("(n r p) d -> n p r d", p=P, r=TILES)
    v_rows = v[0].rearrange("(n r p) d -> n p r d", p=P, r=V_TILES)
    with ExitStack() as ctx:
        sb, ps, step = allocator(ctx, nc, "sas")
        k_in, banks = [sb(f"k_in{i}", [P, TILES, D]) for i in range(2)], ps("banks", [P, BANKS, DC, P])
        v_in = [sb(f"v_in{i}", [P, V_TILES, D]) for i in range(2)]
        stats = sb("stats", [P, G, 6])
        mean_var = sb("mean_var", [P, G, 2])
        var, rstd, power = sb("var", [P, G]), sb("rstd", [P, G]), sb("power", [P, G])
        k_loaded = [step(f"k_loaded{i}", size=16) for i in range(2)]
        turned, k_high, k_low = step("turned"), step("k_high"), step("k_low")
        v_loaded = [step(f"v_loaded{i}", size=16) for i in range(2)]
        v_low = [step("v_low_dve"), step("v_low_pool")]
        v_high, s_loaded = step("v_high"), step("s_loaded", size=16)
        chain, pow_set, root = step("chain"), step("pow_set"), step("root")
        groups = scale[:, :, :, :].rearrange("p b j d -> p (b j) d")

        def k_tile(part, n, r):
            first = (TILES * n + r) * P
            return kT[part][:, :, first:first + P]

        def v_tiles(part, n):
            return vs[part][:, n * V_TILES:(n + 1) * V_TILES, :]

        def low_v(eng, n):
            v_high.wait(eng, n + 1)
            v_low[n % 2].done(eng.tensor_tensor(v_tiles(1, n), v_in[n % 2][:, :, :], words(v_tiles(0, n)), ALU.subtract))

        with nc.Block() as block:
            @block.sync
            def _(sp):
                def load_v(n):
                    if n >= 2:
                        v_low[n % 2].wait(sp, n // 2)
                    v_loaded[n % 2].done(sp.dma_start(v_in[n % 2][:, :, :], v_rows[n]))

                def load_k(n):
                    if n >= 2:
                        turned.wait(sp, TILES * (n - 1))
                    k_loaded[n % 2].done(sp.dma_start(k_in[n % 2][:, :, :], k_rows[n]))

                load_k(0)
                load_k(1)
                s_loaded.done(sp.dma_start(groups, rows_of_scale.partition_broadcast(P)))
                for n in range(2, K_PARTS):
                    load_k(n)
                for n in range(V_PARTS):
                    load_v(n)

            @block.tensor
            def _(pe):
                for n in range(K_PARTS):
                    k_loaded[n % 2].wait(pe, n // 2 + 1)
                    for r in range(TILES):
                        tile = TILES * n + r
                        if tile >= BANKS:
                            k_low.wait(pe, tile - BANKS + 1)
                        for dc in range(DC):
                            last = pe.transpose(banks[:, tile % BANKS, dc, :], k_in[n % 2][:, r, dc * P:(dc + 1) * P],
                                                ident[:, :])
                        turned.done(last)

            @block.scalar
            def _(act):
                def split_k(n):
                    for r in range(TILES):
                        turned.wait(act, TILES * n + r + 1)
                        k_high.done(act.activation(k_tile(0, n, r), banks[:, (TILES * n + r) % BANKS, :, :], ACT.Copy))

                def split_v(n):
                    v_loaded[n % 2].wait(act, n // 2 + 1)
                    v_high.done(act.activation(v_tiles(0, n), v_in[n % 2][:, :, :], ACT.Copy))

                for n in range(K_PARTS):
                    split_k(n)
                for n in range(V_PARTS):
                    split_v(n)

            @block.gpsimd
            def _(pool):
                pow_set.done(pool.memset(power[:, :], -0.5))
                pow_set.wait(pool, 1)
                chain.wait(pool, 2 * G + 1)
                root.done(pool.tensor_tensor(rstd[:, :], var[:, :], power[:, :], ALU.pow))
                for n in range(1, V_PARTS, 2):
                    low_v(pool, n)

            @block.vector
            def _(dve):
                def low_k(n):
                    for r in range(TILES):
                        k_high.wait(dve, TILES * n + r + 1)
                        k_low.done(dve.tensor_tensor(k_tile(1, n, r), banks[:, (TILES * n + r) % BANKS, :, :],
                                                     words(k_tile(0, n, r)), ALU.subtract))

                low_k(0)
                low_k(1)
                s_loaded.wait(dve, 1)
                for g in range(G):
                    chain.done(dve.bn_stats(stats[:, g, :], groups[:, g, :]))
                chain.wait(dve, G)
                for g in range(G):
                    chain.done(dve.bn_aggr(mean_var[:, g, :], stats[:, g, :]))
                chain.wait(dve, 2 * G)
                chain.done(dve.tensor_scalar_add(var[:, :], mean_var[:, :, 1], EPS))
                for n in range(2, K_PARTS):
                    low_k(n)
                low_v(dve, 0)
                root.wait(dve, 1)
                for g in range(G):
                    chain.done(dve.tensor_scalar(groups[:, g, :], groups[:, g, :], mean_var[:, g, 0:1],
                                                 rstd[:, g:g + 1], ALU.subtract, ALU.mult))
                    if g == G // 2:
                        low_v(dve, 2)


def self_attention_loop(nc, ident, x, x1, kT, vs, scale, NB, KB, tiles):
    x_t, x1_t = tokens(x.rearrange("b s n -> (b s) n")), tokens(x1)
    with ExitStack() as ctx:
        sb, ps, step = allocator(ctx, nc, "sal")
        x_norm, x_add = sb("x_norm", [P, D]), sb("x_add", [P, D])
        normed = sb("normed", [P, D])
        nT = [sb(f"nT_{part}", [P, DC, P], F32R) for part in ("high", "low")]
        scaled, prob = sb("scaled", [P, NB, BANK]), sb("prob", [P, NB, BANK])
        pT = [sb(f"pT_{part}", [P, T1C, P], F32R) for part in ("high", "low")]
        out = sb("out", [P, D])
        stats, mean_var, var, rstd, power = sb("stats", [P, 6]), sb("mean_var", [P, 2]), sb("var", [P, 1]), sb("rstd", [P, 1]), sb("power", [P, 1])
        neg_max, total, inv_total = sb("neg_max", [P, 1]), sb("total", [P, 1]), sb("inv_total", [P, 1])
        scores = ps("scores", [P, NB, BANK])
        nT_ps = ps("nT_ps", [P, DC, P])
        pT_ps = [ps(f"pT_ps{i}", [P, KB, P]) for i in range(2)]
        o_ps = ps("o_ps", [P, D])

        norm_in = step("norm_in", size=16)
        add_in = step("add_in", size=16)
        stored = step("stored", size=16, ahead=1)
        constant = step("constant")
        stat = step("stat")
        root = step("root", ahead=1)
        normal = step("normal", ahead=1)
        turned = step("turned", ahead=1)
        nT_high, nT_low = step("nT_high"), step("nT_low")
        scored = step("scored")
        scaled_to = step("scaled_to", ahead=NB)
        peak = step("peak", ahead=1)
        exped = step("exped", ahead=1)
        p_turned = step("p_turned", ahead=NB)
        pT_high, pT_low = step("pT_high"), step("pT_low", ahead=2)
        weighed = step("weighed", ahead=1)
        inverse = step("inverse")
        summed = step("summed", ahead=1)

        with nc.Block() as block:
            @block.sync
            def _(sp):
                def load_norm(t):
                    normal.wait(sp, t)
                    norm_in.done(sp.dma_start(x_norm[:, :], one(x_t, t)))

                def load_add(t):
                    summed.wait(sp, t)
                    add_in.done(sp.dma_start(x_add[:, :], one(x_t, t)))

                def store(t):
                    summed.wait(sp, t + 1)
                    stored.done(sp.dma_start(one(x1_t, t), out[:, :]))

                stored.open(sp)
                load_norm(0)
                load_norm(1)
                with sp.Fori(0, tiles - 2) as t:
                    load_norm(t + 2)
                    load_add(t)
                    store(t)
                for t in (tiles - 2, tiles - 1):
                    load_add(t)
                    store(t)
                stored.wait(sp, tiles)

            @block.gpsimd
            def _(pool):
                root.open(pool)
                constant.done(pool.memset(power[:, :], -0.5))
                constant.wait(pool, 1)
                with pool.Fori(0, tiles) as t:
                    stat.wait(pool, t + 1)
                    root.done(pool.tensor_tensor(rstd[:, :], var[:, :], power[:, :], ALU.pow))

            @block.tensor
            def _(pe):
                def turn(t):
                    normal.wait(pe, t + 1)
                    nT_low.wait(pe, t)
                    for dc in range(DC):
                        last = pe.transpose(nT_ps[:, dc, :], normed[:, dc * P:(dc + 1) * P], ident[:, :])
                    turned.done(last)

                def score(t, j):
                    if j == 0:
                        nT_low.wait(pe, t + 1)
                    scaled_to.wait(pe, NB * (t - 1) + j + 1)
                    for dc in range(DC):
                        last = matmul3(pe, scores[:, j, :], [n[:, dc, :] for n in nT],
                                       [kt[:, dc, j * BANK:(j + 1) * BANK] for kt in kT], dc == 0, dc == DC - 1)
                    scored.done(last)

                def turn_p(t, j):
                    if j == 0:
                        exped.wait(pe, t + 1)
                    pT_low.wait(pe, NB * t + j - 1)
                    for n in range(KB):
                        last = pe.transpose(pT_ps[j % 2][:, n, :], prob[:, j, n * P:(n + 1) * P], ident[:, :])
                    p_turned.done(last)

                def weigh(t, j):
                    if j == 0:
                        summed.wait(pe, t)
                    pT_low.wait(pe, NB * t + j + 1)
                    for n in range(j * KB, (j + 1) * KB):
                        last = matmul3(pe, o_ps[:, :], [p[:, n, :] for p in pT], [w[:, n, :] for w in vs],
                                       n == 0, n == T1C - 1)
                    if j == NB - 1:
                        weighed.done(last)

                def tile(t, ahead):
                    if ahead >= 1:
                        for j in range(NB - 1):
                            score(t + 1, j)
                    turn_p(t, 0)
                    turn_p(t, 1)
                    if ahead >= 1:
                        score(t + 1, NB - 1)
                    if ahead >= 2:
                        turn(t + 2)
                    for j in range(NB):
                        weigh(t, j)
                        if j + 2 < NB:
                            turn_p(t, j + 2)

                turned.open(pe)
                p_turned.open(pe)
                weighed.open(pe)
                turn(0)
                for j in range(NB):
                    score(0, j)
                turn(1)
                with pe.Fori(0, tiles - 2) as t:
                    tile(t, 2)
                tile(tiles - 2, 1)
                tile(tiles - 1, 0)

            @block.scalar
            def _(act):
                def high_n(t):
                    turned.wait(act, t + 1)
                    nT_high.done(act.activation(nT[0][:, :, :], nT_ps[:, :, :], ACT.Copy))

                def exp(t):
                    p_turned.wait(act, NB * t)
                    peak.wait(act, t + 1)
                    exped.done(act.activation(prob[:, :, :], scaled[:, :, :], ACT.Exp, bias=neg_max[:, 0:1],
                                              accum_out=total[:, 0:1]))

                def high_p(t, j):
                    if j == 0:
                        weighed.wait(act, t)
                    p_turned.wait(act, NB * t + j + 1)
                    pT_high.done(act.activation(pT[0][:, j * KB:(j + 1) * KB, :], pT_ps[j % 2][:, :, :], ACT.Copy))

                def tile(t, ahead):
                    high_p(t, 0)
                    high_p(t, 1)
                    if ahead >= 2:
                        high_n(t + 2)
                    high_p(t, 2)
                    high_p(t, 3)
                    if ahead >= 1:
                        exp(t + 1)

                exped.open(act)
                high_n(0)
                high_n(1)
                exp(0)
                with act.Fori(0, tiles - 2) as t:
                    tile(t, 2)
                tile(tiles - 2, 1)
                tile(tiles - 1, 0)

            @block.vector
            def _(dve):
                def normalize(t):
                    norm_in.wait(dve, t + 1)
                    root.wait(dve, t)
                    dve.bn_stats(stats[:, :], x_norm[:, :])
                    dve.drain()
                    dve.bn_aggr(mean_var[:, :], stats[:, :])
                    dve.drain()
                    stat.done(dve.tensor_scalar_add(var[:, :], mean_var[:, 1:2], EPS))
                    turned.wait(dve, t)
                    root.wait(dve, t + 1)
                    normal.done(dve.tensor_scalar(normed[:, :], x_norm[:, :], mean_var[:, 0:1], rstd[:, 0:1],
                                                  ALU.subtract, ALU.mult))

                def low_n(t):
                    nT_high.wait(dve, t + 1)
                    nT_low.done(dve.tensor_tensor(nT[1][:, :, :], nT_ps[:, :, :], words(nT[0][:, :, :]), ALU.subtract))

                def scale_block(t, j):
                    if j == 0:
                        exped.wait(dve, t)
                    scored.wait(dve, NB * t + j + 1)
                    batch = scale[:, ds(t // (S // P), 1), j, :].squeeze(1)
                    scaled_to.done(dve.tensor_tensor(scaled[:, j, :], scores[:, j, :], batch, ALU.mult))

                def row_max(t):
                    scaled_to.wait(dve, NB * (t + 1))
                    peak.done(dve.tensor_reduce(neg_max[:, 0:1], scaled[:, :, :], AX.XY, ALU.max, negate=True))

                def low_p(t, j):
                    pT_high.wait(dve, NB * t + j + 1)
                    pT_low.done(dve.tensor_tensor(pT[1][:, j * KB:(j + 1) * KB, :], pT_ps[j % 2][:, :, :],
                                                  words(pT[0][:, j * KB:(j + 1) * KB, :]), ALU.subtract))

                def invert(t):
                    summed.wait(dve, t)
                    exped.wait(dve, t + 1)
                    inverse.done(dve.reciprocal(inv_total[:, :], total[:, :]))

                def add(t):
                    weighed.wait(dve, t + 1)
                    inverse.wait(dve, t + 1)
                    add_in.wait(dve, t + 1)
                    stored.wait(dve, t)
                    summed.done(dve.scalar_tensor_tensor(out[:, :], o_ps[:, :], inv_total[:, 0:1], x_add[:, :],
                                                         ALU.mult, ALU.add))

                def tile(t, ahead):
                    invert(t)
                    if ahead >= 2:
                        normalize(t + 2)
                    if ahead >= 1:
                        for j in range(NB - 1):
                            scale_block(t + 1, j)
                    low_p(t, 0)
                    low_p(t, 1)
                    if ahead >= 1:
                        scale_block(t + 1, NB - 1)
                        row_max(t + 1)
                    if ahead >= 2:
                        low_n(t + 2)
                    low_p(t, 2)
                    low_p(t, 3)
                    add(t)

                for s in (normal, scaled_to, peak, pT_low, summed):
                    s.open(dve)
                normalize(0)
                low_n(0)
                normalize(1)
                for j in range(NB):
                    scale_block(0, j)
                row_max(0)
                low_n(1)
                with dve.Fori(0, tiles - 2) as t:
                    tile(t, 2)
                tile(tiles - 2, 1)
                tile(tiles - 1, 0)


BLOCKS = 4
FULL = 3
TILES = [FULL] * (BLOCKS - 1) + [FULL + 1]
TILES_B = sum(TILES)
KEYS = [FULL * P] * (BLOCKS - 1) + [S2 - (BLOCKS - 1) * FULL * P]


MASKED = -1e9
QT = S // P
KT = (S2 + P - 1) // P
LAST = S2 - (KT - 1) * P
assert TILES_B == KT


class MaskPreparation:

    ROUNDS = [(0, 8), (8, KT)]

    def __init__(self, sb, ps, step, ident_b, mask, mask_q, mask_t, any_key):
        self.rows = mask[0, 0].rearrange("(t p) n -> t p n", p=P)
        self.ident_b, self.mask_q, self.mask_t, self.any_key = ident_b, mask_q, mask_t, any_key
        self.raw, self.zero, self.tile = sb("mk_raw", [P, S2], I32), sb("mk_zero", [P, S2], BF16), sb("mk_tile", [P, S2], BF16)
        self.none, self.some, self.weight = sb("mk_none", [P, 1]), sb("mk_some", [P, 1]), sb("mk_weight", [P, 1])
        self.some_b = sb("mk_some_b", [P, P], BF16)
        self.turned_ps, self.some_ps = ps("mk_turned_ps", [P, 8, P], BF16), ps("mk_some_ps", [P, BANK])
        self.raw_in, self.zeroed = step("mk_raw_in", size=16), step("mk_zeroed", ahead=1)
        self.weighted, self.turned = step("mk_weighted"), step("mk_turned", ahead=2)
        self.copied, self.kept = step("mk_copied", ahead=2), step("mk_kept", ahead=1)

    def load(self, sp, t):
        source = one(self.rows, t)
        self.zeroed.wait(sp, t)
        self.raw_in.done(sp.dma_start(self.raw[:, :], source))

    def vector(self, dve, t):
        self.raw_in.wait(dve, t + 1)
        self.zeroed.done(dve.tensor_scalar(self.zero[:, :], self.raw[:, :], 0.0, None, ALU.is_equal))
        self.zeroed.wait(dve, t + 1)
        dve.tensor_reduce(self.none[:, :], self.zero[:, :], AX.X, ALU.min)
        dve.drain()
        dve.tensor_scalar(self.some[:, :], self.none[:, :], -1.0, 1.0, ALU.mult, ALU.add)
        dve.tensor_scalar(self.weight[:, :], self.none[:, :], -MASKED, MASKED, ALU.mult, ALU.add)
        dve.drain()
        self.turned.wait(dve, 2 * t)
        dve.tensor_copy(self.some_b[:, :], self.some[:, :].broadcast_to([P, P]))
        dve.drain()
        self.kept.wait(dve, t)
        self.weighted.done(dve.tensor_scalar(self.tile[:, :], self.zero[:, :], self.weight[:, 0:1], None, ALU.mult))

    def transposes(self, pe, t, part):
        self.weighted.wait(pe, t + 1)
        self.copied.wait(pe, 2 * t + part)
        if part == 0:
            pe.matmul(self.some_ps[:, 0:P], self.some_b[:, :], self.ident_b[:, :], start=True, stop=True)
        first, end = self.ROUNDS[part]
        for n in range(first, end):
            keys = min(P, S2 - n * P)
            last = pe.transpose(self.turned_ps[0:keys, n - first, :], self.tile[:, n * P:n * P + keys], self.ident_b[:, :])
        self.turned.done(last)

    def copies(self, act, t, part):
        self.turned.wait(act, 2 * t + part + 1)
        here = ds(t * P, P)
        first, end = self.ROUNDS[part]
        whole = min(end, KT - 1)
        if part == 0:
            act.activation(self.any_key[:, here], self.some_ps[:, 0:P], ACT.Copy)
            self.kept.done(act.activation(self.mask_q[:, ds(t, 1), :].squeeze(1), self.tile[:, :], ACT.Copy))
        else:
            act.activation(self.mask_t[0:LAST, KT - 1, here], self.turned_ps[0:LAST, KT - 1 - first, :], ACT.Copy)
        act.drain()
        self.copied.done(act.activation(self.mask_t[:, first:whole, here], self.turned_ps[:, 0:whole - first, :], ACT.Copy))


def split_weights(nc, ident, tag, weights, outs):
    with ExitStack() as ctx:
        sb, ps, step = allocator(ctx, nc, tag)
        rows = sb("rows", [P, len(weights), DC, D])
        banks = ps("banks", [P, len(weights) * DC, DC, P])
        loaded, turned, high_done, low_done = step("loaded", size=16), step("turned"), step("high"), step("low")
        cases = [(w, r) for w in range(len(weights)) for r in range(DC)]
        with nc.Block() as block:
            @block.sync
            def _(sp):
                for w, weight in enumerate(weights):
                    loaded.done(sp.dma_start(rows[:, w, :, :], weight.rearrange("(r p) n -> p r n", p=P)))

            @block.tensor
            def _(pe):
                loaded.wait(pe, len(weights))
                for n, (w, r) in enumerate(cases):
                    for dc in range(DC):
                        last = pe.transpose(banks[:, n, dc, :], rows[:, w, r, dc * P:(dc + 1) * P], ident[:, :])
                    turned.done(last)

            @block.scalar
            def _(act):
                for n, (w, r) in enumerate(cases):
                    turned.wait(act, n + 1)
                    high_done.done(act.activation(outs[w][0][:, :, r * P:(r + 1) * P], banks[:, n, :, :], ACT.Copy))

            @block.vector
            def _(dve):
                for n, (w, r) in enumerate(cases):
                    high_done.wait(dve, n + 1)
                    low_done.done(dve.tensor_tensor(outs[w][1][:, :, r * P:(r + 1) * P], banks[:, n, :, :],
                                                    words(outs[w][0][:, :, r * P:(r + 1) * P]), ALU.subtract))


def context_keys_values(nc, ident, ident_b, context, Wk, bk, Wv, bv, mask, masks, kT_out, v_out):
    steps = B * BLOCKS
    with ExitStack() as keep:
        sb, _, _ = allocator(keep, nc, "cx")
        wk = [sb(f"wk_{part}", [P, DC, D], F32R) for part in ("high", "low")]
        wv = [sb(f"wv_{part}", [P, DC, D], F32R) for part in ("high", "low")]
        split_weights(nc, ident, "cxw", [Wk, Wv], [wk, wv])
        with ExitStack() as ctx:
            sb, ps, step = allocator(ctx, nc, "cxl")
            k_bias, v_bias = sb("k_bias", [P, DC]), sb("v_bias", [P, D])
            rows = sb("rows", [P, 2, 4, D])
            WIDE = max(KEYS) + 1
            cT = [[sb(f"cT_{part}{i}", [P, DC, WIDE], F32R) for part in ("high", "low")] for i in range(2)]
            kT = [sb(f"kT_{part}", [P, DC, max(KEYS)], F32R) for part in ("high", "low")]
            v_sb = sb("v", [P, 4, D])
            banks = ps("banks", [P, 2, BANK])
            outs = ps("outs", [P, 4, BANK])

            bias_in = step("bias_in", size=16)
            rows_in = [step(f"rows_in{i}", size=16) for i in range(2)]
            turned = step("turned", ahead=TILES_B)
            cT_high, cT_low = step("cT_high"), step("cT_low", ahead=2)
            k_made, k_high, k_low = step("k_made", ahead=4), step("k_high"), step("k_low")
            v_made, v_done = step("v_made", ahead=TILES_B), step("v_done", ahead=TILES_B)
            k_stored, v_stored = step("k_stored", size=16, ahead=2), step("v_stored", size=16, ahead=1)

            padded, carried = step("padded"), step("carried")
            preparation = MaskPreparation(sb, ps, step, ident_b, mask, *masks)

            def even(q):
                return KEYS[q] + KEYS[q] % 2

            def size(q, r):
                return P if r < FULL else LAST

            def span(q):
                return slice(q * FULL * P, q * FULL * P + KEYS[q])

            def before(b, q):
                return TILES_B * b + (FULL * q if q >= 0 else -TILES[q])

            def row_parts(dram, b, q, tile):
                first = q * FULL * P
                yield one(dram, b)[first:first + FULL * P, :].rearrange("(r p) n -> p r n", p=P), tile[:, 0:FULL, :]
                if q == BLOCKS - 1:
                    yield one(dram, b)[S2 - LAST:S2, :], tile[0:LAST, FULL, :]

            def group_parts(b, q):
                first = q * FULL * P
                for r in range(TILES[q]):
                    yield (one(v_out, b)[:, first + r * P:first + r * P + size(q, r), :].rearrange("g p n -> p g n"),
                           v_sb[0:size(q, r), r, :].rearrange("p (g n) -> p g n", n=P))

            def loops(eng, body):
                def batch(b, last):
                    for q in range(BLOCKS):
                        def following(n):
                            return (b, q + n) if q + n < BLOCKS else None if last else (b + 1, q + n - BLOCKS)

                        body(b, q, following)

                with eng.Fori(0, B - 1) as b:
                    batch(b, False)
                batch(B - 1, True)

            with nc.Block() as block:
                @block.sync
                def _(sp):
                    bias_in.done(sp.dma_start(k_bias[:, :], bk.rearrange("(c p) -> p c", p=P),
                                              allow_slow_non_contiguous=True))
                    bias_in.done(sp.dma_start(v_bias[:, :], bv.partition_broadcast(P)))

                    def load(b, q):
                        parts = list(row_parts(context, b, q, rows[:, q % 2, :, :]))
                        turned.wait(sp, before(b, q - 1))
                        for src, dst in parts:
                            rows_in[q % 2].done(sp.dma_start(dst, src))

                    def store(b, q):
                        s = BLOCKS * b + q
                        places = [one(out, b)[:, span(q)].rearrange("(c p) n -> p c n", p=P) for out in kT_out]
                        parts = list(group_parts(b, q))
                        k_low.wait(sp, 4 * (s + 1))
                        sp.sem_inc(carried.sem, 1)
                        for part, dst in enumerate(places):
                            k_stored.done(sp.dma_start(dst, words(kT[part][:, :, 0:KEYS[q]])))
                        v_done.wait(sp, before(b, q) + TILES[q])
                        for dst, src in parts:
                            v_stored.done(sp.dma_start(dst, src))

                    k_stored.open(sp)
                    v_stored.open(sp)
                    load(0, 0)
                    load(0, 1)

                    def body(b, q, following):
                        if following(2):
                            load(*following(2))
                        if q % 2 == 0:
                            preparation.load(sp, 2 * b + q // 2)
                        store(b, q)

                    loops(sp, body)
                    k_stored.wait(sp, 2 * steps)
                    v_stored.wait(sp, TILES_B * B)

                def rows_arrived(b, q):
                    return (2 + q % 2) * b + q // 2 + 1 + (q == BLOCKS - 1)

                @block.gpsimd
                def _(pool):
                    for n, part in enumerate(cT[(BLOCKS - 1) % 2]):
                        padded.done(pool.memset(words(part[:, :, WIDE - 1:WIDE]), 0.0))
                        padded.wait(pool, n + 1)

                @block.tensor
                def _(pe):
                    def turn(b, q, r):
                        if r == 0:
                            rows_in[q % 2].wait(pe, rows_arrived(b, q))
                        cT_low.wait(pe, before(b, q) + max(r - 1, 0))
                        n = size(q, r)
                        for dc in range(DC):
                            last = pe.transpose(banks[:, r % 2, dc * n:(dc + 1) * n],
                                                rows[0:n, q % 2, r, dc * P:(dc + 1) * P], ident[0:n, 0:n])
                        turned.done(last)

                    def keys(b, q, following):
                        s = BLOCKS * b + q
                        for hd in range(DC):
                            if following and hd < TILES[following[1]]:
                                turn(*following, hd)
                            v_done.wait(pe, before(b, q) - max(TILES[q - 1] - 1 - hd, 0))
                            for dc in range(DC):
                                last = matmul3(pe, outs[:, hd, 0:even(q)], [w[:, dc, hd * P:(hd + 1) * P] for w in wk],
                                               [c[:, dc, 0:even(q)] for c in cT[q % 2]], dc == 0, dc == DC - 1)
                            k_made.done(last)

                    def values(b, q):
                        s = BLOCKS * b + q
                        for r in range(TILES[q]):
                            n, first = size(q, r), r * P
                            k_low.wait(pe, 4 * s + r + 1)
                            for dc in range(DC):
                                last = matmul3(pe, outs[0:n, r, :], [c[:, dc, first:first + n] for c in cT[q % 2]],
                                               [w[:, dc, :] for w in wv], dc == 0, dc == DC - 1)
                            v_made.done(last)

                    padded.wait(pe, 2)
                    turned.open(pe)
                    k_made.open(pe)
                    v_made.open(pe)
                    preparation.turned.open(pe)
                    for r in range(TILES[0]):
                        turn(0, 0, r)

                    def body(b, q, following):
                        cT_low.wait(pe, before(b, q) + TILES[q])
                        keys(b, q, following(1))
                        if q % 2 == 1:
                            preparation.transposes(pe, 2 * b + q // 2, 0)
                        values(b, q)
                        if q % 2 == 1:
                            preparation.transposes(pe, 2 * b + q // 2, 1)

                    loops(pe, body)

                @block.scalar
                def _(act):
                    def high_c(b, q, r):
                        v_made.wait(act, before(b, q - 1))
                        n, first = size(q, r), r * P
                        turned.wait(act, before(b, q) + r + 1)
                        cT_high.done(act.activation(
                            cT[q % 2][0][:, :, first:first + n],
                            banks[:, r % 2, 0:DC * n].rearrange("p (c n) -> p c n", c=DC), ACT.Copy))

                    def high_k(b, q, following):
                        s = BLOCKS * b + q
                        for hd in range(DC):
                            if following and hd < TILES[following[1]]:
                                high_c(*following, hd)
                            k_stored.wait(act, 2 * s)
                            k_made.wait(act, 4 * s + hd + 1)
                            k_high.done(act.activation(kT[0][:, hd, 0:KEYS[q]], outs[:, hd, 0:KEYS[q]], ACT.Identity,
                                                       bias=k_bias[:, hd:hd + 1]))

                    bias_in.wait(act, 2)
                    preparation.copied.open(act)
                    preparation.kept.open(act)
                    for r in range(TILES[0]):
                        high_c(0, 0, r)

                    def body(b, q, following):
                        high_k(b, q, following(1))
                        if q % 2 == 1:
                            for part in range(2):
                                preparation.copies(act, 2 * b + q // 2, part)

                    loops(act, body)

                @block.vector
                def _(dve):
                    def low_c(b, q, r):
                        n, first = size(q, r), r * P
                        cT_high.wait(dve, before(b, q) + r + 1)
                        cT_low.done(dve.tensor_tensor(
                            cT[q % 2][1][:, :, first:first + n],
                            banks[:, r % 2, 0:DC * n].rearrange("p (c n) -> p c n", c=DC),
                            words(cT[q % 2][0][:, :, first:first + n]), ALU.subtract))

                    def low_k(b, q, following):
                        s = BLOCKS * b + q
                        for hd in range(DC):
                            if following and hd < TILES[following[1]]:
                                low_c(*following, hd)
                            k_high.wait(dve, 4 * s + hd + 1)
                            k_low.done(dve.scalar_tensor_tensor(
                                kT[1][:, hd, 0:KEYS[q]], outs[:, hd, 0:KEYS[q]], k_bias[:, hd:hd + 1],
                                words(kT[0][:, hd, 0:KEYS[q]]), ALU.add, ALU.subtract))

                    def finish_v(b, q):
                        v_stored.wait(dve, before(b, q))
                        for r in range(TILES[q]):
                            n = size(q, r)
                            v_made.wait(dve, before(b, q) + r + 1)
                            v_done.done(dve.tensor_tensor(v_sb[0:n, r, :], outs[0:n, r, :], v_bias[0:n, :], ALU.add))

                    bias_in.wait(dve, 2)
                    cT_low.open(dve)
                    v_done.open(dve)
                    preparation.zeroed.open(dve)
                    for r in range(TILES[0]):
                        low_c(0, 0, r)

                    def body(b, q, following):
                        low_k(b, q, following(1))
                        finish_v(b, q)
                        if q % 2 == 0:
                            preparation.vector(dve, 2 * b + q // 2)

                    loops(dve, body)


class LayerNorm:

    def __init__(self, sb, step, R):
        self.R = R
        self.stats, self.mean_var = sb("ln_stats", [P, R, 6]), sb("ln_mean_var", [P, R, 2])
        self.var, self.rstd, self.power = sb("ln_var", [P, R]), sb("ln_rstd", [P, R]), sb("ln_power", [P, R])
        self.constant, self.stat, self.root = step("ln_constant"), step("ln_stat"), step("ln_root", ahead=1)

    def pool_setup(self, pool):
        self.root.open(pool)
        self.constant.done(pool.memset(self.power[:, :], -0.5))
        self.constant.wait(pool, 1)

    def pool_step(self, pool, s):
        self.stat.wait(pool, s + 1)
        self.root.done(pool.tensor_tensor(self.rstd[:, :], self.var[:, :], self.power[:, :], ALU.pow))

    def statistics(self, dve, rows, s):
        self.root.wait(dve, s)
        for r in range(self.R):
            dve.bn_stats(self.stats[:, r, :], rows[:, r, :])
        dve.drain()
        for r in range(self.R):
            dve.bn_aggr(self.mean_var[:, r, :], self.stats[:, r, :])
        dve.drain()
        self.stat.done(dve.tensor_scalar_add(self.var[:, :], self.mean_var[:, :, 1], EPS))

    def normalize(self, dve, out, rows, s):
        self.root.wait(dve, s + 1)
        for r in range(self.R):
            last = dve.tensor_scalar(out[:, r, :], rows[:, r, :], self.mean_var[:, r, 0:1], self.rstd[:, r:r + 1],
                                     ALU.subtract, ALU.mult)
        return last


def project_queries(nc, ident, x1, Wq, bq, any_key, qT_out):
    steps = TOK // BANK
    R = BANK // P
    x_rows = x1.rearrange("(s r p) n -> s p r n", p=P, r=R)
    with ExitStack() as keep:
        sb, _, _ = allocator(keep, nc, "pq")
        wq = [sb(f"wq_{part}", [P, DC, D], F32R) for part in ("high", "low")]
        split_weights(nc, ident, "pqw", [Wq], [wq])
        with ExitStack() as ctx:
            sb, ps, step = allocator(ctx, nc, "pql")
            q_bias = sb("q_bias", [P, DC])
            rows = [sb(f"rows{i}", [P, R, D]) for i in range(2)]
            normed = sb("normed", [P, R, D])
            norm = LayerNorm(sb, step, R)
            nT = [[sb(f"nT_{part}{i}", [P, DC, BANK], F32R) for part in ("high", "low")] for i in range(2)]
            q = sb("q", [P, DC, BANK])
            qT = [[sb(f"qT_{part}{i}", [P, DC, BANK], F32R) for part in ("high", "low")] for i in range(2)]
            banks, outs = ps("banks", [P, R, DC, P]), ps("outs", [P, DC, BANK])
            bias_in, rows_in = step("bias_in", size=16), [step(f"rows_in{half}", size=16) for half in range(2)]
            normal = step("normal", ahead=2)
            turned = step("turned", ahead=R)
            high_n, low_n = step("high_n"), step("low_n", ahead=R)
            made = step("made", ahead=2 * DC)
            q_done = step("q_done", ahead=DC)
            high_q, low_q, carried = step("high_q"), step("low_q", ahead=DC), step("carried")
            stored = [step(f"stored{half}", size=16, ahead=2) for half in range(2)]

            def loops(eng, body):
                with eng.Fori(0, B - 1) as b:
                    for half in range(2):
                        body(b, half, 2)
                for half in range(2):
                    body(B - 1, half, 1 - half)

            with nc.Block() as block:
                @block.sync
                def _(sp):
                    bias_in.done(sp.dma_start(q_bias[:, :], bq.rearrange("(c p) -> p c", p=P),
                                              allow_slow_non_contiguous=True))

                    def load(s, half):
                        source = one(x_rows, s)
                        normal.wait(sp, s - 1)
                        rows_in[half].done(sp.dma_start(rows[half][:, :, :], source))

                    def body(b, half, more):
                        if more:
                            load(2 * b + half + 3, 1 - half)
                        places = [one(out, b).rearrange("(c p) n -> p c n", p=P)[:, :, half * BANK:(half + 1) * BANK]
                                  for out in qT_out]
                        low_q.wait(sp, DC * (2 * b + half + 1))
                        sp.sem_inc(carried.sem, 1)
                        for part, dst in enumerate(places):
                            stored[half].done(sp.dma_start(dst, words(qT[half][part][:, :, :])))

                    for st in stored:
                        st.open(sp)
                    load(0, 0)
                    load(1, 1)
                    load(2, 0)
                    with sp.Fori(0, B - 2) as b:
                        for half in range(2):
                            body(b, half, True)
                    for s in range(steps - 4, steps):
                        body(s // 2, s % 2, s + 3 < steps)
                    for st in stored:
                        st.wait(sp, 2 * B)

                @block.gpsimd
                def _(pool):
                    norm.pool_setup(pool)
                    with pool.Fori(0, steps) as s:
                        norm.pool_step(pool, s)

                @block.tensor
                def _(pe):
                    def turn(s, r):
                        normal.wait(pe, s + 1)
                        low_n.wait(pe, R * (s - 1) + r + 1)
                        for dc in range(DC):
                            last = pe.transpose(banks[:, r, dc, :], normed[:, r, dc * P:(dc + 1) * P], ident[:, :])
                        turned.done(last)

                    def body(b, half, more):
                        s = 2 * b + half
                        low_n.wait(pe, R * (s + 1))
                        for hd in range(DC):
                            if more:
                                turn(s + 1, hd)
                            q_done.wait(pe, DC * (s - 1) + hd + 1)
                            for dc in range(DC):
                                last = matmul3(pe, outs[:, hd, :], [w[:, dc, hd * P:(hd + 1) * P] for w in wq],
                                               [n[:, dc, :] for n in nT[half]], dc == 0, dc == DC - 1)
                            made.done(last)

                    turned.open(pe)
                    made.open(pe)
                    for r in range(R):
                        turn(0, r)
                    loops(pe, body)

                @block.scalar
                def _(act):
                    def high(s, half, r):
                        made.wait(act, DC * (s - 1))
                        turned.wait(act, R * s + r + 1)
                        high_n.done(act.activation(nT[half][0][:, :, r * P:(r + 1) * P], banks[:, r, :, :], ACT.Copy))

                    def body(b, half, more):
                        s = 2 * b + half
                        stored[half].wait(act, 2 * b)
                        for hd in range(DC):
                            if more:
                                high(s + 1, 1 - half, hd)
                            q_done.wait(act, DC * s + hd + 1)
                            high_q.done(act.activation(qT[half][0][:, hd, :], q[:, hd, :], ACT.Copy))

                    for r in range(R):
                        high(0, 0, r)
                    loops(act, body)

                @block.vector
                def _(dve):
                    def statistics(b, half):
                        rows_in[half].wait(dve, b + 1)
                        norm.statistics(dve, rows[half], 2 * b + half)

                    def normalize(b, half):
                        s = 2 * b + half
                        turned.wait(dve, R * s)
                        normal.done(norm.normalize(dve, normed, rows[half], s))

                    def low(s, half, r):
                        high_n.wait(dve, R * s + r + 1)
                        low_n.done(dve.tensor_tensor(nT[half][1][:, :, r * P:(r + 1) * P], banks[:, r, :, :],
                                                     words(nT[half][0][:, :, r * P:(r + 1) * P]), ALU.subtract))

                    def split_q(s, half, hd):
                        high_q.wait(dve, DC * s + hd + 1)
                        low_q.done(dve.tensor_tensor(qT[half][1][:, hd, :], q[:, hd, :],
                                                     words(qT[half][0][:, hd, :]), ALU.subtract))

                    def body(b, half, more):
                        s = 2 * b + half
                        stored[half].wait(dve, 2 * b)
                        for hd in range(DC):
                            if more:
                                low(s + 1, 1 - half, hd)
                            if hd == 1 and more == 2:
                                statistics(b + 1, half)
                            if hd == 3 and more == 2:
                                normalize(b + 1, half)
                            made.wait(dve, DC * s + hd + 1)
                            low_q.wait(dve, DC * (s - 1) + hd + 1)
                            q_done.done(dve.scalar_tensor_tensor(
                                q[:, hd, :], outs[:, hd, :], q_bias[:, hd:hd + 1],
                                any_key[:, half * BANK:(half + 1) * BANK], ALU.add, ALU.mult))
                            if hd > 0:
                                split_q(s, half, hd - 1)
                        split_q(s, half, DC - 1)

                    for s in (normal, low_n, q_done, low_q):
                        s.open(dve)
                    bias_in.wait(dve, 1)
                    statistics(0, 0)
                    normalize(0, 0)
                    for r in range(R):
                        low(0, 0, r)
                    statistics(0, 1)
                    normalize(0, 1)
                    loops(dve, body)


GROUPS = D // P
GH = H // GROUPS
PAIRS = GH // 2


def cross_attention(nc, ident, ident_b, kT, qT, v, mask_q, mask_t, row, oT):
    HALF = S // BANK
    units = B * GROUPS * HALF
    QB = BANK // P
    MB, MKEYS = 4, 402
    MFIRST = [0, 400, 800, S2 - MKEYS]
    SLOTS = GH * QB * MB
    SLOTS_OF = [2, 7, 8, 8, 8, 8, 8, 8, 7] + [0] * (KT - 9)
    SLOT_OF = [sum(SLOTS_OF[:n]) for n in range(KT + 1)]
    assert SLOT_OF[KT] == SLOTS
    TURN = 9
    OWN = {"pool": tuple(range(9)), "dve": (9, 10, 11)}
    POOL_ADDS, DVE_ADDS = len(OWN["pool"]) - 1, len(OWN["dve"])
    RING = 4
    LOADS = 8
    SCALE = float(1.0 / np.sqrt(np.float32(DK)))
    MAXROW = 3 * DK
    ROWS97 = MAXROW + 1

    with ExitStack() as ctx:
        sb, ps, step = allocator(ctx, nc, "xa")
        kp = [sb(f"kp{i}", [P, GH, S2], F32R) for i in range(2)]
        qp = [sb(f"qp{i}", [P, GH, S], F32R) for i in range(2)]
        vg = [sb(f"vg{i}", [P, KT, P]) for i in range(2)]
        prob = [[sb(f"prob{i}{pr}", [P, 2, BANK]) for pr in range(PAIRS)] for i in range(RING)]
        sums = [sb(f"sums{pr}", [P, 2, BANK]) for pr in range(PAIRS)]
        ones = sb("ones", [P, DK])
        unread = [sb(f"unread{i}", [P, MKEYS], BF16) for i in range(2)]
        maxima, neg_max = sb("maxima", [P, GH * QB, MB]), sb("neg_max", [P, GH * QB])
        max_row = sb("max_row", [GH * QB, P], F32R)
        o_sb, sum_sb = [[sb(f"{name}{i}", [P, BANK]) for i in range(2)] for name in ("o_sb", "sum_sb")]
        out = sb("out", [P, BANK])
        scores = [ps(f"scores{pr}", [P, 2, BANK]) for pr in range(PAIRS)]
        o_ps = ps("o_ps", [P, BANK])
        mx_ps = [ps(f"mx_ps{i}", [P, BANK]) for i in range(3)]
        peak_ps, sum_ps = mx_ps[0], mx_ps[1]

        loaded = step("loaded", size=16)
        const = step("const")
        mx_made, mx_read = step("mx_made"), step("mx_read", ahead=3)
        carried = step("carried")
        peaks = step("peaks", ahead=1)
        row_made = step("row_made")
        row_kept = step("row_kept", ahead=1)
        row_out, row_in = step("row_out", size=16, ahead=1), step("row_in", size=16)
        scored, exped = step("scored"), step("exped", ahead=PAIRS)
        weighed = step("weighed", ahead=RING)
        pool_added = step("pool_added", ahead=PAIRS * POOL_ADDS)
        dve_added = step("dve_added", ahead=PAIRS * DVE_ADDS)
        total_made = step("total_made", ahead=1)
        o_kept, sum_kept = step("o_kept", ahead=1), step("sum_kept", ahead=1)
        inverted, finished = step("inverted", ahead=1), step("finished", ahead=1)
        stored = step("stored", size=16, ahead=1)

        def keys_of(kt):
            return LAST if kt == KT - 1 else P

        def wait_added(eng, u, kt):
            if kt < 0:
                u, kt = u - 1, kt + KT
            if kt == KT - 1:
                return
            if kt in OWN["dve"]:
                dve_added.wait(eng, PAIRS * (DVE_ADDS * u + OWN["dve"].index(kt) + 1))
            else:
                pool_added.wait(eng, PAIRS * (POOL_ADDS * u + max(OWN["pool"].index(kt), 1)))

        def loops(eng, unit):
            def four(first, last):
                for n in range(2 * HALF):
                    unit(first + n, n // HALF, n % HALF, (KT * n) % RING, not (last and n == 2 * HALF - 1))

            with eng.Fori(0, units // (2 * HALF) - 1) as it:
                four(it * (2 * HALF), False)
            four(units - 2 * HALF, True)

        def later_loops(eng, unit):
            four = 2 * HALF

            def each(first, n):
                unit(first + n, n // HALF % 2, n % HALF, (KT * n) % RING, True)

            unit(0, 0, 0, 0, True)
            with eng.Fori(0, units // four - 1) as it:
                for n in range(1, four + 1):
                    each(it * four, n)
            for n in range(1, four - 1):
                each(units - four, n)
            unit(units - 1, 1, HALF - 1, KT * (four - 1) % RING, False)

        with nc.Block() as block:
            @block.sync
            def _(sp):
                def load(i, par):
                    for high_or_low, first in ((0, 0), (0, DK), (1, 2 * DK)):
                        loaded.done(sp.dma_start(words(kp[par][first:first + DK, :, :]),
                                                 one(kT[high_or_low], i).rearrange("(j p) n -> p j n", p=DK)))
                    for high_or_low, first in ((0, 0), (1, DK), (0, 2 * DK)):
                        loaded.done(sp.dma_start(words(qp[par][first:first + DK, :, :]),
                                                 one(qT[high_or_low], i).rearrange("(j p) n -> p j n", p=DK)))
                    whole = (KT - 1) * P
                    loaded.done(sp.dma_start(vg[par][:, 0:KT - 1, :],
                                             one(v, i)[0:whole, :].rearrange("(t p) n -> p t n", p=P)))
                    loaded.done(sp.dma_start(vg[par][0:LAST, KT - 1, :], one(v, i)[whole:S2, :]))

                def set_row(u, par, half):
                    row_kept.wait(sp, u + 1)
                    row_out.done(sp.dma_start(row, words(max_row[:, :])))
                    row_out.wait(sp, u + 1)
                    row_in.done(sp.dma_start(words(qp[par][MAXROW:ROWS97, :, half * BANK:(half + 1) * BANK]),
                                             row.rearrange("(o j t) n -> o j (t n)", o=1, j=GH)))

                def store(u, half):
                    place = one(oT, u // HALF)[:, half * BANK:(half + 1) * BANK]
                    finished.wait(sp, u + 1)
                    stored.done(sp.dma_start(place, out[:, :]))

                def unit(u, par, half, _, more):
                    if half == 0 and not (isinstance(u, int) and u == units - HALF):
                        weighed.wait(sp, u * KT)
                        load_index = (u // HALF) + 1
                        load(load_index, 1 - par)
                    if more:
                        set_row(u + 1, par if half == 0 else 1 - par, 1 - half)
                    if not (isinstance(u, int) and u == 0):
                        store(u - 1, 1 - half)

                row_out.open(sp)
                stored.open(sp)
                load(0, 0)
                set_row(0, 0, 0)
                later_loops(sp, unit)
                store(units - 1, HALF - 1)
                stored.wait(sp, units)

            @block.gpsimd
            def _(pool):
                const.done(pool.memset(ones[:, :], 1.0))
                for i in range(2):
                    const.wait(pool, i + 1)
                    const.done(pool.memset(words(kp[i][MAXROW:ROWS97, :, :]), 1.0))

                def add(u, kt, left, right):
                    for pr in range(PAIRS):
                        exped.wait(pool, PAIRS * (KT * u + kt) + pr + 1)
                        pool_added.done(pool.tensor_tensor(sums[pr][:, :, :], left[pr][:, :, :],
                                                           right[pr][:, :, :], ALU.add))

                def unit(u, par, half, at, more):
                    total_made.wait(pool, u)
                    add(u, 1, prob[at], prob[(at + 1) % RING])
                    for n, kt in enumerate(OWN["pool"][2:]):
                        pool_added.wait(pool, PAIRS * (POOL_ADDS * u + n + 1))
                        add(u, kt, sums, prob[(at + kt) % RING])

                pool_added.open(pool)
                loops(pool, unit)

            @block.tensor
            def _(pe):
                def mx(u, par, half, slot):
                    j, qt, kb = slot // (QB * MB), slot // MB % QB, slot % MB
                    m = SLOTS * u + slot
                    mx_read.wait(pe, m - 2)
                    first = half * BANK + qt * P
                    mx_made.done(pe.matmul(mx_ps[slot % 3][:, 0:MKEYS], qp[par][0:MAXROW, j, first:first + P],
                                           kp[par][0:MAXROW, j, MFIRST[kb]:MFIRST[kb] + MKEYS], start=True, stop=True))

                def turn_peaks(u):
                    peaks.wait(pe, u + 1)
                    row_made.done(pe.transpose(peak_ps[0:GH * QB, 0:P], neg_max[:, :], ident[:, :]))

                def score(u, par, half, kt, pr, between):
                    keys = keys_of(kt)
                    if kt == 0 and pr == 0:
                        row_in.wait(pe, u + 1)
                    queries = slice(half * BANK, (half + 1) * BANK)
                    exped.wait(pe, PAIRS * (KT * u + kt - 1) + pr + 1)
                    for jj in range(2):
                        j = 2 * pr + jj
                        pe.matmul(scores[pr][0:keys, jj, :], kp[par][0:ROWS97, j, kt * P:kt * P + keys],
                                  qp[par][0:ROWS97, j, queries], start=True, stop=False)
                        between(j - GH)
                        last = pe.matmul(scores[pr][0:keys, jj, :], ident_b[0:keys, 0:keys],
                                         mask_t[0:keys, kt, queries], start=False, stop=True)
                        if jj == 1:
                            scored.done(last)
                        between(j)

                def four_heads(total, left, right, start, stop):
                    for j in range(GH):
                        mine = slice(j * DK, (j + 1) * DK)
                        last = pe.matmul(total[mine, :], left(mine), right[j // 2][0:left(mine).shape[0], j % 2, :],
                                         start=start, stop=stop, tile_position=(0, j * DK))
                    return last

                def weigh(u, par, kt, ring):
                    keys = keys_of(kt)
                    if kt == 0:
                        o_kept.wait(pe, u)
                    exped.wait(pe, PAIRS * (KT * u + kt + 1))
                    if kt == KT - 1:
                        sum_kept.wait(pe, u)
                        four_heads(sum_ps, lambda mine: ones[0:keys, :], prob[ring], True, False)
                    weighed.done(four_heads(o_ps, lambda mine: vg[par][0:keys, kt, mine], prob[ring],
                                            kt == 0, kt == KT - 1))

                def add_up(u):
                    wait_added(pe, u, OWN["dve"][-1])
                    total_made.done(four_heads(sum_ps, lambda mine: ones[:, :], sums, False, True))

                def unit(u, par, half, at, more):
                    nxt = (par if half == 0 else 1 - par, 1 - half)
                    for kt in range(KT):
                        slots = iter(range(SLOT_OF[kt], SLOT_OF[kt + 1]) if more else ())

                        def between(place):
                            if kt and (place >= 0 or place == -1 and SLOTS_OF[kt] > 7):
                                maximum()

                        def maximum():
                            for slot in itertools.islice(slots, 1):
                                mx(u + 1, *nxt, slot)

                        for pr in range(PAIRS):
                            if kt + 1 < KT:
                                score(u, par, half, kt + 1, pr, between)
                            elif more:
                                score(u + 1, *nxt, 0, pr, between)
                        if more and kt == TURN:
                            turn_peaks(u + 1)
                        if SLOTS_OF[kt] > 6:
                            maximum()
                        weigh(u, par, kt, (at + kt) % RING)
                        if more and kt == 0:
                            row_kept.wait(pe, u + 1)
                            sum_kept.wait(pe, u)
                            if half == 1:
                                loaded.wait(pe, LOADS * (u // HALF + 2))
                        for _ in range(SLOTS_OF[kt]):
                            maximum()
                    add_up(u)

                weighed.open(pe)
                total_made.open(pe)
                const.wait(pe, 3)
                loaded.wait(pe, LOADS)
                for slot in range(SLOTS):
                    mx(0, 0, 0, slot)
                turn_peaks(0)
                for pr in range(PAIRS):
                    score(0, 0, 0, 0, pr, lambda place: None)
                loops(pe, unit)

            @block.scalar
            def _(act):
                def keep_row(u):
                    row_made.wait(act, u + 1)
                    row_out.wait(act, u)
                    row_kept.done(act.activation(max_row[:, :], peak_ps[0:GH * QB, 0:P], ACT.Copy))

                def exp(u, kt, ring):
                    n, keys = KT * u + kt, keys_of(kt)
                    weighed.wait(act, n - RING + 1)
                    wait_added(act, u, kt - RING)
                    for pr in range(PAIRS):
                        scored.wait(act, PAIRS * n + pr + 1)
                        exped.done(act.activation(prob[ring][pr][0:keys, :, :], scores[pr][0:keys, :, :], ACT.Exp,
                                                  scale=SCALE))

                def unit(u, par, half, at, more):
                    for kt in range(KT):
                        if kt + 1 < KT:
                            exp(u, kt + 1, (at + kt + 1) % RING)
                        elif more:
                            exp(u + 1, 0, (at + KT) % RING)
                        if more and kt == TURN:
                            keep_row(u + 1)
                    weighed.wait(act, KT * (u + 1))
                    finished.wait(act, u - 1)
                    o_kept.done(act.activation(o_sb[half][:, :], o_ps[:, :], ACT.Copy))
                    total_made.wait(act, u + 1)
                    sum_kept.done(act.activation(sum_sb[half][:, :], sum_ps[:, :], ACT.Copy))

                for s in (row_kept, exped, o_kept, sum_kept):
                    s.open(act)
                keep_row(0)
                exp(0, 0, 0)
                loops(act, unit)

            @block.vector
            def _(dve):
                def read(u, half, slot):
                    j_qt, kb, qt = slot // MB, slot % MB, slot // MB % QB
                    m = SLOTS * u + slot
                    mx_read.wait(dve, m - 1)
                    mx_made.wait(dve, m + 1)
                    dve.sem_inc(carried.sem, 1)
                    mx_read.done(dve.tensor_tensor_reduce(
                        out=unread[slot % 2][:, :], in0=mx_ps[slot % 3][:, 0:MKEYS],
                        in1=mask_q[:, half * QB + qt, MFIRST[kb]:MFIRST[kb] + MKEYS], scale=1.0, scalar=LOWEST,
                        op0=ALU.add, op1=ALU.max, accum_out=maxima[:, j_qt, kb:kb + 1]))

                def peak(u):
                    mx_read.wait(dve, SLOTS * (u + 1))
                    row_made.wait(dve, u)
                    peaks.done(dve.tensor_reduce(neg_max[:, :], maxima[:, :, :], AX.X, ALU.max, negate=True))

                def add(u, kt, ring, i, pr):
                    if i == 0:
                        pool_added.wait(dve, PAIRS * POOL_ADDS * (u + 1))
                    else:
                        dve_added.wait(dve, PAIRS * (DVE_ADDS * u + i))
                    exped.wait(dve, PAIRS * (KT * u + kt) + pr + 1)
                    mine = sums[pr][:, :, :]
                    dve_added.done(dve.tensor_tensor(mine, mine, prob[ring][pr][:, :, :], ALU.add))

                def finish(u, half):
                    sum_kept.wait(dve, u + 1)
                    inverted.done(dve.reciprocal(sum_sb[half][:, :], sum_sb[half][:, :]))
                    inverted.wait(dve, u + 1)
                    o_kept.wait(dve, u + 1)
                    stored.wait(dve, u)
                    finished.done(dve.tensor_tensor(out[:, :], o_sb[half][:, :], sum_sb[half][:, :], ALU.mult))

                def unit(u, par, half, at, more):
                    for slot in range(SLOTS) if more else ():
                        read(u + 1, 1 - half, slot)
                    if more:
                        peak(u + 1)
                    for i, kt in enumerate(OWN["dve"]):
                        for pr in range(PAIRS):
                            add(u, kt, (at + kt) % RING, i, pr)
                    if not (isinstance(u, int) and u == 0):
                        finish(u - 1, 1 - half)

                for s in (mx_read, peaks, dve_added, finished, inverted):
                    s.open(dve)
                for slot in range(SLOTS):
                    read(0, 0, slot)
                peak(0)
                later_loops(dve, unit)
                finish(units - 1, HALF - 1)


def hidden_layers(nc, ident, oT, Wo, bo, x1, w_in, w_gate, gate_bias, x2, hT, weights):
    R = BANK // P
    steps = TOK // BANK
    NH = 2 * DC
    x_rows = x1.rearrange("(s r p) n -> s p r n", p=P, r=R)
    x2_rows = x2.rearrange("(s r p) n -> s p r n", p=P, r=R)
    oT_half = oT.rearrange("(b g) p n -> b p g n", g=GROUPS)
    hT_rows = hT.rearrange("(s r) p w c n -> s w p c r n", r=R)
    with ExitStack() as keep:
        sb, _, _ = allocator(keep, nc, "hd")
        parts = ("high", "low")
        wo = [sb(f"wo_{part}", [P, DC, D], F32R) for part in parts]
        wi = [[sb(f"wi{w}_{part}", [P, DC, 2 * D], F32R) for part in parts] for w in range(2)]
        wg = [sb(f"wg_{part}", [P, DC, E], F32R) for part in parts]
        split_weights(nc, ident, "hdo", [Wo], [wo])
        by_chunk = "(c p) n -> p c n"
        pieces = [(w_in[w].rearrange(by_chunk, p=P)[:, part, :], wi[w][0][:, part, :], wi[w][1][:, part, :])
                  for w in range(2) for part in (slice(0, DC // 2), slice(DC // 2, DC))]
        pieces += [(w_gate.rearrange(by_chunk, p=P), wg[0][:, :, :], wg[1][:, :, :])]
        with ExitStack() as ctx:
            sb, ps, step = allocator(ctx, nc, "hdl")
            o_bias, g_bias = sb("o_bias", [P, D]), sb("g_bias", [P, E])
            w_raw = [sb(f"w_raw{i}", [P, DC // 2, 2 * D]) for i in range(2)]
            w_loaded, w_high, w_low = [step(f"w_loaded{i}", size=16) for i in range(2)], step("w_high"), step("w_low")

            def raw(n):
                m, width = pieces[n][1].shape[1:]
                return w_raw[n % 2][:, 0:m, 0:width] if m <= DC // 2 else w_raw[n % 2][:, 0, 0:m * width].rearrange(
                    "p (m n) -> p m n", m=m)

            o_in = sb("o_in", [P, GROUPS, BANK])
            o_parts = [sb(f"o_{part}", [P, GROUPS, BANK], F32R) for part in parts]
            rows, rows2 = sb("rows", [P, R, D]), sb("rows2", [P, R, D])
            norm = LayerNorm(sb, step, R)
            nT = [[sb(f"nT_{part}{i}", [P, DC, BANK], F32R) for part in parts] for i in range(2)]
            gated = [sb(f"gated{i}", [P, BANK]) for i in range(2)]
            hidden = [sb(f"hidden{w}", [P, DC, BANK]) for w in range(2)]
            logits_t = sb("logits_t", [P, BANK])
            logits, probs = sb("logits", [P, R, E]), sb("probs", [P, R, E])
            top, sums, inv_sums = sb("top", [P, R]), sb("sums", [P, R]), sb("inv_sums", [P, R])
            best, best_at, best_at_f = sb("best", [P, R, 8]), sb("best_at", [P, R, 8], U32), sb("best_at_f", [P, R, 8])
            number = sb("number", [P, E])
            second = sb("second", [P, R, E])
            proj_ps = [ps(f"proj_ps{i}", [P, BANK]) for i in range(2)]
            turn_ps = ps("turn_ps", [P, DC, P])
            pair_ps = [ps(f"pair_ps{i}", [P, 2, BANK]) for i in range(2)]
            gate_ps = ps("gate_ps", [P, BANK])

            setup_in, const = step("setup_in", size=16), step("const")
            o_loaded, x_loaded = step("o_loaded", size=16), step("x_loaded", size=16)
            o_high, o_low = step("o_high", ahead=1), step("o_low", ahead=1)
            biased = step("biased")
            projected, added = step("projected", ahead=R), step("added", ahead=2)
            x2_stored = step("x2_stored", size=16, ahead=1)
            normal, turned = step("normal", ahead=1), step("turned")
            high_n, low_n = step("high_n"), step("low_n", ahead=1)
            paired, silu, hid = step("paired"), step("silu"), step("hid", ahead=2)
            h_stored = [step(f"h_stored{w}", size=16, ahead=R) for w in range(2)]
            gated_t, gate_kept, gate_turned = step("gated_t", ahead=1), step("gate_kept", ahead=1), step("gate_turned", ahead=1)
            shifted, gate_exp, routed = step("shifted"), step("gate_exp"), step("routed", ahead=1)

            def loops(eng, body):
                with eng.Fori(0, B - 1) as b:
                    for half in range(2):
                        body(2 * b + half, half, 2)
                body(steps - 2, 0, 1)
                body(steps - 1, 1, 0)

            with nc.Block() as block:
                @block.sync
                def _(sp):
                    setup_in.done(sp.dma_start(o_bias[:, :], bo.partition_broadcast(P)))
                    setup_in.done(sp.dma_start(g_bias[:, :], gate_bias.partition_broadcast(P)))

                    def load(s, half):
                        o_low.wait(sp, s)
                        b = s // 2
                        o_loaded.done(sp.dma_start(o_in[:, :, :], one(oT_half, b)[:, :, half * BANK:(half + 1) * BANK]))
                        x2_stored.wait(sp, s)
                        normal.wait(sp, s)
                        x_loaded.done(sp.dma_start(rows[:, :, :], one(x_rows, s)))

                    def store_x2(s):
                        added.wait(sp, R * (s + 1))
                        x2_stored.done(sp.dma_start(one(x2_rows, s), rows[:, :, :]))

                    def body(s, half, more):
                        if more:
                            store_x2(s + 1)
                        if more == 2:
                            load(s + 2, half)
                        for w in range(2):
                            hid.wait(sp, NH * s + DC * (w + 1))
                            for r in range(R):
                                h_stored[w].done(sp.dma_start(one(hT_rows, s)[w, :, :, r, :],
                                                              hidden[w][:, :, r * P:(r + 1) * P]))

                    x2_stored.open(sp)
                    for w in range(2):
                        h_stored[w].open(sp)
                    load(0, 0)
                    for n, (source, _, _) in enumerate(pieces):
                        if n >= 2:
                            w_low.wait(sp, n - 1)
                        w_loaded[n % 2].done(sp.dma_start(raw(n), source))
                    store_x2(0)
                    load(1, 1)
                    loops(sp, body)
                    x2_stored.wait(sp, steps)
                    for w in range(2):
                        h_stored[w].wait(sp, R * steps)

                @block.gpsimd
                def _(pool):
                    norm.pool_setup(pool)
                    for e in range(E):
                        const.done(pool.memset(number[:, e:e + 1], float(e)))
                        const.wait(pool, e + 1)
                    const.done(pool.memset(logits_t[:, :], 0.0))
                    setup_in.wait(pool, 2)
                    with pool.Fori(0, steps) as s:
                        x_loaded.wait(pool, s + 1)
                        for r in range(R):
                            last = pool.tensor_tensor(rows[:, r, :], rows[:, r, :], o_bias[:, :], ALU.add)
                            biased.done(last)
                            biased.wait(pool, R * s + r + 1)
                        norm.pool_step(pool, s)

                @block.tensor
                def _(pe):
                    def project(s):
                        o_low.wait(pe, s + 1)
                        for r in range(R):
                            added.wait(pe, R * s + r - 1)
                            for g in range(GROUPS):
                                last = matmul3(pe, proj_ps[r % 2][:, :], [o[:, g, r * P:(r + 1) * P] for o in o_parts],
                                               [w[:, g, :] for w in wo], g == 0, g == GROUPS - 1)
                            projected.done(last)

                    def turn(s, r):
                        normal.wait(pe, s + 1)
                        low_n.wait(pe, R * s + r)
                        for dc in range(DC):
                            last = pe.transpose(turn_ps[:, dc, :], rows2[:, r, dc * P:(dc + 1) * P], ident[:, :])
                        turned.done(last)

                    def pair(s, half, n):
                        w, c = n // DC, n % DC
                        hid.wait(pe, NH * s + n - 1)
                        for side in range(2):
                            cols = slice(side * D + c * P, side * D + (c + 1) * P)
                            for dc in range(DC):
                                last = matmul3(pe, pair_ps[n % 2][:, side, :], [x[:, dc, cols] for x in wi[w]],
                                               [x[:, dc, :] for x in nT[half]], dc == 0, dc == DC - 1)
                        paired.done(last)

                    def gate(s, half):
                        routed.wait(pe, s)
                        for dc in range(DC):
                            last = matmul3(pe, gate_ps[0:E, :], [x[:, dc, :] for x in wg],
                                           [x[:, dc, :] for x in nT[half]], dc == 0, dc == DC - 1)
                        gated_t.done(last)

                    def turn_gate(s):
                        gate_kept.wait(pe, s + 1)
                        for r in range(R):
                            last = pe.transpose(gate_ps[:, r * P:(r + 1) * P], logits_t[:, r * P:(r + 1) * P], ident[:, :])
                        gate_turned.done(last)

                    def body(s, half, more):
                        if more:
                            project(s + 1)
                        low_n.wait(pe, R * (s + 1))
                        for n in range(NH // 2):
                            pair(s, half, n)
                        gate(s, half)
                        for n in range(NH // 2, NH):
                            if more:
                                turn(s + 1, n - NH // 2)
                            pair(s, half, n)
                            if n == NH // 2:
                                turn_gate(s)

                    for st in (projected, gated_t, gate_turned):
                        st.open(pe)
                    project(0)
                    for r in range(R):
                        turn(0, r)
                    w_low.wait(pe, len(pieces))
                    loops(pe, body)

                @block.scalar
                def _(act):
                    def split_o(s):
                        o_loaded.wait(act, s + 1)
                        projected.wait(act, R * s)
                        o_high.done(act.activation(o_parts[0][:, :, :], o_in[:, :, :], ACT.Copy))

                    def split_n(s, half, r):
                        turned.wait(act, R * s + r + 1)
                        high_n.done(act.activation(nT[half][0][:, :, r * P:(r + 1) * P], turn_ps[:, :, :], ACT.Copy))

                    def activate(s, n):
                        hid.wait(act, NH * s + n - 1)
                        paired.wait(act, NH * s + n + 1)
                        silu.done(act.activation(gated[n % 2][:, :], pair_ps[n % 2][:, 0, :], ACT.Silu))

                    def body(s, half, more):
                        for n in range(NH // 2):
                            activate(s, n)
                        if more == 2:
                            split_o(s + 2)
                        gated_t.wait(act, s + 1)
                        gate_turned.wait(act, s)
                        gate_kept.done(act.activation(logits_t[0:E, :], gate_ps[0:E, :], ACT.Copy))
                        for n in range(NH // 2, NH):
                            if more:
                                split_n(s + 1, 1 - half, n - NH // 2)
                            activate(s, n)
                            if n == NH // 2 + 1:
                                shifted.wait(act, s + 1)
                                gate_exp.done(act.activation(probs[:, :, :], logits[:, :, :], ACT.Exp))

                    o_high.open(act)
                    gate_kept.open(act)
                    const.wait(act, E + 1)
                    split_o(0)
                    for n, (_, high, _) in enumerate(pieces):
                        w_loaded[n % 2].wait(act, n // 2 + 1)
                        w_high.done(act.activation(high, raw(n), ACT.Copy))
                    for r in range(R):
                        split_n(0, 0, r)
                    split_o(1)
                    loops(act, body)

                @block.vector
                def _(dve):
                    def split_o(s):
                        o_high.wait(dve, s + 1)
                        projected.wait(dve, R * s)
                        o_low.done(dve.tensor_tensor(o_parts[1][:, :, :], o_in[:, :, :], words(o_parts[0][:, :, :]),
                                                     ALU.subtract))

                    def add(s):
                        for r in range(R):
                            biased.wait(dve, R * s + r + 1)
                            projected.wait(dve, R * s + r + 1)
                            added.done(dve.tensor_tensor(rows[:, r, :], proj_ps[r % 2][:, :], rows[:, r, :], ALU.add))
                        added.wait(dve, R * (s + 1))
                        norm.statistics(dve, rows, s)
                        turned.wait(dve, R * s)
                        normal.done(norm.normalize(dve, rows2, rows, s))

                    def split_n(s, half, r):
                        high_n.wait(dve, R * s + r + 1)
                        low_n.done(dve.tensor_tensor(nT[half][1][:, :, r * P:(r + 1) * P], turn_ps[:, :, :],
                                                     words(nT[half][0][:, :, r * P:(r + 1) * P]), ALU.subtract))

                    def multiply(s, n):
                        w, c = n // DC, n % DC
                        if c == 0:
                            h_stored[w].wait(dve, R * s)
                        silu.wait(dve, NH * s + n + 1)
                        hid.done(dve.tensor_tensor(hidden[w][:, c, :], gated[n % 2][:, :], pair_ps[n % 2][:, 1, :],
                                                   ALU.mult))

                    def shift(s):
                        gate_turned.wait(dve, s + 1)
                        for r in range(R):
                            last = dve.tensor_tensor(logits[:, r, :], gate_ps[:, r * P:r * P + E], g_bias[:, :], ALU.add)
                        dve.drain()
                        dve.tensor_reduce(top[:, :], logits[:, :, :], AX.X, ALU.max)
                        dve.drain()
                        for r in range(R):
                            last = dve.tensor_scalar(logits[:, r, :], logits[:, r, :], top[:, r:r + 1], None,
                                                     ALU.subtract)
                        shifted.done(last)

                    def route(s):
                        gate_exp.wait(dve, s + 1)
                        dve.tensor_reduce(sums[:, :], probs[:, :, :], AX.X, ALU.add)
                        dve.drain()
                        dve.reciprocal(inv_sums[:, :], sums[:, :])
                        dve.drain()
                        for r in range(R):
                            dve.tensor_scalar(probs[:, r, :], probs[:, r, :], inv_sums[:, r:r + 1], None, ALU.mult)
                        dve.drain()
                        for r in range(R):
                            dve.max(best[:, r, :], probs[:, r, :])
                        dve.drain()
                        for r in range(R):
                            dve.max_index(best_at[:, r, :], best[:, r, :], probs[:, r, :])
                        dve.drain()
                        dve.tensor_copy(best_at_f[:, :, :], best_at[:, :, :])
                        dve.drain()
                        first = [probs, second]
                        for r in range(R):
                            for k in range(2):
                                dve.tensor_scalar(first[k][:, r, :], number[:, :], best_at_f[:, r, k:k + 1],
                                                  best[:, r, k:k + 1], ALU.is_equal, ALU.mult)
                        dve.drain()
                        routed.done(dve.tensor_tensor(weights[:, ds(R * s, R), :], probs[:, :, :], second[:, :, :],
                                                      ALU.add))

                    def body(s, half, more):
                        if more:
                            add(s + 1)
                        for n in range(NH // 2):
                            multiply(s, n)
                        if more == 2:
                            split_o(s + 2)
                        for n in range(NH // 2, NH):
                            if more:
                                split_n(s + 1, 1 - half, n - NH // 2)
                            multiply(s, n)
                            if n == NH // 2:
                                shift(s)
                            if n == NH // 2 + 1:
                                route(s)

                    for st in (o_low, added, normal, low_n, hid, routed):
                        st.open(dve)
                    setup_in.wait(dve, 2)
                    const.wait(dve, E)
                    def split_piece(n):
                        w_high.wait(dve, n + 1)
                        w_low.done(dve.tensor_tensor(pieces[n][2], raw(n), words(pieces[n][1]), ALU.subtract))

                    split_o(0)
                    for n in range(2):
                        split_piece(n)
                    add(0)
                    for n in range(2, len(pieces)):
                        split_piece(n)
                    for r in range(R):
                        split_n(0, 0, r)
                    split_o(1)
                    loops(dve, body)


def experts(nc, hT, x2, w_out, w2, weights, y):
    tiles = TOK // P
    OUTS = E + 1
    BANKS = 6
    parts = ("high", "low")
    x_t, y_t = tokens(x2), tokens(y)
    with ExitStack() as keep:
        sb, _, _ = allocator(keep, nc, "ex")
        wo = [sb(f"wo_{part}", [P, DC, D], F32R) for part in parts]
        wx = [sb(f"wx_{part}", [P, E, DC, D], F32R) for part in parts]
        with ExitStack() as ctx:
            sb, ps, step = allocator(ctx, nc, "exl")
            STAGES = 3
            sources = [w.rearrange("(c p) n -> p c n", p=P) for w in [w_out] + [w2[e] for e in range(E)]]
            w_in = [sb(f"w_in{i}", [P, DC, D]) for i in range(STAGES)]
            w_loaded = [step(f"w_loaded{i}", size=16) for i in range(STAGES)]
            w_high, w_low = step("w_high"), step("w_low")

            def weight(part, o):
                return wo[part][:, :, :] if o == 0 else wx[part][:, o - 1, :, :]

            h_in = [sb(f"h_in{i}", [P, 2, DC, P]) for i in range(2)]
            h = [[sb(f"h_{part}{i}", [P, 2, DC, P], F32R) for part in parts] for i in range(2)]
            rows = [sb(f"rows{i}", [P, D]) for i in range(2)]
            banks = [ps(f"banks{i}", [P, D]) for i in range(BANKS)]
            h_loaded = [step(f"h_loaded{i}", size=16) for i in range(2)]
            x_loaded = [step(f"x_loaded{i}", size=16) for i in range(2)]
            high, low = step("high", ahead=2), step("low", ahead=2)
            made, summed = step("made", ahead=2 * OUTS), step("summed", ahead=max(BANKS, OUTS))
            stored = [step(f"stored{i}", size=16, ahead=1) for i in range(2)]

            with nc.Block() as block:
                @block.sync
                def _(sp):
                    def load(n, t, odd):
                        low.wait(sp, t - 1)
                        h_loaded[odd].done(sp.dma_start(h_in[odd][:, :, :, :], one(hT, t)))
                        stored[odd].wait(sp, n)
                        x_loaded[odd].done(sp.dma_start(rows[odd][:, :], one(x_t, t)))

                    def body(n, t, odd, more=True):
                        if more:
                            load(n + odd, t + 1, 1 - odd)
                        summed.wait(sp, OUTS * (t + 1))
                        stored[odd].done(sp.dma_start(one(y_t, t), rows[odd][:, :]))

                    for st in stored:
                        st.open(sp)
                    load(0, 0, 0)
                    for o in range(OUTS):
                        if o >= STAGES:
                            w_low.wait(sp, o - STAGES + 1)
                        w_loaded[o % STAGES].done(sp.dma_start(w_in[o % STAGES][:, :, :], sources[o]))
                    with sp.Fori(0, tiles // 2 - 1) as n:
                        for odd in range(2):
                            body(n, 2 * n + odd, odd)
                    body(tiles // 2 - 1, tiles - 2, 0)
                    body(tiles // 2 - 1, tiles - 1, 1, False)
                    for st in stored:
                        st.wait(sp, tiles // 2)

                @block.scalar
                def _(act):
                    def body(n, t, odd):
                        h_loaded[odd].wait(act, n + 1)
                        made.wait(act, OUTS * (t - 1))
                        high.done(act.activation(h[odd][0][:, :, :, :], h_in[odd][:, :, :, :], ACT.Copy))

                    high.open(act)
                    body(0, 0, 0)
                    for o in range(OUTS):
                        w_loaded[o % STAGES].wait(act, o // STAGES + 1)
                        w_high.done(act.activation(weight(0, o), w_in[o % STAGES][:, :, :], ACT.Copy))
                    body(0, 1, 1)
                    with act.Fori(1, tiles // 2) as n:
                        for odd in range(2):
                            body(n, 2 * n + odd, odd)

                @block.tensor
                def _(pe):
                    def body(n, t, odd, first_of_all=False):
                        low.wait(pe, t + 1)
                        for o in range(OUTS):
                            if first_of_all:
                                w_low.wait(pe, o + 1)
                            which = min(o, 1)
                            summed.wait(pe, OUTS * t + o - BANKS + 1)
                            out = banks[(OUTS * odd + o) % BANKS]
                            right = wo if o == 0 else [w[:, o - 1, :, :] for w in wx]
                            for c in range(DC):
                                last = matmul3(pe, out[:, :], [x[:, which, c, :] for x in h[odd]],
                                               [w[:, c, :] for w in right], c == 0, c == DC - 1)
                            made.done(last)

                    made.open(pe)
                    body(0, 0, 0, True)
                    body(0, 1, 1)
                    with pe.Fori(1, tiles // 2) as n:
                        for odd in range(2):
                            body(n, 2 * n + odd, odd)

                @block.vector
                def _(dve):
                    def split(t, odd):
                        high.wait(dve, t + 1)
                        low.done(dve.tensor_tensor(h[odd][1][:, :, :, :], h_in[odd][:, :, :, :],
                                                   words(h[odd][0][:, :, :, :]), ALU.subtract))

                    def split_weights_of(o):
                        w_high.wait(dve, o + 1)
                        w_low.done(dve.tensor_tensor(weight(1, o), w_in[o % STAGES][:, :, :], words(weight(0, o)),
                                                     ALU.subtract))

                    def body(n, t, odd, more=True, first_of_all=False):
                        x_loaded[odd].wait(dve, n + 1)
                        for o in range(OUTS):
                            if first_of_all and o + 1 < OUTS:
                                split_weights_of(o + 1)
                            made.wait(dve, OUTS * t + o + 1)
                            out = banks[(OUTS * odd + o) % BANKS]
                            if o == 0:
                                summed.done(dve.tensor_tensor(rows[odd][:, :], out[:, :], rows[odd][:, :], ALU.add))
                            else:
                                summed.wait(dve, OUTS * t + o)
                                summed.done(dve.scalar_tensor_tensor(
                                    rows[odd][:, :], out[:, :], weights[:, ds(t, 1), o - 1:o].squeeze(1), rows[odd][:, :],
                                    ALU.mult, ALU.add))
                            if o == OUTS // 2 and more:
                                split(t + 1, 1 - odd)

                    low.open(dve)
                    summed.open(dve)
                    split(0, 0)
                    split_weights_of(0)
                    body(0, 0, 0, first_of_all=True)
                    body(0, 1, 1)
                    with dve.Fori(1, tiles // 2 - 1) as n:
                        for odd in range(2):
                            body(n, 2 * n + odd, odd)
                    body(tiles // 2 - 1, tiles - 2, 0)
                    body(tiles // 2 - 1, tiles - 1, 1, False)


def decoder_layer(nc, x, context, mask, k, v, Wq, bq, Wk, bk, Wv, bv, Wo, bo, w_shared_in, w_shared_out, w1, w2,
                  w_gate, gate_bias, y):
    def dram(name, shape, dt=F32):
        return nc.dram_tensor(name, shape, dt).ap()

    x1, x2 = dram("x1", [TOK, D]), dram("x2", [TOK, D])
    kT = [dram(f"kT_{part}", [B, D, S2]) for part in ("high", "low")]
    qT = [dram(f"qT_{part}", [B, D, S]) for part in ("high", "low")]
    values = dram("values", [B, GROUPS, S2, P])
    row = dram("row", [H, P])
    oT = dram("oT", [B * GROUPS, P, S])
    hT = dram("hT", [TOK // P, P, 2, DC, P])
    by_group = "b (g p) n -> (b g) p n"
    with ExitStack() as ctx:
        def sb(name, shape, dt=F32):
            return ctx.enter_context(nc.sbuf_tensor(name, shape, dt))

        ident, ident_b = sb("ident", [P, P]), sb("ident_b", [P, P], BF16)
        make_identity(nc, ident, ident_b)
        self_attention(nc, ident, x, k, v, x1)
        with ExitStack() as masks:
            mask_q = masks.enter_context(nc.sbuf_tensor("mask_q", [P, QT, S2], BF16))
            mask_t = masks.enter_context(nc.sbuf_tensor("mask_t", [P, KT, S], BF16))
            with nc.sbuf_tensor("any_key", [P, S], F32) as any_key:
                context_keys_values(nc, ident, ident_b, context, Wk, bk, Wv, bv, mask, (mask_q, mask_t, any_key), kT, values)
                project_queries(nc, ident, x1, Wq, bq, any_key, qT)
            cross_attention(nc, ident, ident_b, [a.rearrange(by_group, p=P) for a in kT],
                            [a.rearrange(by_group, p=P) for a in qT], values.rearrange("b g n p -> (b g) n p"),
                            mask_q, mask_t, row, oT)
        weights = sb("weights", [P, TOK // P, E])
        hidden_layers(nc, ident, oT, Wo, bo, x1, [w_shared_in, w1], w_gate, gate_bias, x2, hT, weights)
        experts(nc, hT, x2, w_shared_out, w2, weights, y)


INPUTS = ["x", "ctx_1024", "mask_1x1xSxS2_ik0", "L0_attn_k", "L0_attn_v", "L0_xattn_Wq_w", "L0_xattn_Wq_b",
          "L0_xattn_Wk_w", "L0_xattn_Wk_b", "L0_xattn_Wv_w", "L0_xattn_Wv_b", "L0_xattn_Wo_w", "L0_xattn_Wo_b",
          "L0_ffn_w_shared_in", "L0_ffn_w_shared_out", "L0_ffn_w1_shared", "L0_ffn_w2", "L0_ffn_w_gate",
          "L0_ffn_gate_bias"]


def kernel(**inputs):
    import concourse.bacc as bacc
    from concourse.bass_utils import run_bass_kernel_spmd

    nc = bacc.Bacc("TRN2", target_bir_lowering=False, num_devices=1)
    arrays, args = {}, []
    for name in INPUTS:
        a = np.ascontiguousarray(inputs[name])
        arrays[f"in_{name}"] = a
        args.append(nc.dram_tensor(f"in_{name}", a.shape, mybir.dt.from_np(a.dtype), kind="ExternalInput").ap())
    y = nc.dram_tensor("out_y", [TOK, D], F32, kind="ExternalOutput").ap()
    decoder_layer(nc, *args, y)
    result = run_bass_kernel_spmd(nc, [arrays], core_ids=[0])
    return result.results[0]["out_y"].reshape(B, S, D)
```
